# Optimizing a Trainium2 kernel written in Bass

```python
import numpy as np
import jax
import jax.numpy as jnp

def _softmax(x, axis=-1):
    return jax.nn.softmax(x, axis=axis)

def _gelu(x):
    return jax.nn.gelu(x, approximate=True)

def _silu(x):
    return jax.nn.silu(x)

def _sigmoid(x):
    return jax.nn.sigmoid(x)

def _layernorm(x, axis=-1, eps=1e-05):
    m = jnp.mean(x, axis=axis, keepdims=True)
    v = jnp.var(x, axis=axis, keepdims=True)
    return (x - m) / jnp.sqrt(v + eps)

def _scatter_add(tgt, idx, src, axis=0):
    return tgt.at[idx].add(src)

def _segment_sum(src, seg, n):
    return jax.ops.segment_sum(src, seg, n)
kernel_name = 'mk_adaln_d2_jaxref_r8_f9ac0c'

def setup_inputs(seed: int=0):
    np.random.seed(seed)
    _w = jnp.asarray

    def _L0_attn_setup():
        import jax, jax.numpy as jnp
        import numpy as np
        D_MODEL = 128
        D_K = 128
        LN_EPS = 1e-05
        key = jax.random.key(seed)
        k1, k2, k3 = jax.random.split(key, 3)
        B, N = (4, 1024)
        J = jax.random.normal(k1, (B, N, D_MODEL), dtype=jnp.float32)
        s = 1.0 / np.sqrt(D_MODEL)
        W_Q = jax.random.uniform(k2, (D_K, D_MODEL), jnp.float32, -s, s)
        W_K = jax.random.uniform(k3, (D_K, D_MODEL), jnp.float32, -s, s)
        gamma = jnp.ones((D_MODEL,), jnp.float32)
        beta = jnp.zeros((D_MODEL,), jnp.float32)
        return {'J': J, 'W_Q': W_Q, 'W_K': W_K, 'gamma': gamma, 'beta': beta}
    _L0_attn_in = _L0_attn_setup()

    def _L0_ffn_setup():
        import jax, jax.numpy as jnp
        import numpy as np
        NUM_EXPERTS = 8
        TOP_K = 2
        D = 128
        H = 4 * D
        B, S = (4, 256)
        key = jax.random.key(seed)
        ks = jax.random.split(key, 8)
        s = 0.02
        return {'x': jax.random.normal(ks[0], (B, S, D), dtype=jnp.float32), 'gate_w': jax.random.normal(ks[1], (NUM_EXPERTS, D), dtype=jnp.float32) * s, 'gate_b': jnp.zeros((NUM_EXPERTS,), dtype=jnp.float32), 'w1': jax.random.normal(ks[2], (NUM_EXPERTS, D, H), dtype=jnp.float32) * s, 'b1': jnp.zeros((NUM_EXPERTS, H), dtype=jnp.float32), 'w2': jax.random.normal(ks[3], (NUM_EXPERTS, H, D), dtype=jnp.float32) * s, 'b2': jnp.zeros((NUM_EXPERTS, D), dtype=jnp.float32)}
    _L0_ffn_in = _L0_ffn_setup()
    _L0_c = _w((lambda *s: np.random.randn(*s).astype(np.float32) * 0.05)(4, 128))
    _L0_wmod = _w((lambda *s: np.random.randn(*s).astype(np.float32) * 0.05)(128, 6 * 128) * 128 ** (-0.5))

    def _L1_attn_setup():
        import jax, jax.numpy as jnp
        import numpy as np
        HEADS = 16
        DIM_HEAD = 64
        ANCHORS = 64
        DIM = 128
        INNER = HEADS * DIM_HEAD
        SCALE = DIM_HEAD ** (-0.5)
        key = jax.random.key(seed)
        ks = jax.random.split(key, 5)
        b, n = (8, 512)
        x = jax.random.normal(ks[0], (b, n, DIM), dtype=jnp.float32)
        W_emb = jax.random.normal(ks[1], (2 * INNER, DIM), dtype=jnp.float32) * DIM ** (-0.5)
        W_anchor = jax.random.normal(ks[2], (ANCHORS, DIM_HEAD), dtype=jnp.float32) * DIM_HEAD ** (-0.5)
        W_out = jax.random.normal(ks[3], (DIM, INNER), dtype=jnp.float32) * INNER ** (-0.5)
        b_out = jnp.zeros((DIM,), dtype=jnp.float32)
        return {'x': x, 'W_emb': W_emb, 'W_anchor': W_anchor, 'W_out': W_out, 'b_out': b_out}
    _L1_attn_in = _L1_attn_setup()

    def _L1_ffn_setup():
        import jax, jax.numpy as jnp
        import numpy as np
        D_IN, D_HID = (128, 512)

        def _ternary(key, shape):
            return jax.random.randint(key, shape, -1, 2).astype(jnp.float32)

        def _tlin(x, w, s):
            return jnp.einsum('bsi,oi->bso', x, w) * s
        key = jax.random.key(seed)
        ks = jax.random.split(key, 12)
        inv = lambda fan: 1.0 / np.sqrt(fan).astype(np.float32)
        return {'x': jax.random.normal(ks[0], (4, 256, D_IN), dtype=jnp.float32), 'w1_w': _ternary(ks[1], (D_HID, D_IN)), 'w1_s': jax.random.uniform(ks[2], (D_HID,), dtype=jnp.float32) * inv(D_IN), 'w2_w': _ternary(ks[3], (D_HID, D_IN)), 'w2_s': jax.random.uniform(ks[4], (D_HID,), dtype=jnp.float32) * inv(D_IN), 'h1_w': _ternary(ks[5], (D_HID, D_HID)), 'h1_s': jax.random.uniform(ks[6], (D_HID,), dtype=jnp.float32) * inv(D_HID), 'h2_w': _ternary(ks[7], (D_HID, D_HID)), 'h2_s': jax.random.uniform(ks[8], (D_HID,), dtype=jnp.float32) * inv(D_HID), 'w3_w': _ternary(ks[9], (D_IN, D_HID)), 'w3_s': jax.random.uniform(ks[10], (D_IN,), dtype=jnp.float32) * inv(D_HID)}
    _L1_ffn_in = _L1_ffn_setup()
    _L1_c = _w((lambda *s: np.random.randn(*s).astype(np.float32) * 0.05)(4, 128))
    _L1_wmod = _w((lambda *s: np.random.randn(*s).astype(np.float32) * 0.05)(128, 6 * 128) * 128 ** (-0.5))
    _d = {'L0_attn_J': _L0_attn_in['J'], 'L0_attn_W_Q': _L0_attn_in['W_Q'], 'L0_attn_W_K': _L0_attn_in['W_K'], 'L0_attn_gamma': _L0_attn_in['gamma'], 'L0_attn_beta': _L0_attn_in['beta'], 'L0_ffn_gate_w': _L0_ffn_in['gate_w'], 'L0_ffn_gate_b': _L0_ffn_in['gate_b'], 'L0_ffn_w1': _L0_ffn_in['w1'], 'L0_ffn_b1': _L0_ffn_in['b1'], 'L0_ffn_w2': _L0_ffn_in['w2'], 'L0_ffn_b2': _L0_ffn_in['b2'], 'L0_c': _L0_c, 'L0_wmod': _L0_wmod, 'L1_attn_W_emb': _L1_attn_in['W_emb'], 'L1_attn_W_anchor': _L1_attn_in['W_anchor'], 'L1_attn_W_out': _L1_attn_in['W_out'], 'L1_attn_b_out': _L1_attn_in['b_out'], 'L1_ffn_w1_w': _L1_ffn_in['w1_w'], 'L1_ffn_w1_s': _L1_ffn_in['w1_s'], 'L1_ffn_w2_w': _L1_ffn_in['w2_w'], 'L1_ffn_w2_s': _L1_ffn_in['w2_s'], 'L1_ffn_h1_w': _L1_ffn_in['h1_w'], 'L1_ffn_h1_s': _L1_ffn_in['h1_s'], 'L1_ffn_h2_w': _L1_ffn_in['h2_w'], 'L1_ffn_h2_s': _L1_ffn_in['h2_s'], 'L1_ffn_w3_w': _L1_ffn_in['w3_w'], 'L1_ffn_w3_s': _L1_ffn_in['w3_s'], 'L1_c': _L1_c, 'L1_wmod': _L1_wmod}
    _x0 = _d['L0_attn_J']
    _d['L0_attn_J'] = jax.random.normal(jax.random.fold_in(jax.random.key(seed), 1), (4, 1024, 128), dtype=_x0.dtype)
    del _x0
    return _d

def reference(L0_attn_J, L0_attn_W_Q, L0_attn_W_K, L0_attn_gamma, L0_attn_beta, L0_ffn_gate_w, L0_ffn_gate_b, L0_ffn_w1, L0_ffn_b1, L0_ffn_w2, L0_ffn_b2, L0_c, L0_wmod, L1_attn_W_emb, L1_attn_W_anchor, L1_attn_W_out, L1_attn_b_out, L1_ffn_w1_w, L1_ffn_w1_s, L1_ffn_w2_w, L1_ffn_w2_s, L1_ffn_h1_w, L1_ffn_h1_s, L1_ffn_h2_w, L1_ffn_h2_s, L1_ffn_w3_w, L1_ffn_w3_s, L1_c, L1_wmod):

    def _L0_attn_ref(J, W_Q, W_K, gamma, beta):
        import jax, jax.numpy as jnp
        import numpy as np
        D_MODEL = 128
        D_K = 128
        LN_EPS = 1e-05
        Q = jnp.einsum('bnd,kd->bnk', J, W_Q)
        K = jnp.einsum('bnd,kd->bnk', J, W_K)
        M = jnp.einsum('bnk,bnd->bkd', K, J)
        J_new = jnp.einsum('bnk,bkd->bnd', Q, M) / jnp.sqrt(jnp.float32(D_K)) + J
        mu = jnp.mean(J_new, axis=-1, keepdims=True)
        var = jnp.mean(jnp.square(J_new - mu), axis=-1, keepdims=True)
        return (J_new - mu) * jax.lax.rsqrt(var + LN_EPS) * gamma + beta

    def _L0_ffn_ref(x, gate_w, gate_b, w1, b1, w2, b2):
        import jax, jax.numpy as jnp
        import numpy as np
        NUM_EXPERTS = 8
        TOP_K = 2
        D = 128
        H = 4 * D
        B, S = (4, 256)
        orig_shape = x.shape
        xf = x.reshape(-1, orig_shape[-1])
        gates = xf @ gate_w.T + gate_b
        weights, indices = jax.lax.top_k(gates, TOP_K)
        weights = jax.nn.softmax(weights, axis=-1)
        out = jnp.zeros_like(xf)
        for e in range(NUM_EXPERTS):
            w_e = jnp.sum(weights * (indices == e), axis=-1, keepdims=True)
            h = jax.nn.gelu(xf @ w1[e] + b1[e], approximate=False)
            out = out + w_e * (h @ w2[e] + b2[e])
        return out.reshape(orig_shape)

    def _L1_attn_ref(x, W_emb, W_anchor, W_out, b_out):
        import jax, jax.numpy as jnp
        import numpy as np
        HEADS = 16
        DIM_HEAD = 64
        ANCHORS = 64
        DIM = 128
        INNER = HEADS * DIM_HEAD
        SCALE = DIM_HEAD ** (-0.5)
        b, n, _ = x.shape
        emb = x @ W_emb.T
        qk, v = jnp.split(emb, 2, axis=-1)
        qk = qk.reshape(b, n, HEADS, DIM_HEAD).transpose(0, 2, 1, 3)
        v = v.reshape(b, n, HEADS, DIM_HEAD).transpose(0, 2, 1, 3)
        anchor_B = qk @ W_anchor.T * SCALE
        attn = jax.nn.softmax(anchor_B, axis=-1)
        s = jnp.sum(attn, axis=-2)
        recip = s ** (-1.0)
        recip = jnp.where(jnp.isinf(recip), 0.0, recip)
        out = jnp.einsum('bhna,bhnd->bhad', attn, v)
        out = recip[..., None] * out
        out = jnp.einsum('bhna,bhad->bhnd', attn, out)
        out = out.transpose(0, 2, 1, 3).reshape(b, n, INNER)
        return out @ W_out.T + b_out

    def _L1_ffn_ref(x, w1_w, w1_s, w2_w, w2_s, h1_w, h1_s, h2_w, h2_s, w3_w, w3_s):
        import jax, jax.numpy as jnp
        import numpy as np
        D_IN, D_HID = (128, 512)

        def _ternary(key, shape):
            return jax.random.randint(key, shape, -1, 2).astype(jnp.float32)

        def _tlin(x, w, s):
            return jnp.einsum('bsi,oi->bso', x, w) * s
        h = jax.nn.silu(_tlin(x, w1_w, w1_s)) * _tlin(x, w2_w, w2_s)
        h = jax.nn.gelu(_tlin(h, h1_w, h1_s), approximate=False)
        h = jax.nn.gelu(_tlin(h, h2_w, h2_s), approximate=False)
        return _tlin(h, w3_w, w3_s)
    x = L0_attn_J
    mod = (_silu(L0_c) @ L0_wmod).reshape(L0_c.shape[0], 6, 1, -1)
    sa, ca, ga, sb, cb, gb = (mod[:, 0], mod[:, 1], mod[:, 2], mod[:, 3], mod[:, 4], mod[:, 5])
    ga = (2 * (ga >= 0) - 1) * jnp.maximum(jnp.abs(ga), 0.25)
    gb = (2 * (gb >= 0) - 1) * jnp.maximum(jnp.abs(gb), 0.25)
    h = _layernorm(x, axis=-1) * (1 + ca) + sa
    x = x + ga * _L0_attn_ref(h, L0_attn_W_Q, L0_attn_W_K, L0_attn_gamma, L0_attn_beta)
    h = _layernorm(x, axis=-1) * (1 + cb) + sb
    x = x + gb * _L0_ffn_ref(h, L0_ffn_gate_w, L0_ffn_gate_b, L0_ffn_w1, L0_ffn_b1, L0_ffn_w2, L0_ffn_b2)
    mod = (_silu(L1_c) @ L1_wmod).reshape(L1_c.shape[0], 6, 1, -1)
    sa, ca, ga, sb, cb, gb = (mod[:, 0], mod[:, 1], mod[:, 2], mod[:, 3], mod[:, 4], mod[:, 5])
    ga = (2 * (ga >= 0) - 1) * jnp.maximum(jnp.abs(ga), 0.25)
    gb = (2 * (gb >= 0) - 1) * jnp.maximum(jnp.abs(gb), 0.25)
    h = _layernorm(x, axis=-1) * (1 + ca) + sa
    x = x + ga * _L1_attn_ref(h, L1_attn_W_emb, L1_attn_W_anchor, L1_attn_W_out, L1_attn_b_out)
    h = _layernorm(x, axis=-1) * (1 + cb) + sb
    x = x + gb * _L1_ffn_ref(h, L1_ffn_w1_w, L1_ffn_w1_s, L1_ffn_w2_w, L1_ffn_w2_s, L1_ffn_h1_w, L1_ffn_h1_s, L1_ffn_h2_w, L1_ffn_h2_s, L1_ffn_w3_w, L1_ffn_w3_s)
    return x

_drawn_inputs = setup_inputs


def setup_inputs(seed=0):
    import zlib

    import numpy as np

    out = dict(_drawn_inputs(seed))
    spreads = {'L0_attn_gamma': (1.0, 0.2),
     'L0_attn_beta': (0.0, 0.1),
     'L0_ffn_gate_b': (0.0, 0.1),
     'L0_ffn_b1': (0.0, 0.1),
     'L0_ffn_b2': (0.0, 0.1),
     'L1_attn_b_out': (0.0, 0.1)}
    factors = {}
    for name, (base, spread) in spreads.items():
        noise = np.random.default_rng([zlib.crc32(name.encode()), seed]).standard_normal(out[name].shape)
        drawn = base * np.exp(spread * noise) if base else spread * noise
        out[name] = jnp.asarray(drawn.astype(out[name].dtype))
    for name, factor in factors.items():
        out[name] = (out[name] * factor).astype(out[name].dtype)
    return out
```

```python
from contextlib import ExitStack

import concourse.bass as bass
from concourse import mybir

ALU = mybir.AluOpType
ACT = mybir.ActivationFunctionType
F32 = mybir.dt.float32
F32R = mybir.dt.float32r
X = mybir.AxisListType.X

B, N, D = 4, 1024, 128
T = N // 128
G, GT = 2, 4
GW = GT * 128
E, HC = 8, 4
H, DH, A = 16, 64, 64
AC = H * A // 128
EPS = 1e-5
NCOL = 8
C1B0, SB0, GB0, GA1, GABO, C1B1, SB1, GBS3 = range(NCOL)
R_C1A0, R_SA0, R_GG, R_GBETA, R_C1A1, R_SA1 = range(6)
DVE_STEPS = 173


class Events:

    def __init__(self, sem, jobs, by=1):
        self.sem, self.jobs, self.by = sem, list(jobs), by
        self.at = {job: i for i, job in enumerate(self.jobs)}
        self.raised = 0

    def credit(self):
        return len(self.jobs) * self.by

    def now(self, job, b):
        return self.sem, ((b + 1) * len(self.jobs) + self.at[job] + 1) * self.by

    def before(self, job, b):
        return self.sem, (b * len(self.jobs) + self.at[job] + 1) * self.by

    def raise_(self, job):
        assert self.jobs[self.raised % len(self.jobs)] == job, (job, self.jobs[self.raised])
        self.raised += 1
        return self.sem, self.by


def build(nc, ins, out):
    ctx = ExitStack()
    with ctx:
        def sb(name, shape, dt=F32):
            return ctx.enter_context(nc.sbuf_tensor(name, shape, dt))

        def sem(name):
            return ctx.enter_context(nc.semaphore(name))

        w1 = sb("w1", [128, 2, E * HC * 128], F32R)
        w2 = sb("w2", [128, 2, E * HC * 128], F32R)
        fab = sb("fab", [128, 2, 2 * HC * 128], F32R)
        fh1 = sb("fh1", [128, 2, HC * HC * 128], F32R)
        fh2 = sb("fh2", [128, 2, HC * HC * 128], F32R)
        fy = sb("fy", [128, 2, HC * 128], F32R)
        anch = sb("anch", [128, 2, H * A], F32R)
        gatew = sb("gatew", [128, 2, E], F32R)
        onehot = sb("onehot", [32, 1024], F32R)
        vout = sb("vout", [128, H * 128])
        wwt = sb("wwt", [128, 128])
        ident = sb("ident", [128, 128])
        ones = sb("ones", [128, 1])
        b1 = sb("b1", [128, E * HC])
        b2 = sb("b2", [128, E])
        gateb = sb("gateb", [128, E])
        order = sb("order", [128, E])
        fs = sb("fs", [128, 4 * HC + 1])
        neghalf = sb("neghalf", [128, T])
        modt = sb("modt", [128, B * NCOL])
        xa = sb("xa", [128, T, 128])
        xb = sb("xb", [128, T, 128])
        hn = sb("hn", [128, T, 128])
        hT = sb("hT", [128, 2, G, GW], F32R)
        ring = sb("ring", [128, 4, GW])
        misc = sb("misc", [128, 2, GW])
        tmp = sb("tmp", [128, 2, GW])
        hid_at = nc.sbuf_base
        hid = sb("hid", [128, 2, HC, 2, GW], F32R)
        cmat_at = nc.sbuf_base
        cmat = sb("cmat", [128, AC, 128])
        rows = sb("rows", [128, 6, 128])
        cols = sb("cols", [128, NCOL])
        pad = sb("pad", [128, 1])
        gs = sb("gs", [128, 128])
        pmat = sb("pmat", [128, 128])
        stats = sb("stats", [128, T, 6])
        mv = sb("mv", [128, T, 2])
        ve = sb("ve", [128, T])
        rs = sb("rs", [128, T])
        gt = sb("gt", [128, GT, E])
        top = sb("top", [128, GT, 8])
        above = sb("above", [128, GT, E])
        equal = sb("equal", [128, GT, E])
        tops = sb("tops", [128, GT, 8])
        gap = sb("gap", [128, GT])
        th = sb("th", [128, GT])
        wa = sb("wa", [128, 2, GT])
        w32 = sb("w32", [128, GT, 16, 2], F32R)
        nmax = sb("nmax", [128, H])
        m32 = sb("m32", [128, 2 * H], F32R)
        lsum = sb("lsum", [128, H])
        lrec = sb("lrec", [128, H])
        srec = sb("srec", [128, 3, AC])
        attnT = nc.alloc_sbuf_tensor_at("attnT", [128, AC, N], F32, offset=hid_at)
        wT = nc.alloc_sbuf_tensor_at("wT", [32, G, GW], F32R, offset=cmat_at)
        mTs = wT[:, 0, 0:128]
        stage = attnT[:, :, :].rearrange("p k n -> p (k n)")

        ps = ctx.enter_context(nc.psum_tensor("ps", [128, 8, 512], F32))
        scratch = nc.dram_tensor("rows_by_batch", (B, 6 * 128), F32, kind="Internal").ap()

        def f(ap):
            return ap.bitcast(F32)

        gs2 = range(G)
        ns = range(G * E)
        ts = range(T)
        cs = range(HC)
        x_loaded = Events(sem("x_loaded"), ["x"], 16)
        rows_loaded = Events(sem("rows_loaded"), ["rows"], 16)
        out_stored = [Events(sem(f"out_stored{g}"), ["out"], 16) for g in range(G)]
        pe_prep = Events(sem("pe_prep"), [("h0T", 0), ("h0T", 1), "gram", "P", ("jn", 0), ("jn", 1),
                                          ("h1T", 0), ("h1T", 1), ("gate", 0), ("gate", 1),
                                          ("wT", 0), ("wT", 1)])
        pe_hid = Events(sem("pe_hid"), range(G * E * HC))
        pe_wb = Events(sem("pe_wb"), ns)
        pe_out = Events(sem("pe_out"), ns)
        pe_res = Events(sem("pe_res"), [("M", 0), ("h2T", 0), ("M", 1), ("h2T", 1), ("A", 0), ("A", 1),
                                        ("h3T", 0), ("h3T", 1), ("F", 0), ("F", 1)])
        pe_logits = Events(sem("pe_logits"), ts)
        pe_maxT = Events(sem("pe_maxT"), ts)
        pe_shift = Events(sem("pe_shift"), ts)
        pe_z = Events(sem("pe_z"), ts)
        pe_attnT = Events(sem("pe_attnT"), [(t, h) for t in ts for h in range(2)])
        pe_fin = Events(sem("pe_fin"), ["s"] + [("C", j) for j in range(4)] + [("O", g) for g in gs2])

        def ffn_jobs(g, part):
            if part == "ab":
                return [(g, k, c) for c in cs for k in "ab"]
            return [(g, part)] if part == "y" else [(g, part, c) for c in cs]

        ffn_order = [(0, "ab"), (0, "h1"), (0, "h2"), (1, "ab"), (0, "y"), (1, "h1"), (1, "h2"), (1, "y")]
        pe_ffn = Events(sem("pe_ffn"), [j for o in ffn_order for j in ffn_jobs(*o)])
        act_cols = Events(sem("act_cols"), ["cols"])
        act_prep = Events(sem("act_prep"), [("h0T", 0), ("h0T", 1), "gram", ("h1T", 0), ("h1T", 1),
                                            ("th", 0), ("wT", 0), ("th", 1), ("wT", 1)])
        act_gelu = Events(sem("act_gelu"), range(G * E * HC))
        act_wb = Events(sem("act_wb"), ns)
        act_gb = Events(sem("act_gb"), gs2)
        act_maxT = Events(sem("act_maxT"), ts)
        act_exp = Events(sem("act_exp"), ts)
        act_attnT = Events(sem("act_attnT"), [(t, h) for t in ts for h in range(2)])
        act_z = Events(sem("act_z"), ["z"])
        act_y = Events(sem("act_y"), [("A", 0), ("A", 1), ("F", 0), ("F", 1)])
        act_h3T = Events(sem("act_h3T"), gs2)
        hidden_order = [(0, "ab"), (0, "h1"), (0, "h2"), (1, "ab"), (1, "h1"), (1, "h2")]
        act_ffn = Events(sem("act_ffn"), [(g, p, c) for g, p in hidden_order for c in cs])
        lns = ["L0a", "L0i", "L0b", ("L1a", 0), ("L1a", 1), ("L1b", 0), ("L1b", 1)]
        dve_var = Events(sem("dve_var"), lns)
        dve_norm = Events(sem("dve_norm"), lns)
        dve_p = Events(sem("dve_p"), ["P"])
        dve_gap = Events(sem("dve_gap"), gs2)
        dve_w = Events(sem("dve_w"), gs2)
        dve_hT = Events(sem("dve_hT"), [(p, g) for p in ("moe", "attn", "ffn") for g in gs2])
        dve_split = Events(sem("dve_split"), list(range(G * E * HC)) + [(g, p, c) for g, p in hidden_order for c in cs])
        dve_gated = Events(sem("dve_gated"), ns)
        dve_res = Events(sem("dve_res"), [(p, g) for p in "MAF" for g in gs2])
        dve_max = Events(sem("dve_max"), ts)
        dve_attn = Events(sem("dve_attn"), ts)
        dve_c = Events(sem("dve_c"), range(4))
        dve_prod = Events(sem("dve_prod"), [(g, c) for g in gs2 for c in cs])
        dve_step = Events(sem("dve_step"), range(DVE_STEPS))
        pool_rs = Events(sem("pool_rs"), lns)
        pool_mul = Events(sem("pool_mul"), [("L0", 0), ("L0", 1), ("L1", 0), ("L1", 1)])
        pool_h = Events(sem("pool_h"), [("L0", 0), ("L0", 1), ("L1", 0), ("L1", 1)])
        pool_beta = Events(sem("pool_beta"), ["x"])
        pool_acc = Events(sem("pool_acc"), [n for n in ns if n % E])
        pool_asum = Events(sem("pool_asum"), range(1, T))
        every = [v for v in list(locals().values()) if isinstance(v, Events)] + out_stored

        l_small, l_l1, l_emb, l_mod, l_scr = (sem(n) for n in
            ("small_loaded", "ffn_loaded", "emb_loaded", "mod_loaded", "rows_written"))
        l_moe = [sem(f"moe_loaded{q}") for q in range(4)]
        u_pool, u_act, u_hi, u_lo, u_pe, u_dve = (sem(n) for n in
            ("consts_made", "act_setup", "hi_parts", "lo_parts", "pe_setup", "dve_setup"))

        MOE_W = E * HC * 128
        L1_PARTS = [(fab, 0, 1024), (fh1, 1024, 2048), (fh2, 3072, 2048), (fy, 5120, 512)]
        EMB = 5632
        block = ctx.enter_context(nc.Block())

        def by_tile(ap):
            return ap.rearrange("(p t) d -> p t d", t=T)

        @block.sync
        def _(sp):
            for ev in every:
                sp.sem_inc(ev.sem, ev.credit())
            small = [(b1[:, :], ins["b1"]), (b2[:, :], ins["b2"]), (gs[:, 0:E], ins["gate_w"]),
                     (gateb[:, :], ins["gate_b"].partition_broadcast(128)),
                     (pmat[:, 0:128], ins["W_Q"]), (hn[:, 0, :], ins["W_K"]), (fs[:, :], ins["scales"]),
                     (stats[:, 0, 0:1], ins["b_out"]), (stats[0:64, 1:2, :], None)]
            for dst, src in small[:-1]:
                sp.dma_start(dst, src).then_inc(l_small, 16)
            sp.dma_start(cols[:, 0:2 * B], ins["cT"]).then_inc(l_mod, 16)
            sp.dma_start(ring[:, 0:3, :].rearrange("p a n -> p (a n)"), ins["wmod"]).then_inc(l_mod, 16)
            sp.dma_start(cmat[0:B, 0, :], ins["gamma"].partition_broadcast(B)).then_inc(l_mod, 16)
            sp.dma_start(cmat[0:B, 1, :], ins["beta"].partition_broadcast(B)).then_inc(l_mod, 16)
            for q in range(4):
                w = slice(q * 2048, (q + 1) * 2048)
                src = ins["w1"][:, w] if q < 2 else ins["w2"][:, slice((q - 2) * 2048, (q - 1) * 2048)]
                sp.dma_start(stage[:, w], src).then_inc(l_moe[q], 16)
            sp.dma_start(xa[:, :, :], by_tile(ins["x"][0])).then_inc(x_loaded.sem, 16)
            sp.wait_ge(u_lo, 4)
            sp.dma_start(stage[:, 0:EMB], ins["ffn"]).then_inc(l_l1, 16)
            sp.dma_start(stage[:, EMB:EMB + 2048], ins["w_emb"]).then_inc(l_emb, 16)
            sp.dma_start(stage[0:64, EMB + 2048:EMB + 2048 + A], ins["w_anchor"]).then_inc(l_emb, 16)
            sp.wait_ge(u_pe, 1)
            sp.dma_start(hn[64:128, :, :], ins["w_out"][:, 0:8, :]).then_inc(l_emb, 16)
            sp.dma_start(xb[64:128, :, :], ins["w_out"][:, 8:16, :]).then_inc(l_emb, 16)
            sp.wait_ge(u_dve, 1)
            sp.dma_start(scratch.rearrange("b (r d) -> b r d", r=6), rows[0:B, :, :]).then_inc(l_scr, 16)
            sp.wait_ge(l_scr, 16)
            sp.dma_start(rows[:, :, :], scratch[0].rearrange("(r d) -> r d", r=6).partition_broadcast(128))\
                .then_inc(rows_loaded.sem, 16)

            def store(b):
                for g in gs2:
                    sp.wait_ge(*dve_res.now(("F", g), b))
                    sp.dma_start(by_tile(out[b])[:, g * GT:(g + 1) * GT, :], xb[:, g * GT:(g + 1) * GT, :])\
                        .then_inc(out_stored[g].sem, 16)

            with sp.Fori(0, B - 1) as b:
                sp.wait_ge(*dve_res.now(("M", 1), b))
                sp.dma_start(xa[:, :, :], by_tile(ins["x"][b + 1])).then_inc(x_loaded.sem, 16)
                sp.wait_ge(*pool_h.now(("L1", 1), b))
                sp.dma_start(rows[:, :, :], scratch[b + 1].rearrange("(r d) -> r d", r=6).partition_broadcast(128))\
                    .then_inc(rows_loaded.sem, 16)
                store(b)
            store(B - 1)
            for g in gs2:
                sp.wait_ge(out_stored[g].sem, (B + 1) * 16)

        @block.gpsimd
        def _(pool):
            gp = nc.gpsimd
            oh = tmp[0:32, :, :].rearrange("p a n -> p (a n)")
            gp.memset(ident[:, :], 0.0).then_inc(u_pool, 1)
            gp.memset(oh, 0.0).then_inc(u_pool, 1)
            gp.memset(ones[:, :], 1.0).then_inc(u_pool, 1)
            gp.memset(neghalf[:, :], -0.5).then_inc(u_pool, 1)
            for e in range(E):
                gp.memset(order[:, e:e + 1], float(E - e)).then_inc(u_pool, 1)
            pool.wait_ge(u_pool, 12)
            gp.affine_select(out=ident[:, :], in_=ident[:, :], compare_op=ALU.not_equal, fill=1.0, base=0,
                             pattern=[[-1, 128]], channel_multiplier=1).then_inc(u_pool, 1)
            for base in (0, -H):
                v = oh.rearrange("p (h a) -> p h a", h=H)
                gp.affine_select(out=v, in_=v, compare_op=ALU.not_equal, fill=1.0, base=base,
                                 pattern=[[-1, H], [0, A]], channel_multiplier=1).then_inc(u_pool, 1)
                pool.wait_ge(u_pool, 14 if base == 0 else 15)

            with pool.Fori(0, B) as b:
                def rstd(k, n):
                    pool.wait_ge(*dve_var.now(k, b))
                    gp.tensor_tensor(rs[:, 0:n], ve[:, 0:n], neghalf[:, 0:n], ALU.pow).then_inc(*pool_rs.raise_(k))

                def modulate(layer, g, mul, add):
                    h = hn[:, g * GT:(g + 1) * GT, :]
                    gp.tensor_tensor(h, h, rows[:, mul, :].unsqueeze(1).broadcast_to([128, GT, 128]), ALU.mult)\
                        .then_inc(*pool_mul.raise_((layer, g)))
                    pool.wait_ge(*pool_mul.now((layer, g), b))
                    gp.tensor_tensor(h, h, rows[:, add, :].unsqueeze(1).broadcast_to([128, GT, 128]), ALU.add)\
                        .then_inc(*pool_h.raise_((layer, g)))

                rstd("L0a", T)
                pool.wait_ge(*rows_loaded.before("rows", b) if False else rows_loaded.now("rows", b))
                pool.wait_ge(*dve_norm.now("L0a", b))
                for g in gs2:
                    modulate("L0", g, R_C1A0, R_SA0)
                gp.tensor_tensor(xa[:, :, :], xa[:, :, :],
                                 rows[:, R_GBETA, :].unsqueeze(1).broadcast_to([128, T, 128]), ALU.add)\
                    .then_inc(*pool_beta.raise_("x"))
                rstd("L0i", T)
                rstd("L0b", T)
                acc = hn[:, GT:T, :].rearrange("p t d -> p (t d)")
                for n in ns:
                    if n % E:
                        pool.wait_ge(*dve_gated.now(n, b))
                        if n % E > 1:
                            pool.wait_ge(*pool_acc.now(n - 1, b))
                        gp.tensor_tensor(acc, acc, tmp[:, n % 2, :], ALU.add).then_inc(*pool_acc.raise_(n))
                    if n == 10:
                        rstd(("L1a", 0), GT)
                        pool.wait_ge(*dve_norm.now(("L1a", 0), b))
                        modulate("L1", 0, R_C1A1, R_SA1)
                rstd(("L1a", 1), GT)
                pool.wait_ge(*dve_norm.now(("L1a", 1), b))
                modulate("L1", 1, R_C1A1, R_SA1)
                asum = misc[:, :, :].rearrange("p a n -> p (a n)")
                for t in range(1, T):
                    pool.wait_ge(*dve_attn.now(t, b))
                    first = ring[:, 0:2, :].rearrange("p a n -> p (a n)") if t == 1 else asum
                    if t > 1:
                        pool.wait_ge(*pool_asum.now(t - 1, b))
                    gp.tensor_tensor(asum, first, ring[:, 2 * (t % 2):2 * (t % 2) + 2, :]
                                     .rearrange("p a n -> p (a n)"), ALU.add).then_inc(*pool_asum.raise_(t))
                rstd(("L1b", 0), GT)
                rstd(("L1b", 1), GT)

        @block.scalar
        def _(act):
            sc = nc.scalar

            def copy(dst, src, scale=1.0):
                return sc.activation(dst, src, ACT.Copy, scale=scale)

            act.wait_ge(l_mod, 64)
            sc.activation(stats[:, 2:4, 0:4], cols[:, 0:2 * B].rearrange("p (l b) -> p l b", l=2), ACT.Silu)\
                .then_inc(u_act, 1)
            for q in range(4):
                act.wait_ge(l_moe[q], 16)
                w, o = (w1, q) if q < 2 else (w2, q - 2)
                copy(w[:, 0, o * 2048:(o + 1) * 2048], stage[:, q * 2048:(q + 1) * 2048]).then_inc(u_hi, 1)
            act.wait_ge(l_l1, 16)
            for w, at, n in L1_PARTS:
                copy(w[:, 0, :], stage[:, at:at + n]).then_inc(u_hi, 1)
            act.wait_ge(u_pe, 3)
            sc.activation(tmp[:, :, :].rearrange("p a n -> p (a n)"), ps[:, 4:6, :].rearrange("p a n -> p (a n)"),
                          ACT.Copy, scale=DH ** -0.5).then_inc(u_act, 1)
            act.wait_ge(u_pe, 4)
            copy(vout[:, :], ps[:, 0:4, :].rearrange("p a n -> p (a n)")).then_inc(u_act, 1)

            act.wait_ge(u_dve, 2)

            with act.Fori(0, B) as b:
                def from_psum(bank, dst, ev, job, func=ACT.Copy, **kw):
                    src = ps[:, bank, :]
                    sc.activation(dst, src, func, **kw).then_inc(*ev.raise_(job))

                def col(j):
                    return cols[:, j:j + 1]

                act.wait_ge(*act_y.before(("F", 1), b))
                copy(cols[:, :], modt[:, bass.ds(b * NCOL, NCOL)]).then_inc(*act_cols.raise_("cols"))
                act.wait_ge(*act_cols.now("cols", b))
                act.wait_ge(*pe_fin.before("s", b))
                for g in gs2:
                    act.wait_ge(*pe_prep.now(("h0T", g), b))
                    from_psum(g, misc[:, g, :], act_prep, ("h0T", g))
                act.wait_ge(*pe_prep.now("gram", b))
                copy(gs[:, :], ps[:, 6, 0:128]).then_inc(*act_prep.raise_("gram"))
                act.wait_ge(*dve_split.before((1, "h2", 3), b))
                for g in gs2:
                    act.wait_ge(*pe_prep.now(("h1T", g), b))
                    from_psum(g, ring[:, g, :], act_prep, ("h1T", g), ACT.Identity, scale=col(C1B0), bias=col(SB0))
                for g in gs2:
                    act.wait_ge(*dve_gap.now(g, b))
                    sc.activation(th[:, :], gap[:, :], ACT.Tanh, scale=0.5).then_inc(*act_prep.raise_(("th", g)))
                    act.wait_ge(*pe_prep.now(("wT", g), b))
                    copy(wT[:, g, :], ps[0:32, 6 + g, :]).then_inc(*act_prep.raise_(("wT", g)))

                for n in ns:
                    g, e = divmod(n, E)
                    for c in cs:
                        m = n * HC + c
                        act.wait_ge(*pe_hid.now(m, b))
                        act.wait_ge(*(dve_split.now(m - 4, b) if m >= 4 else dve_hT.now(("moe", 1), b)))
                        from_psum(2 + m % 4, ring[:, m % 4, :], act_gelu, m, ACT.Gelu,
                                  bias=b1[:, e * HC + c:e * HC + c + 1])
                    act.wait_ge(*pe_wb.now(n, b))
                    if n >= 2:
                        act.wait_ge(*dve_gated.now(n - 2, b))
                    from_psum(0, misc[:, n % 2, :], act_wb, n)
                    if n == 9:
                        act.wait_ge(*pool_acc.now(E - 1, b))
                        acc = hn[:, GT:T, :]
                        copy(acc, acc, scale=col(GB0)).then_inc(*act_gb.raise_(0))
                act.wait_ge(*pool_acc.now(2 * E - 1, b))
                copy(acc, acc, scale=col(GB0)).then_inc(*act_gb.raise_(1))

                def attnT_out(t):
                    if t == 0:
                        act.wait_ge(*pe_out.now(2 * E - 1, b))
                    for h in range(2):
                        act.wait_ge(*pe_attnT.now((t, h), b))
                        copy(attnT[:, 4 * h:4 * h + 4, t * 128:(t + 1) * 128],
                             ps[:, h, :].rearrange("p (k n) -> p k n", k=4)).then_inc(*act_attnT.raise_((t, h)))

                for t in range(T + 2):
                    if t < T:
                        act.wait_ge(*pe_maxT.now(t, b))
                        if t >= 1:
                            act.wait_ge(*pe_shift.now(t - 1, b))
                        copy(mTs, ps[0:32, 1, 0:128]).then_inc(*act_maxT.raise_(t))
                    if t >= 2:
                        attnT_out(t - 2)
                    if t < T:
                        act.wait_ge(*pe_shift.now(t, b))
                        if t >= 2:
                            act.wait_ge(*pe_attnT.now((t - 2, 1), b))
                            act.wait_ge(*pool_asum.now(max(t - 2, 1), b))
                        else:
                            act.wait_ge(*dve_split.now(G * E * HC - 1, b))
                        e0 = 2 * (t % 2)
                        k0 = 2 + 2 * (t % 2)
                        sc.activation(ring[:, e0:e0 + 2, :], ps[:, k0:k0 + 2, :], ACT.Exp)\
                            .then_inc(*act_exp.raise_(t))
                act.wait_ge(*pe_z.now(T - 1, b))
                act.wait_ge(*pool_asum.now(T - 2, b))
                copy(ring[:, 0:2, :], ps[:, 6:8, :]).then_inc(*act_z.raise_("z"))
                for g in gs2:
                    act.wait_ge(*pe_fin.now(("O", g), b))
                    act.wait_ge(*pool_acc.now(2 * E - 1, b))
                    from_psum(2 + g, tmp[:, g, :], act_y, ("A", g), ACT.Identity, scale=col(GA1), bias=col(GABO))
                for g in gs2:
                    act.wait_ge(*pe_res.now(("h3T", g), b))
                    from_psum(0, ring[:, g, :], act_h3T, g, ACT.Identity, scale=col(C1B1), bias=col(SB1))

                def hidden(g, part):
                    for c in cs:
                        m = 2 * c if part == "ab" else {"h1": 8, "h2": 12}[part] + c
                        act.wait_ge(*pe_ffn.now((g, "a" if part == "ab" else part, c), b))
                        if part == "ab":
                            if c >= 2:
                                act.wait_ge(*dve_prod.now((g, c - 2), b))
                            else:
                                act.wait_ge(*(dve_split.now((0, "h2", 3), b) if g else dve_hT.now(("ffn", 1), b)))
                            sc.activation(ring[:, 2 * (c % 2), :], ps[:, 2 + m % 4, :], ACT.Silu,
                                          scale=fs[:, c:c + 1]).then_inc(*act_ffn.raise_((g, part, c)))
                        else:
                            act.wait_ge(*dve_split.now((g, "ab", 2 + c // 2) if part == "h1" else (g, "h1", c), b))
                            s = HC * (2 if part == "h1" else 3) + c
                            sc.activation(ring[:, c, :], ps[:, 2 + m % 4, :], ACT.Gelu,
                                          scale=fs[:, s:s + 1]).then_inc(*act_ffn.raise_((g, part, c)))

                def out_y(g):
                    act.wait_ge(*pe_ffn.now((g, "y"), b))
                    from_psum(6 + g, tmp[:, g, :], act_y, ("F", g), ACT.Copy, scale=col(GBS3))

                hidden(0, "ab")
                hidden(0, "h1")
                hidden(0, "h2")
                hidden(1, "ab")
                out_y(0)
                hidden(1, "h1")
                hidden(1, "h2")
                out_y(1)

        @block.vector
        def _(dve):
            v = nc.vector
            flat = "p a n -> p (a n)"
            for q in range(4):
                dve.wait_ge(u_hi, q + 1)
                w, o = (w1, q) if q < 2 else (w2, q - 2)
                v.tensor_tensor(w[:, 1, o * 2048:(o + 1) * 2048], stage[:, q * 2048:(q + 1) * 2048],
                                f(w[:, 0, o * 2048:(o + 1) * 2048]), ALU.subtract).then_inc(u_lo, 1)
            chain = [0]
            u_chain = sem("setup_chain")

            def link(ins_):
                chain[0] += 1
                ins_.then_inc(u_chain, 1)
                dve.wait_ge(u_chain, chain[0])

            dve.wait_ge(u_pool, 15)
            dve.wait_ge(l_small, 8 * 16)
            link(v.tensor_copy(onehot[:, :], tmp[0:32, :, :].rearrange(flat)))
            link(v.tensor_copy(gatew[:, 0, :], gs[:, 0:E]))
            link(v.tensor_tensor(gatew[:, 1, :], gs[:, 0:E], f(gatew[:, 0, :]), ALU.subtract))
            dve.wait_ge(u_pe, 1)
            link(v.tensor_copy(wwt[:, :], ps[:, 6, 0:128]))
            dve.wait_ge(u_pe, 2)
            raw = misc[0:B, :, :].rearrange(flat)
            raw1 = xb[0:B, :, :].rearrange("p t d -> p (t d)")
            m = [raw[:, 0:768].rearrange("p (j d) -> p j d", j=6), raw1[:, 0:768].rearrange("p (j d) -> p j d", j=6)]
            for l in range(2):
                for j in range(2):
                    link(v.tensor_copy(m[l][:, 3 * j:3 * j + 3, :].rearrange("p j d -> p (j d)"),
                                       ps[0:B, 2 * l + j, 0:384]))
                for j in (1, 4):
                    link(v.tensor_scalar(m[l][:, j, :], m[l][:, j, :], 1.0, None, ALU.add))
                for j in (2, 5):
                    s0, s1 = cmat[0:B, 2, :], cmat[0:B, 3, :]
                    link(v.tensor_scalar(s0, m[l][:, j, :], 0.0, 2.0, ALU.is_ge, ALU.mult))
                    link(v.scalar_tensor_tensor(s1, m[l][:, j, :], -1.0, m[l][:, j, :], ALU.mult, ALU.max))
                    link(v.tensor_scalar(s1, s1, 0.25, None, ALU.max))
                    link(v.scalar_tensor_tensor(m[l][:, j, :], s0, -1.0, s1, ALU.add, ALU.mult))
            link(v.tensor_copy(rows[0:B, R_C1A0, :], m[0][:, 1, :]))
            link(v.tensor_copy(rows[0:B, R_SA0, :], m[0][:, 0, :]))
            link(v.tensor_tensor(rows[0:B, R_GG, :], m[0][:, 2, :], cmat[0:B, 0, :], ALU.mult))
            link(v.tensor_tensor(rows[0:B, R_GBETA, :], m[0][:, 2, :], cmat[0:B, 1, :], ALU.mult))
            link(v.tensor_copy(rows[0:B, R_C1A1, :], m[1][:, 1, :]))
            v.tensor_copy(rows[0:B, R_SA1, :], m[1][:, 0, :]).then_inc(u_dve, 1)
            dve.wait_ge(u_pe, 5)
            mt = modt[:, :].rearrange("p (b j) -> p b j", b=B)
            pt = ps[:, 7, 0:7 * B].rearrange("p (j b) -> p b j", b=B)
            link(v.tensor_copy(mt[:, :, C1B0:GA1 + 1], pt[:, :, 0:4]))
            link(v.tensor_scalar(mt[:, :, GABO], pt[:, :, 3], stats[:, 0, 0:1], None, ALU.mult))
            link(v.tensor_copy(mt[:, :, C1B1:SB1 + 1], pt[:, :, 4:6]))
            v.tensor_scalar(mt[:, :, GBS3], pt[:, :, 6], fs[:, 4 * HC:4 * HC + 1], None, ALU.mult).then_inc(u_dve, 1)
            for i, (w, at, n) in enumerate(L1_PARTS):
                dve.wait_ge(u_hi, 5 + i)
                v.tensor_tensor(w[:, 1, :], stage[:, at:at + n], f(w[:, 0, :]), ALU.subtract).then_inc(u_lo, 1)
            dve.wait_ge(u_act, 2)
            a_raw = tmp[:, :, :].rearrange(flat)
            link(v.tensor_copy(anch[:, 0, :], a_raw))
            v.tensor_tensor(anch[:, 1, :], a_raw, f(anch[:, 0, :]), ALU.subtract).then_inc(u_dve, 1)

            with dve.Fori(0, B) as b:
                steps = [0]

                def step(ins_):
                    ins_.then_inc(*dve_step.raise_(steps[0]))
                    steps[0] += 1
                    return steps[0] - 1

                def settle(ins_):
                    dve.wait_ge(*dve_step.now(step(ins_), b))

                def settle_alone(ins_):
                    settle(ins_)
                    v.memset(pad[:, :], 0.0)

                def layer_norm(k, srcs, dst):
                    n = len(srcs)
                    for i, s in enumerate(srcs):
                        last = v.bn_stats(stats[:, i, :], s)
                    settle_alone(last)
                    for i in range(n):
                        last = v.bn_aggr(mv[:, i, :], stats[:, i, :])
                    settle(last)
                    v.tensor_scalar(ve[:, 0:n], mv[:, 0:n, 1], EPS, None, ALU.add).then_inc(*dve_var.raise_(k))
                    dve.wait_ge(*pool_rs.now(k, b))
                    for i, s in enumerate(srcs):
                        last = v.tensor_scalar(dst[:, i, :], s, mv[:, i, 0:1], rs[:, i:i + 1],
                                               ALU.subtract, ALU.mult)
                    last.then_inc(*dve_norm.raise_(k))

                def tiles(x, g):
                    return [x[:, t, :] for t in range(g * GT, (g + 1) * GT)]

                def split(dst_hi, dst_lo, src, ev, job):
                    settle(v.tensor_copy(dst_hi, src))
                    v.tensor_tensor(dst_lo, src, f(dst_hi), ALU.subtract).then_inc(*ev.raise_(job))

                dve.wait_ge(*x_loaded.now("x", b))
                dve.wait_ge(*pe_res.before(("h3T", 1), b))
                layer_norm("L0a", tiles(xa, 0) + tiles(xa, 1), hn)
                dve.wait_ge(*pe_prep.now("P", b))
                v.scalar_tensor_tensor(pmat[:, :], ps[:, 7, 0:128], D ** -0.5, ident[:, :], ALU.mult, ALU.add)\
                    .then_inc(*dve_p.raise_("P"))
                for g in gs2:
                    dve.wait_ge(*pe_prep.now(("jn", g), b))
                layer_norm("L0i", [ps[:, g, t * 128:(t + 1) * 128] for g in gs2 for t in range(GT)], hn)
                dve.wait_ge(*dve_norm.now("L0i", b))
                settle(v.tensor_tensor(hn[:, :, :], hn[:, :, :],
                                       rows[:, R_GG, :].unsqueeze(1).broadcast_to([128, T, 128]), ALU.mult))
                dve.wait_ge(*pool_beta.now("x", b))
                settle(v.tensor_tensor(xa[:, :, :], xa[:, :, :], hn[:, :, :], ALU.add))
                layer_norm("L0b", tiles(xa, 0) + tiles(xa, 1), hn)
                dve.wait_ge(*pe_ffn.before((1, "b", 3), b))
                for g in gs2:
                    dve.wait_ge(*act_prep.now(("h1T", g), b))
                    split(hT[:, 0, g, :], hT[:, 1, g, :], ring[:, g, :], dve_hT, ("moe", g))

                for g in gs2:
                    def over_e(ap):
                        return ap.unsqueeze(2).broadcast_to([128, GT, E])

                    dve.wait_ge(*pe_prep.now(("gate", g), b))
                    settle_alone(v.tensor_tensor(gt[:, :, :], ps[:, 6 + g, 0:GT * E].rearrange("p (t e) -> p t e", t=GT),
                                           gateb[:, :].unsqueeze(1).broadcast_to([128, GT, E]), ALU.add))
                    for t in range(GT):
                        last = v.max(top[:, t, :], gt[:, t, :])
                    settle(last)
                    if g:
                        dve.wait_ge(*act_prep.now(("th", 0), b))
                    v.tensor_tensor(gap[:, :], top[:, :, 0], top[:, :, 1], ALU.subtract)\
                        .then_inc(*dve_gap.raise_(g))
                    v.tensor_tensor(above[:, :, :], gt[:, :, :], over_e(top[:, :, 1]), ALU.is_gt)
                    settle(v.tensor_tensor(equal[:, :, :], gt[:, :, :], over_e(top[:, :, 1]), ALU.is_equal))
                    settle_alone(v.tensor_tensor(equal[:, :, :], equal[:, :, :],
                                                 order[:, :].unsqueeze(1).broadcast_to([128, GT, E]), ALU.mult))
                    for t in range(GT):
                        last = v.max(tops[:, t, :], equal[:, t, :])
                    settle(last)
                    settle(v.tensor_tensor(wa[:, 0, :], top[:, :, 0], top[:, :, 1], ALU.is_gt))
                    settle(v.tensor_tensor(wa[:, 1, :], tops[:, :, 0], tops[:, :, 1], ALU.subtract))
                    settle(v.tensor_tensor(wa[:, 0, :], wa[:, 0, :], wa[:, 1, :], ALU.mult))
                    settle(v.tensor_tensor(wa[:, 0, :], wa[:, 0, :], tops[:, :, 1], ALU.add))
                    settle(v.tensor_tensor(equal[:, :, :], equal[:, :, :], over_e(wa[:, 0, :]), ALU.is_ge))
                    dve.wait_ge(*act_prep.now(("th", g), b))
                    v.tensor_scalar(wa[:, 0, :], th[:, :], 0.5, 0.5, ALU.mult, ALU.add)
                    settle(v.tensor_scalar(wa[:, 1, :], th[:, :], -0.5, 0.5, ALU.mult, ALU.add))
                    v.tensor_tensor(above[:, :, :], above[:, :, :], over_e(wa[:, 0, :]), ALU.mult)
                    settle(v.tensor_tensor(equal[:, :, :], equal[:, :, :], over_e(wa[:, 1, :]), ALU.mult))
                    settle(v.tensor_tensor(above[:, :, :], above[:, :, :], equal[:, :, :], ALU.add))
                    if g:
                        dve.wait_ge(*pe_prep.now(("wT", 0), b))
                    for r in range(2):
                        last = v.tensor_copy(w32[:, :, 0:8, r], above[:, :, :])
                    settle(last)
                    for r in range(2):
                        last = v.tensor_tensor(w32[:, :, 8:16, r], above[:, :, :], f(w32[:, :, 0:8, r]), ALU.subtract)
                    last.then_inc(*dve_w.raise_(g))

                def split_hidden(job, slot, s, c):
                    split(hid[:, s, c, 0, :], hid[:, s, c, 1, :], ring[:, slot, :], dve_split, job)

                def gated(n):
                    dve.wait_ge(*pe_out.now(n, b))
                    dve.wait_ge(*act_wb.now(n, b))
                    if n % E == 0:
                        if n:
                            dve.wait_ge(*pe_res.now(("M", 0), b))
                        dst = hn[:, GT:T, :].rearrange("p t d -> p (t d)")
                    else:
                        if (n - 2) % E and n >= 3:
                            dve.wait_ge(*pool_acc.now(n - 2, b))
                        dst = tmp[:, n % 2, :]
                    v.scalar_tensor_tensor(dst, ps[:, 6 + n % 2, :], b2[:, n % E:n % E + 1], misc[:, n % 2, :],
                                           ALU.add, ALU.mult).then_inc(*dve_gated.raise_(n))

                def residual(p, g, src):
                    dve.wait_ge(*pe_res.now((p, g), b))
                    if p == "M":
                        dve.wait_ge(*out_stored[g].before("out", b))
                    xg = xb[:, g * GT:(g + 1) * GT, :]
                    v.tensor_tensor(xg, src[:, g * GT:(g + 1) * GT, :],
                                    ps[:, 1, :].rearrange("p (t d) -> p t d", t=GT), ALU.add)\
                        .then_inc(*dve_res.raise_((p, g)))
                    dve.wait_ge(*dve_res.now((p, g), b))

                def hT_attn(g):
                    dve.wait_ge(*pe_res.now(("h2T", g), b))
                    dve.wait_ge(*pe_hid.now(g * 32 + 31, b))
                    split(hT[:, 0, g, :], hT[:, 1, g, :], ps[:, 1, :], dve_hT, ("attn", g))

                dve.wait_ge(*pe_ffn.before((1, "y"), b))
                for n in ns:
                    for c in cs:
                        mm = n * HC + c
                        dve.wait_ge(*act_gelu.now(mm, b))
                        if c == 0 and n >= 2:
                            dve.wait_ge(*pe_out.now(n - 2, b))
                        split_hidden(mm, mm % 4, n % 2, c)
                    if n:
                        gated(n - 1)
                    if n == 11:
                        residual("M", 0, xa)
                        layer_norm(("L1a", 0), tiles(xb, 0), hn[:, 0:GT, :])
                    if n == 13:
                        hT_attn(0)
                gated(2 * E - 1)

                def neg_max(t):
                    dve.wait_ge(*pe_logits.now(t, b))
                    k0 = 2 + 2 * (t % 2)
                    settle(v.tensor_reduce(nmax[:, :], ps[:, k0:k0 + 2, :].rearrange("p k (h a) -> p (k h) a", a=A),
                                           X, ALU.max, negate=True))
                    if t:
                        dve.wait_ge(*pe_maxT.now(t - 1, b))
                    settle(v.tensor_copy(m32[:, 0:H], nmax[:, :]))
                    v.tensor_tensor(m32[:, H:2 * H], nmax[:, :], f(m32[:, 0:H]), ALU.subtract)\
                        .then_inc(*dve_max.raise_(t))

                def normalize(t):
                    dve.wait_ge(*act_exp.now(t, b))
                    e = ring[:, 2 * (t % 2):2 * (t % 2) + 2, :].rearrange("p k (h a) -> p (k h) a", a=A)
                    settle(v.tensor_reduce(lsum[:, :], e, X, ALU.add))
                    settle(v.reciprocal(lrec[:, :], lsum[:, :]))
                    v.tensor_tensor(e, e, lrec[:, :].unsqueeze(2).broadcast_to([128, H, A]), ALU.mult)\
                        .then_inc(*dve_attn.raise_(t))

                neg_max(0)
                residual("M", 1, xa)
                layer_norm(("L1a", 1), tiles(xb, 1), hn[:, GT:T, :])
                for t in range(1, T + 1):
                    if t < T:
                        neg_max(t)
                    normalize(t - 1)
                    if t == 3:
                        hT_attn(1)
                dve.wait_ge(*pe_fin.now("s", b))
                TINY = 2.938737e-39
                v.tensor_scalar(srec[:, 0, :], ps[:, 1, 0:AC], TINY, None, ALU.is_ge)
                settle(v.tensor_scalar(srec[:, 1, :], ps[:, 1, 0:AC], TINY, None, ALU.max))
                settle(v.reciprocal(srec[:, 2, :], srec[:, 1, :]))
                settle(v.tensor_tensor(srec[:, 2, :], srec[:, 2, :], srec[:, 0, :], ALU.mult))
                for j in range(4):
                    dve.wait_ge(*pe_fin.now(("C", j), b))
                    src = ps[:, 2 + j, :].rearrange("p (k n) -> p k n", k=2)
                    for half in range(2):
                        p = slice(64 * half, 64 * half + 64)
                        last = v.tensor_tensor(cmat[p, 2 * j:2 * j + 2, :], src[p, :, half * 128:half * 128 + 128],
                                               srec[p, 2, 2 * j:2 * j + 2].unsqueeze(2).broadcast_to([64, 2, 128]),
                                               ALU.mult)
                    last.then_inc(*dve_c.raise_(j))
                for g in gs2:
                    residual("A", g, xb)
                    layer_norm(("L1b", g), tiles(xb, g), hn[:, g * GT:(g + 1) * GT, :])
                for g in gs2:
                    dve.wait_ge(*act_h3T.now(g, b))
                    split(hT[:, 0, g, :], hT[:, 1, g, :], ring[:, g, :], dve_hT, ("ffn", g))

                sets = {(0, "ab"): 0, (0, "h1"): 1, (0, "h2"): 0, (1, "ab"): 1, (1, "h1"): 0, (1, "h2"): 1}
                free = {(0, "ab"): (pe_fin, ("O", 1)), (0, "h1"): (pe_fin, ("O", 1)), (0, "h2"): (pe_ffn, (0, "h1", 3)),
                        (1, "ab"): (pe_ffn, (0, "h2", 3)), (1, "h1"): (pe_ffn, (0, "y")),
                        (1, "h2"): (pe_ffn, (1, "h1", 3))}

                def hidden(g, part):
                    ev, job = free[g, part]
                    dve.wait_ge(*ev.now(job, b))
                    for c in cs:
                        dve.wait_ge(*act_ffn.now((g, part, c), b))
                        slot = c
                        if part == "ab":
                            dve.wait_ge(*pe_ffn.now((g, "b", c), b))
                            slot = 2 * (c % 2) + 1
                            v.scalar_tensor_tensor(ring[:, slot, :], ps[:, 2 + (2 * c + 1) % 4, :],
                                                   fs[:, HC + c:HC + c + 1], ring[:, slot - 1, :], ALU.mult, ALU.mult)\
                                .then_inc(*dve_prod.raise_((g, c)))
                            dve.wait_ge(*dve_prod.now((g, c), b))
                        split_hidden((g, part, c), slot, sets[g, part], c)

                hidden(0, "ab")
                hidden(0, "h1")
                hidden(0, "h2")
                hidden(1, "ab")
                hidden(1, "h1")
                residual("F", 0, xb)
                hidden(1, "h2")
                residual("F", 1, xb)
                assert steps[0] == DVE_STEPS, steps[0]

        @block.tensor
        def _(pe):
            te = nc.tensor
            pe.wait_ge(l_small, 8 * 16)
            te.matmul(ps[:, 6, 0:128], hn[:, 0, :], pmat[:, :], start=True, stop=True).then_inc(u_pe, 1)
            pe.wait_ge(u_act, 1)
            wm = ring[:, 0:3, :].rearrange("p a n -> p (a n)")
            for l in range(2):
                for j in range(2):
                    last = te.matmul(ps[0:B, 2 * l + j, 0:384], stats[:, 2 + l, 0:4],
                                     wm[:, 768 * l + 384 * j:768 * l + 384 * (j + 1)], start=True, stop=True)
            last.then_inc(u_pe, 1)
            pe.wait_ge(l_emb, 4 * 16)
            pe.wait_ge(u_dve, 1)
            w_a = stage[0:64, EMB + 2048:EMB + 2048 + A]
            for h in range(H):
                last = te.matmul(ps[:, 4 + h // 8, (h % 8) * A:(h % 8 + 1) * A],
                                 stage[0:64, EMB + h * 128:EMB + (h + 1) * 128], w_a, start=True, stop=True)
            last.then_inc(u_pe, 1)
            for h in range(H):
                w_o = (hn if h < 8 else xb)[64:128, h % 8, :]
                last = te.matmul(ps[:, h // 4, (h % 4) * 128:(h % 4 + 1) * 128],
                                 stage[64:128, EMB + h * 128:EMB + (h + 1) * 128], w_o, start=True, stop=True)
            last.then_inc(u_pe, 1)
            m0 = misc[0:B, :, :].rearrange("p a n -> p (a n)")
            m1 = xb[0:B, :, :].rearrange("p t d -> p (t d)")
            for j, (src, at) in enumerate([(m0, 4), (m0, 3), (m0, 5), (m1, 2), (m1, 4), (m1, 3), (m1, 5)]):
                last = te.transpose(ps[:, 7, j * B:(j + 1) * B], src[:, at * 128:(at + 1) * 128], ident[0:B, 0:B])
            last.then_inc(u_pe, 1)
            pe.wait_ge(u_dve, 3)
            pe.wait_ge(u_lo, 8)
            pe.wait_ge(u_act, 3)

            with pe.Fori(0, B) as b:
                def transposes(bank, srcs, ev, job, rows_=128):
                    for i, s in enumerate(srcs):
                        last_ = te.transpose(ps[0:rows_, bank, i * 128:(i + 1) * 128], s, ident[:, :])
                    last_.then_inc(*ev.raise_(job))

                def three(out_, w, x, first, last_):
                    te.matmul(out_, w(0), x(0), start=first, stop=False)
                    te.matmul(out_, w(0), x(1), start=False, stop=False)
                    return te.matmul(out_, w(1), x(0), start=False, stop=last_)

                def tiles(x, g):
                    return [x[:, t, :] for t in range(g * GT, (g + 1) * GT)]

                def quarters(x):
                    return [x[:, t * 128:(t + 1) * 128] for t in range(GT)]

                for g in gs2:
                    pe.wait_ge(*pool_h.now(("L0", g), b))
                    pe.wait_ge(*(dve_res.before(("F", 1), b) if g else act_attnT.before((T - 1, 0), b)))
                    transposes(g, tiles(hn, g), pe_prep, ("h0T", g))
                pe.wait_ge(*act_y.before(("F", 1), b))
                for t in ts:
                    last = te.matmul(ps[:, 6, 0:128], hn[:, t, :], hn[:, t, :], start=t == 0, stop=t == T - 1)
                last.then_inc(*pe_prep.raise_("gram"))
                pe.wait_ge(*act_prep.now("gram", b))
                te.matmul(ps[:, 7, 0:128], wwt[:, :], gs[:, :], start=True, stop=True).then_inc(*pe_prep.raise_("P"))
                pe.wait_ge(*dve_p.now("P", b))
                for g in gs2:
                    pe.wait_ge(*act_prep.now(("h0T", g), b))
                    for t in range(GT):
                        last = te.matmul(ps[:, g, t * 128:(t + 1) * 128], misc[:, g, t * 128:(t + 1) * 128],
                                         pmat[:, :], start=True, stop=True)
                    last.then_inc(*pe_prep.raise_(("jn", g)))
                pe.wait_ge(*dve_norm.now("L0b", b))
                for g in gs2:
                    transposes(g, tiles(hn, g), pe_prep, ("h1T", g))
                for g in gs2:
                    pe.wait_ge(*dve_hT.now(("moe", g), b))
                    for t in range(GT):
                        last = three(ps[:, 6 + g, t * E:(t + 1) * E],
                                     lambda i: hT[:, i, g, t * 128:(t + 1) * 128],
                                     lambda i: gatew[:, i, :], True, True)
                    last.then_inc(*pe_prep.raise_(("gate", g)))
                for g in gs2:
                    pe.wait_ge(*dve_w.now(g, b))
                    transposes(6 + g, [f(w32[:, t, :, :]).rearrange("p a r -> p (a r)") for t in range(GT)],
                               pe_prep, ("wT", g), 32)

                def first_product(n):
                    g, e = divmod(n, E)
                    for c in cs:
                        mm = n * HC + c
                        pe.wait_ge(*(act_gelu.now(mm - 4, b) if mm >= 4 else act_ffn.before((1, "h2", c), b)))
                        at = (e * HC + c) * 128
                        three(ps[:, 2 + mm % 4, :], lambda i: w1[:, i, at:at + 128], lambda i: hT[:, i, g, :],
                              True, True).then_inc(*pe_hid.raise_(mm))

                def spread_gates(n):
                    g, e = divmod(n, E)
                    pe.wait_ge(*(act_wb.now(n - 1, b) if n else act_prep.now(("wT", 1), b)))
                    te.matmul(ps[:, 0, :], onehot[:, e * 128:(e + 1) * 128], wT[:, g, :], start=True, stop=True)\
                        .then_inc(*pe_wb.raise_(n))

                def second_product(n):
                    e = n % E
                    if n >= 2:
                        pe.wait_ge(*dve_gated.now(n - 2, b))
                    for c in cs:
                        pe.wait_ge(*dve_split.now(n * HC + c, b))
                        at = (e * HC + c) * 128
                        last_ = three(ps[:, 6 + n % 2, :], lambda i: w2[:, i, at:at + 128],
                                      lambda i: hid[:, n % 2, c, i, :], c == 0, c == HC - 1)
                    last_.then_inc(*pe_out.raise_(n))

                acc = hn[:, GT:T, :].rearrange("p t d -> p (t d)")
                for n in ns:
                    first_product(n)
                    spread_gates(n)
                    if n:
                        second_product(n - 1)
                    if n == 10:
                        pe.wait_ge(*act_gb.now(0, b))
                        transposes(1, quarters(acc), pe_res, ("M", 0))
                    if n == 12:
                        pe.wait_ge(*pool_h.now(("L1", 0), b))
                        transposes(1, tiles(hn, 0), pe_res, ("h2T", 0))
                second_product(2 * E - 1)

                def logits(t):
                    pe.wait_ge(*dve_hT.now(("attn", t // GT), b))
                    pe.wait_ge(*(act_exp.now(t - 2, b) if t >= 2 else act_gelu.now(G * E * HC - 1, b)))
                    tok = slice((t % GT) * 128, (t % GT + 1) * 128)
                    for h in range(2):
                        last_ = three(ps[:, 2 + 2 * (t % 2) + h, :], lambda i: hT[:, i, t // GT, tok],
                                      lambda i: anch[:, i, h * 512:(h + 1) * 512], True, True)
                    last_.then_inc(*pe_logits.raise_(t))

                def max_transposed(t):
                    pe.wait_ge(*dve_max.now(t, b))
                    if t == 3:
                        pe.wait_ge(*dve_hT.now(("attn", 1), b))
                    if t >= 3:
                        pe.wait_ge(*act_attnT.now((t - 3, 1), b))
                    transposes(1, [f(m32[:, :])], pe_maxT, t, 32)

                def shift(t):
                    pe.wait_ge(*act_maxT.now(t, b))
                    for h in range(2):
                        last_ = te.matmul(ps[:, 2 + 2 * (t % 2) + h, :], mTs, onehot[:, h * 512:(h + 1) * 512],
                                          start=False, stop=True, skip_group_check=True)
                    last_.then_inc(*pe_shift.raise_(t))

                def gather(t):
                    pe.wait_ge(*dve_attn.now(t, b))
                    for h in range(2):
                        last_ = te.matmul(ps[:, 6 + h, :], hn[:, t, :], ring[:, 2 * (t % 2) + h, :],
                                          start=t == 0, stop=t == T - 1)
                    last_.then_inc(*pe_z.raise_(t))

                def attn_transposed(t):
                    for h in range(2):
                        if t:
                            pe.wait_ge(*act_attnT.now((t - 1, h), b))
                        elif h == 0:
                            pe.wait_ge(*act_wb.now(2 * E - 1, b))
                        if h == 1 and t + 2 < T:
                            pe.wait_ge(*act_maxT.now(t + 2, b))
                        transposes(h, quarters(ring[:, 2 * (t % 2) + h, :]), pe_attnT, (t, h))

                logits(0)
                pe.wait_ge(*act_gb.now(1, b))
                pe.wait_ge(*dve_hT.now(("attn", 0), b))
                transposes(1, quarters(acc), pe_res, ("M", 1))
                pe.wait_ge(*dve_gated.now(2 * E - 1, b))
                for t in range(T + 2):
                    if t >= 2:
                        gather(t - 2)
                    if t < T:
                        if t == 0:
                            pe.wait_ge(*dve_res.now(("M", 1), b))
                        max_transposed(t)
                    if t >= 2:
                        attn_transposed(t - 2)
                    if t + 1 < T:
                        logits(t + 1)
                    if t < T:
                        shift(t)
                    if t == 2:
                        pe.wait_ge(*pool_h.now(("L1", 1), b))
                        pe.wait_ge(*act_attnT.now((0, 1), b))
                        transposes(1, tiles(hn, 1), pe_res, ("h2T", 1))
                pe.wait_ge(*pool_asum.now(T - 1, b))
                pe.wait_ge(*act_attnT.now((T - 1, 1), b))
                asum = misc[:, :, :].rearrange("p a n -> p (a n)")
                for k in range(AC):
                    last = te.matmul(ps[:, 1, k:k + 1], asum[:, k * 128:(k + 1) * 128], ones[:, :], start=True, stop=True)
                last.then_inc(*pe_fin.raise_("s"))
                pe.wait_ge(*act_z.now("z", b))
                zT = ring[:, 0:2, :].rearrange("p a n -> p (a n)")
                for j in range(4):
                    for k in range(2):
                        q = 2 * j + k
                        last = te.matmul(ps[:, 2 + j, k * 256:(k + 1) * 256], zT[:, q * 128:(q + 1) * 128],
                                         vout[:, q * 256:(q + 1) * 256], start=True, stop=True)
                    last.then_inc(*pe_fin.raise_(("C", j)))
                pe.wait_ge(*dve_c.now(3, b))
                for g in gs2:
                    for k in range(AC):
                        last = te.matmul(ps[:, 2 + g, :], cmat[:, k, :], attnT[:, k, g * GW:(g + 1) * GW],
                                         start=k == 0, stop=k == AC - 1)
                    last.then_inc(*pe_fin.raise_(("O", g)))
                for g in gs2:
                    pe.wait_ge(*act_y.now(("A", g), b))
                    if g:
                        pe.wait_ge(*dve_res.now(("A", 0), b))
                    transposes(1, quarters(tmp[:, g, :]), pe_res, ("A", g))
                for g in gs2:
                    pe.wait_ge(*dve_norm.now(("L1b", g), b))
                    if g:
                        pe.wait_ge(*act_h3T.now(0, b))
                    transposes(0, tiles(hn, g), pe_res, ("h3T", g))

                def bank_read(g, m_):
                    if m_ < 4:
                        return act_ffn.now((0, "h2", m_), b) if g else act_y.now(("A", 1), b)
                    m_ -= 4
                    if m_ >= 8:
                        return act_ffn.now((g, "h1", m_ - 8), b)
                    return dve_prod.now((g, m_ // 2), b) if m_ % 2 else act_ffn.now((g, "ab", m_ // 2), b)

                def first_layer(g):
                    pe.wait_ge(*dve_hT.now(("ffn", g), b))
                    for c in cs:
                        for k in range(2):
                            m_ = 2 * c + k
                            pe.wait_ge(*bank_read(g, m_))
                            at = (k * HC + c) * 128
                            three(ps[:, 2 + m_ % 4, :], lambda i: fab[:, i, at:at + 128],
                                  lambda i: hT[:, i, g, :], True, True).then_inc(*pe_ffn.raise_((g, "ab"[k], c)))

                def hidden_layer(g, part, w, src, src_set, base):
                    for pair in range(2):
                        for kc in cs:
                            pe.wait_ge(*dve_split.now((g, src, kc), b))
                            for o in (2 * pair, 2 * pair + 1):
                                if kc == 0:
                                    pe.wait_ge(*bank_read(g, base + o))
                                at = kc * 512 + o * 128
                                last_ = three(ps[:, 2 + (base + o) % 4, :], lambda i: w[:, i, at:at + 128],
                                              lambda i: hid[:, src_set, kc, i, :], kc == 0, kc == HC - 1)
                                if kc == HC - 1:
                                    last_.then_inc(*pe_ffn.raise_((g, part, o)))

                def last_layer(g, src_set):
                    for kc in cs:
                        pe.wait_ge(*dve_split.now((g, "h2", kc), b))
                        last_ = three(ps[:, 6 + g, :], lambda i: fy[:, i, kc * 128:(kc + 1) * 128],
                                      lambda i: hid[:, src_set, kc, i, :], kc == 0, kc == HC - 1)
                    last_.then_inc(*pe_ffn.raise_((g, "y")))

                def residual_transposed(g):
                    pe.wait_ge(*act_y.now(("F", g), b))
                    pe.wait_ge(*dve_res.now(("F", 0) if g else ("A", 1), b))
                    transposes(1, quarters(tmp[:, g, :]), pe_res, ("F", g))

                first_layer(0)
                hidden_layer(0, "h1", fh1, "ab", 0, 8)
                hidden_layer(0, "h2", fh2, "h1", 1, 12)
                first_layer(1)
                last_layer(0, 0)
                hidden_layer(1, "h1", fh1, "ab", 1, 8)
                residual_transposed(0)
                hidden_layer(1, "h2", fh2, "h1", 0, 12)
                last_layer(1, 1)
                residual_transposed(1)


def kernel(**inputs):
    import numpy as np
    import concourse.bacc as bacc
    from concourse.bass_utils import run_bass_kernel_spmd

    i = {k: np.asarray(v) for k, v in inputs.items()}

    def c(a):
        return np.ascontiguousarray(a)

    def out_chunks(w, k):
        o, n = w.shape
        return w.T.reshape(k, 128, o).transpose(1, 0, 2).reshape(128, k * o)

    emb = i["L1_attn_W_emb"]
    heads = emb.reshape(2, H, DH, D).transpose(0, 2, 1, 3).reshape(2 * DH, H * D)
    scales = np.concatenate([i[f"L1_ffn_{n}_s"].reshape(-1, 128).T for n in ("w1", "w2", "h1", "h2", "w3")], axis=1)
    arrays = {
        "x": c(i["L0_attn_J"]),
        "W_Q": c(i["L0_attn_W_Q"]), "W_K": c(i["L0_attn_W_K"]),
        "gamma": c(i["L0_attn_gamma"]), "beta": c(i["L0_attn_beta"]),
        "gate_w": c(i["L0_ffn_gate_w"].T), "gate_b": c(i["L0_ffn_gate_b"]),
        "w1": c(i["L0_ffn_w1"].transpose(1, 0, 2).reshape(128, -1)),
        "b1": c(i["L0_ffn_b1"].reshape(E * HC, 128).T),
        "w2": c(i["L0_ffn_w2"].reshape(E * HC, 128, D).transpose(1, 0, 2).reshape(128, -1)),
        "b2": c(i["L0_ffn_b2"].T),
        "cT": c(np.concatenate([i["L0_c"].T, i["L1_c"].T], axis=1)),
        "wmod": c(np.concatenate([i["L0_wmod"], i["L1_wmod"]], axis=1)),
        "w_emb": c(heads),
        "w_anchor": c(i["L1_attn_W_anchor"].T),
        "w_out": c(i["L1_attn_W_out"].reshape(D, H, DH).transpose(2, 1, 0)),
        "b_out": c(i["L1_attn_b_out"].reshape(D, 1)),
        "ffn": c(np.concatenate([i["L1_ffn_w1_w"].T, i["L1_ffn_w2_w"].T, out_chunks(i["L1_ffn_h1_w"], 4),
                                 out_chunks(i["L1_ffn_h2_w"], 4), out_chunks(i["L1_ffn_w3_w"], 4)], axis=1)),
        "scales": c(scales),
    }
    nc = bacc.Bacc("TRN2", target_bir_lowering=False, num_devices=1)
    aps = {k: nc.dram_tensor(f"in_{k}", a.shape, mybir.dt.from_np(a.dtype), kind="ExternalInput").ap()
           for k, a in arrays.items()}
    out = nc.dram_tensor("out_x", (B, N, D), F32, kind="ExternalOutput").ap()
    build(nc, aps, out)
    r = run_bass_kernel_spmd(nc, [{f"in_{k}": a for k, a in arrays.items()}], core_ids=[0])
    return r.results[0]["out_x"]
```

```python
from contextlib import ExitStack

import concourse.bass as bass
from concourse import mybir

ALU = mybir.AluOpType
ACT = mybir.ActivationFunctionType
F32 = mybir.dt.float32
F32R = mybir.dt.float32r
X = mybir.AxisListType.X

B, N, D = 4, 1024, 128
T = N // 128
G, GT = 2, 4
GW = GT * 128
E, HC = 8, 4
H, DH, A = 16, 64, 64
AC = H * A // 128
EPS = 1e-5
ACT_HI = (0, 2)
NC0, NC1 = 3, 5
NCOL = NC0 + NC1
C1B0, SB0, GB0, GA1, GABO, C1B1, SB1, GBS3 = range(NCOL)
R_C1A0, R_SA0, R_GG, R_GBETA, R_C1A1, R_SA1 = range(6)
TINY = 2.938737e-39
PREP_STEPS, MAIN_STEPS = 21, 94


class Events:

    def __init__(self, sem, jobs, by=1):
        self.sem, self.jobs, self.by = sem, list(jobs), by
        self.at = {job: i for i, job in enumerate(self.jobs)}
        self.raised = 0

    def credit(self):
        return len(self.jobs) * self.by

    def now(self, job, b):
        return self.sem, ((b + 1) * len(self.jobs) + self.at[job] + 1) * self.by

    def before(self, job, b):
        return self.sem, (b * len(self.jobs) + self.at[job] + 1) * self.by

    def raise_(self, job):
        assert self.jobs[self.raised % len(self.jobs)] == job, (job, self.jobs[self.raised])
        self.raised += 1
        return self.sem, self.by


def build(nc, ins, out):
    ctx = ExitStack()
    with ctx:
        def sb(name, shape, dt=F32):
            return ctx.enter_context(nc.sbuf_tensor(name, shape, dt))

        def sem(name):
            return ctx.enter_context(nc.semaphore(name))

        w1 = sb("w1", [128, 2, E * HC * 128], F32R)
        w2 = sb("w2", [128, 2, E * HC * 128], F32R)
        fab = sb("fab", [128, 2, 2 * HC * 128], F32R)
        fh1 = sb("fh1", [128, 2, HC * HC * 128], F32R)
        fh2 = sb("fh2", [128, 2, HC * HC * 128], F32R)
        fy = sb("fy", [128, 2, HC * 128], F32R)
        anch = sb("anch", [128, 2, H * A], F32R)
        gatew = sb("gatew", [128, 2, E], F32R)
        onehot = sb("onehot", [32, 1024], F32R)
        vout = sb("vout", [128, H * 128])
        wwt = sb("wwt", [128, 128])
        ident = sb("ident", [128, 128])
        ones = sb("ones", [128, 1])
        b1 = sb("b1", [128, E * HC])
        b2 = sb("b2", [128, E])
        gateb = sb("gateb", [128, E])
        order = sb("order", [128, E])
        fs = sb("fs", [128, 4 * HC + 1])
        neghalf = sb("neghalf", [128, T])
        modt = sb("modt", [128, B * NCOL])
        xa = sb("xa", [128, T, 128])
        xb = sb("xb", [128, T, 128])
        hn = sb("hn", [128, T, 128])
        hT = sb("hT", [128, 2, G, GW], F32R)
        ring = sb("ring", [128, 4, GW])
        misc = sb("misc", [128, 2, GW])
        tmp = sb("tmp", [128, 2, GW])
        hid_at = nc.sbuf_base
        hid = sb("hid", [128, 2, HC, 2, GW], F32R)
        cmat_at = nc.sbuf_base
        cmat = sb("cmat", [128, AC, 128])
        rows = sb("rows", [128, 6, 128])
        cols = sb("cols", [128, NCOL])
        pad = sb("pad", [128, 1])
        unused = sb("unused", [128, 1])
        rest = sb("rest", [128, 4])
        flag = sb("flag", [1, 1])
        flag_i = sb("flag_i", [1, 1], mybir.dt.int32)
        gs = sb("gs", [128, 128])
        pmat = sb("pmat", [128, 128])
        stats = sb("stats", [128, T, 6])
        mv = sb("mv", [128, T, 2])
        ve = sb("ve", [128, T])
        rs = sb("rs", [128, T])
        gt = sb("gt", [128, GT, E])
        top = sb("top", [128, GT, 8])
        above = sb("above", [128, GT, E])
        equal = sb("equal", [128, GT, E])
        tops = sb("tops", [128, GT, 8])
        gap = sb("gap", [128, GT])
        th = sb("th", [128, GT])
        wa = sb("wa", [128, 2, GT])
        w32 = sb("w32", [128, GT, 16, 2], F32R)
        nmax = sb("nmax", [128, H])
        m32 = sb("m32", [128, 2 * H], F32R)
        lsum = sb("lsum", [128, H])
        lrec = sb("lrec", [128, H])
        srec = sb("srec", [128, 3, AC])
        attnT = nc.alloc_sbuf_tensor_at("attnT", [128, AC, N], F32, offset=hid_at)
        wT = nc.alloc_sbuf_tensor_at("wT", [32, G, GW], F32R, offset=cmat_at)
        mTs = wT[:, 0, 0:128]
        h0T = cmat[:, :, :].rearrange("p (g k) n -> p g (k n)", g=G)
        stage = attnT[:, :, :].rearrange("p k n -> p (k n)")

        ps = ctx.enter_context(nc.psum_tensor("ps", [128, 8, 512], F32))
        scratch = nc.dram_tensor("rows_by_batch", (B, 6 * 128), F32, kind="Internal").ap()

        def f(ap):
            return ap.bitcast(F32)

        gs2 = range(G)
        ns = range(G * E)
        ts = range(T)
        cs = range(HC)
        x_loaded = Events(sem("x_loaded"), ["x"], 16)
        rows_loaded = Events(sem("rows_loaded"), ["rows"], 16)
        out_stored = [Events(sem(f"out_stored{g}"), ["out"], 16) for g in range(G)]
        pe_prep = Events(sem("pe_prep"), [("h0T", 0), ("h0T", 1), "gram", "P", ("jn", 0), ("jn", 1),
                                          ("h1T", 0), ("h1T", 1)])
        pe_gate = Events(sem("pe_gate"), [("gate", 0), ("wT", 0), ("gate", 1), ("wT", 1)])
        pe_hid = Events(sem("pe_hid"), range(G * E * HC))
        pe_wb = Events(sem("pe_wb"), ns)
        pe_out = Events(sem("pe_out"), ns)
        pe_res = Events(sem("pe_res"), [("M", 0), ("h2T", 0), ("M", 1), ("h2T", 1), ("A", 0), ("A", 1),
                                        ("h3T", 0), ("h3T", 1), ("F", 0), ("F", 1)])
        pe_logits = Events(sem("pe_logits"), ts)
        pe_maxT = Events(sem("pe_maxT"), ts)
        pe_shift = Events(sem("pe_shift"), ts)
        pe_z = Events(sem("pe_z"), ts)
        pe_attnT = Events(sem("pe_attnT"), [(t, h) for t in ts for h in range(2)])
        pe_fin = Events(sem("pe_fin"), ["s"] + [("C", j) for j in range(4)] + [("O", g) for g in gs2])

        def ffn_jobs(g, part):
            if part == "ab":
                return [(g, k, c) for c in cs for k in "ab"]
            return [(g, part)] if part == "y" else [(g, part, c) for c in cs]

        ffn_order = [(0, "ab"), (0, "h1"), (0, "h2"), (1, "ab"), (0, "y"), (1, "h1"), (1, "h2"), (1, "y")]
        pe_ffn = Events(sem("pe_ffn"), [j for o in ffn_order for j in ffn_jobs(*o)])
        act_cols = Events(sem("act_cols"), [0, 1])
        act_prep = Events(sem("act_prep"), [("h0T", 0), ("h0T", 1), "gram", ("h1T", 0), ("h1T", 1)])
        act_hi = Events(sem("act_hi"), [(g, c) for g in gs2 for c in cs])
        act_gate = Events(sem("act_gate"), [("th", 0), ("wT", 0), ("th", 1), ("wT", 1)])
        act_gelu = Events(sem("act_gelu"), range(G * E * HC))
        act_wb = Events(sem("act_wb"), ns)
        act_gb = Events(sem("act_gb"), gs2)
        act_maxT = Events(sem("act_maxT"), ts)
        act_exp = Events(sem("act_exp"), ts)
        act_attnT = Events(sem("act_attnT"), [(t, h) for t in ts for h in range(2)])
        act_z = Events(sem("act_z"), ["z"])
        act_y = Events(sem("act_y"), [("A", 0), ("A", 1), ("F", 0), ("F", 1)])
        act_h3T = Events(sem("act_h3T"), gs2)
        hidden_order = [(0, "ab"), (0, "h1"), (0, "h2"), (1, "ab"), (1, "h1"), (1, "h2")]
        act_ffn = Events(sem("act_ffn"), [(g, p, c) for g, p in hidden_order for c in cs])
        var, norm, root, every_ln = {}, {}, {}, []
        for layer, lns in ("L0", ["L0a", "L0i", "L0b"]), ("L1", [("L1a", 0), ("L1a", 1), ("L1b", 0), ("L1b", 1)]):
            events = [Events(sem(f"{n}_{layer}"), lns) for n in ("dve_var", "dve_norm", "pool_rs")]
            for k in lns:
                var[k], norm[k], root[k] = events
            every_ln += events
        dve_p = Events(sem("dve_p"), ["P"])
        dve_gap = Events(sem("dve_gap"), gs2)
        dve_w = Events(sem("dve_w"), gs2)
        dve_hT = Events(sem("dve_hT"), [(p, g) for p in ("moe", "attn", "ffn") for g in gs2])
        dve_split = Events(sem("dve_split"), list(range(G * E * HC)) + [(g, p, c) for g, p in hidden_order for c in cs])
        dve_gated = Events(sem("dve_gated"), ns)
        dve_res = Events(sem("dve_res"), [(p, g) for p in "MAF" for g in gs2])
        dve_max = Events(sem("dve_max"), ts)
        dve_attn = Events(sem("dve_attn"), ts)
        dve_srec = Events(sem("dve_srec"), ["s"])
        dve_c = Events(sem("dve_c"), range(4))
        dve_flag = Events(sem("dve_flag"), ["rest", "flag"])
        pe_flag = Events(sem("pe_flag"), ["rest"])
        dve_prod = Events(sem("dve_prod"), [(g, c) for g in gs2 for c in cs])
        prep_step = Events(sem("prep_step"), range(PREP_STEPS))
        main_step = Events(sem("main_step"), range(MAIN_STEPS))
        pool_mul = Events(sem("pool_mul"), [("L0", 0), ("L0", 1), ("L1", 0), ("L1", 1)])
        pool_h = Events(sem("pool_h"), [("L0", 0), ("L0", 1), ("L1", 0), ("L1", 1)])
        pool_x = Events(sem("pool_x"), ["beta", "gamma", "x"])
        pool_acc = Events(sem("pool_acc"), [n for n in ns if n % E])
        pool_asum = Events(sem("pool_asum"), range(1, T))
        every = [v for v in list(locals().values()) if isinstance(v, Events)] + out_stored + every_ln

        l_small, l_l1, l_emb, l_mod, l_mod1, l_ln, l_scr0, l_scr1, l_rows1 = (sem(n) for n in
            ("small_loaded", "ffn_loaded", "emb_loaded", "mod_loaded", "mod1_loaded", "gamma_beta_loaded",
             "rows0_written", "rows1_written", "rows1_loaded"))
        u_raw, u_rows0 = sem("raw_rows0"), sem("rows0_made")
        u_wwt = sem("wwt_made")
        l_moe = [sem(f"moe_loaded{q}") for q in range(4)]
        u_pool, u_act, u_hi, u_lo, u_pe, u_dve = (sem(n) for n in
            ("consts_made", "act_setup", "hi_parts", "lo_parts", "pe_setup", "dve_setup"))

        sets = {(0, "ab"): 0, (0, "h1"): 1, (0, "h2"): 0, (1, "ab"): 1, (1, "h1"): 0, (1, "h2"): 1}
        set_free = {(0, "ab"): (pe_fin, ("O", 1)), (0, "h1"): (pe_fin, ("O", 1)),
                    (0, "h2"): (pe_ffn, (0, "h1", 3)), (1, "ab"): (pe_ffn, (0, "h2", 3)),
                    (1, "h1"): (pe_ffn, (0, "y")), (1, "h2"): (pe_ffn, (1, "h1", 3))}
        L1_PARTS = [(fab, 0, 1024), (fh1, 1024, 2048), (fh2, 3072, 2048), (fy, 5120, 512)]
        EMB = 5632
        block = ctx.enter_context(nc.Block())

        def by_tile(ap):
            return ap.rearrange("(p t) d -> p t d", t=T)

        @block.sync
        def _(sp):
            for ev in every:
                sp.sem_inc(ev.sem, ev.credit())
            sp.dma_start(cols[:, :], ins["cT"]).then_inc(l_mod, 16)
            wm = ring[:, 0:3, :].rearrange("p a n -> p (a n)")
            sp.dma_start(wm[:, 0:768], ins["wmod"][:, 0:768]).then_inc(l_mod, 16)
            sp.dma_start(xa[:, :, :], by_tile(ins["x"][0])).then_inc(x_loaded.sem, 16)
            sp.dma_start(cmat[0:B, 0, :], ins["gamma"].partition_broadcast(B)).then_inc(l_ln, 16)
            sp.dma_start(cmat[0:B, 1, :], ins["beta"].partition_broadcast(B)).then_inc(l_ln, 16)
            sp.dma_start(wm[:, 768:1536], ins["wmod"][:, 768:1536]).then_inc(l_mod1, 16)
            for dst, src in [(vout[:, 0:128], ins["W_K"]), (vout[:, 128:256], ins["W_Q"]),
                             (vout[:, 256:256 + E], ins["gate_w"]), (nmax[:, 0:1], ins["b_out"]),
                             (fs[:, :], ins["scales"]), (b1[:, :], ins["b1"]), (b2[:, :], ins["b2"]),
                             (gateb[:, :], ins["gate_b"].partition_broadcast(128))]:
                sp.dma_start(dst, src).then_inc(l_small, 16)
            def expert_weights(q):
                w = slice(q * 2048, (q + 1) * 2048)
                src = ins["w1"][:, w] if q < 2 else ins["w2"][:, slice((q - 2) * 2048, (q - 1) * 2048)]
                sp.dma_start(stage[:, w], src).then_inc(l_moe[q], 16)

            expert_weights(0)
            by_row = scratch.rearrange("b (r d) -> b r d", r=6)
            first = scratch[0].rearrange("(r d) -> r d", r=6)
            sp.wait_ge(u_rows0, 1)
            sp.dma_start(by_row[:, 0:4, :], rows[0:B, 0:4, :]).then_inc(l_scr0, 16)
            sp.wait_ge(l_scr0, 16)
            sp.dma_start(rows[:, 0:4, :], first[0:4].partition_broadcast(128)).then_inc(rows_loaded.sem, 16)
            for q in range(1, 4):
                expert_weights(q)
            sp.dma_start(xb[64:128, :, :], ins["w_out"][:, 8:16, :]).then_inc(l_emb, 16)
            sp.wait_ge(u_dve, 1)
            sp.dma_start(by_row[:, 4:6, :], rows[0:B, 4:6, :]).then_inc(l_scr1, 16)
            sp.dma_start(misc[64:128, :, :].rearrange("p a (h d) -> p (a h) d", d=128), ins["w_out"][:, 0:8, :])\
                .then_inc(l_emb, 16)
            sp.wait_ge(l_scr1, 16)
            sp.dma_start(rows[:, 4:6, :], first[4:6].partition_broadcast(128)).then_inc(l_rows1, 16)
            sp.wait_ge(u_lo, 4)
            sp.dma_start(stage[:, EMB:EMB + 2048], ins["w_emb"]).then_inc(l_emb, 16)
            sp.dma_start(stage[0:64, EMB + 2048:EMB + 2048 + A], ins["w_anchor"]).then_inc(l_emb, 16)
            sp.dma_start(stage[:, 0:EMB], ins["ffn"]).then_inc(l_l1, 16)

            def store(b):
                for g in gs2:
                    sp.wait_ge(*dve_res.now(("F", g), b))
                    sp.dma_start(by_tile(out[b])[:, g * GT:(g + 1) * GT, :], xb[:, g * GT:(g + 1) * GT, :])\
                        .then_inc(out_stored[g].sem, 16)

            with sp.Fori(0, B - 1) as b:
                sp.wait_ge(*dve_res.now(("M", 1), b))
                sp.dma_start(xa[:, :, :], by_tile(ins["x"][b + 1])).then_inc(x_loaded.sem, 16)
                sp.wait_ge(*pool_h.now(("L1", 1), b))
                sp.dma_start(rows[:, :, :], scratch[b + 1].rearrange("(r d) -> r d", r=6).partition_broadcast(128))\
                    .then_inc(rows_loaded.sem, 16)
                store(b)
            store(B - 1)
            for g in gs2:
                sp.wait_ge(out_stored[g].sem, (B + 1) * 16)

        @block.gpsimd
        def _(pool):
            gp = nc.gpsimd
            oh = tmp[0:32, :, :].rearrange("p a n -> p (a n)")
            gp.memset(ident[:, :], 0.0).then_inc(u_pool, 1)
            gp.memset(oh, 0.0).then_inc(u_pool, 1)
            gp.memset(ones[:, :], 1.0).then_inc(u_pool, 1)
            gp.memset(neghalf[:, :], -0.5).then_inc(u_pool, 1)
            for e in range(E):
                gp.memset(order[:, e:e + 1], float(E - e)).then_inc(u_pool, 1)
            pool.wait_ge(u_pool, 12)
            gp.affine_select(out=ident[:, :], in_=ident[:, :], compare_op=ALU.not_equal, fill=1.0, base=0,
                             pattern=[[-1, 128]], channel_multiplier=1).then_inc(u_pool, 1)
            for base in (0, -H):
                v = oh.rearrange("p (h a) -> p h a", h=H)
                gp.affine_select(out=v, in_=v, compare_op=ALU.not_equal, fill=1.0, base=base,
                                 pattern=[[-1, H], [0, A]], channel_multiplier=1).then_inc(u_pool, 1)
                pool.wait_ge(u_pool, 14 if base == 0 else 15)

            def rstd(k, n, b):
                pool.wait_ge(*var[k].now(k, b))
                gp.tensor_tensor(rs[:, 0:n], ve[:, 0:n], neghalf[:, 0:n], ALU.pow).then_inc(*root[k].raise_(k))

            def modulate(layer, g, mul, add, b):
                h = hn[:, g * GT:(g + 1) * GT, :]
                gp.tensor_tensor(h, h, rows[:, mul, :].unsqueeze(1).broadcast_to([128, GT, 128]), ALU.mult)\
                    .then_inc(*pool_mul.raise_((layer, g)))
                pool.wait_ge(*pool_mul.now((layer, g), b))
                gp.tensor_tensor(h, h, rows[:, add, :].unsqueeze(1).broadcast_to([128, GT, 128]), ALU.add)\
                    .then_inc(*pool_h.raise_((layer, g)))

            def prepare_1(b):
                rstd("L0a", T, b)
                pool.wait_ge(*rows_loaded.now("rows", b))
                pool.wait_ge(*norm["L0a"].now("L0a", b))
                for g in gs2:
                    modulate("L0", g, R_C1A0, R_SA0, b)
                gp.tensor_tensor(xa[:, :, :], xa[:, :, :],
                                 rows[:, R_GBETA, :].unsqueeze(1).broadcast_to([128, T, 128]), ALU.add)\
                    .then_inc(*pool_x.raise_("beta"))

            def prepare_2(b):
                rstd("L0i", T, b)
                pool.wait_ge(*norm["L0i"].now("L0i", b))
                gp.tensor_tensor(hn[:, :, :], hn[:, :, :], rows[:, R_GG, :].unsqueeze(1).broadcast_to([128, T, 128]),
                                 ALU.mult).then_inc(*pool_x.raise_("gamma"))
                pool.wait_ge(*pool_x.now("gamma", b))
                gp.tensor_tensor(xa[:, :, :], xa[:, :, :], hn[:, :, :], ALU.add).then_inc(*pool_x.raise_("x"))
                rstd("L0b", T, b)

            def batch(b, more):
                acc = hn[:, GT:T, :].rearrange("p t d -> p (t d)")
                for n in ns:
                    if n % E:
                        pool.wait_ge(*dve_gated.now(n, b))
                        if n % E > 1:
                            pool.wait_ge(*pool_acc.now(n - 1, b))
                        gp.tensor_tensor(acc, acc, tmp[:, n % 2, :], ALU.add).then_inc(*pool_acc.raise_(n))
                    if n == 10:
                        rstd(("L1a", 0), GT, b)
                        pool.wait_ge(*norm[("L1a", 0)].now(("L1a", 0), b))
                        modulate("L1", 0, R_C1A1, R_SA1, b)
                rstd(("L1a", 1), GT, b)
                pool.wait_ge(*norm[("L1a", 1)].now(("L1a", 1), b))
                modulate("L1", 1, R_C1A1, R_SA1, b)
                asum = misc[:, :, :].rearrange("p a n -> p (a n)")
                for t in range(1, T):
                    pool.wait_ge(*dve_attn.now(t, b))
                    first = ring[:, 0:2, :].rearrange("p a n -> p (a n)") if t == 1 else asum
                    if t > 1:
                        pool.wait_ge(*pool_asum.now(t - 1, b))
                    gp.tensor_tensor(asum, first, ring[:, 2 * (t % 2):2 * (t % 2) + 2, :]
                                     .rearrange("p a n -> p (a n)"), ALU.add).then_inc(*pool_asum.raise_(t))
                if more:
                    prepare_1(b + 1)
                rstd(("L1b", 0), GT, b)
                rstd(("L1b", 1), GT, b)
                if more:
                    prepare_2(b + 1)

            prepare_1(0)
            prepare_2(0)
            w, at, n = L1_PARTS[2]
            pool.wait_ge(u_hi, 7)
            gp.tensor_tensor(w[:, 1, :], stage[:, at:at + n], f(w[:, 0, :]), ALU.subtract).then_inc(u_lo, 1)
            pool.wait_ge(l_rows1, 16)
            with pool.Fori(0, B - 1) as b:
                batch(b, True)
            batch(B - 1, False)

        @block.scalar
        def _(act):
            sc = nc.scalar

            def copy(dst, src, scale=1.0):
                return sc.activation(dst, src, ACT.Copy, scale=scale)

            act.wait_ge(l_mod, 32)
            sc.activation(lsum[:, 0:8].rearrange("p (l b) -> p l b", l=2), cols[:, :].rearrange("p (l b) -> p l b", l=2), ACT.Silu)\
                .then_inc(u_act, 1)
            def expert_hi(q):
                act.wait_ge(l_moe[q], 16)
                w, o = (w1, q) if q < 2 else (w2, q - 2)
                copy(w[:, 0, o * 2048:(o + 1) * 2048], stage[:, q * 2048:(q + 1) * 2048]).then_inc(u_hi, 1)

            expert_hi(0)
            expert_hi(1)

            def col(j):
                return cols[:, j:j + 1]

            def load_table(func):
                sc.activation(unused[:, :], ones[:, :], func)

            def from_psum(bank, dst, ev, job, func=ACT.Copy, **kw):
                sc.activation(dst, ps[:, bank, :], func, **kw).then_inc(*ev.raise_(job))

            def load_cols(layer, b):
                at, n = ((0, NC0), (NC0, NC1))[layer]
                copy(cols[:, at:at + n], modt[:, bass.ds(b * NCOL + at, n)]).then_inc(*act_cols.raise_(layer))
                act.wait_ge(*act_cols.now(layer, b))

            def prepare_1(b):
                act.wait_ge(*pe_fin.before(("O", 1), b))
                for g in gs2:
                    act.wait_ge(*pe_prep.now(("h0T", g), b))
                    from_psum(4 + g, h0T[:, g, :], act_prep, ("h0T", g))

            def prepare_1b(b):
                act.wait_ge(*pe_prep.now("gram", b))
                copy(gs[:, :], ps[:, 6, 0:128]).then_inc(*act_prep.raise_("gram"))

            def prepare_2(b):
                act.wait_ge(*act_gb.before(1, b))
                load_cols(0, b)
                act.wait_ge(*dve_hT.before(("ffn", 1), b))
                for g in gs2:
                    act.wait_ge(*pe_prep.now(("h1T", g), b))
                    from_psum(g, misc[:, g, :], act_prep, ("h1T", g), ACT.Identity, scale=col(C1B0), bias=col(SB0))

            def gates(step, g, b):
                if step == "th":
                    act.wait_ge(*dve_gap.now(g, b))
                    sc.activation(th[:, :], gap[:, :], ACT.Tanh, scale=0.5).then_inc(*act_gate.raise_(("th", g)))
                else:
                    act.wait_ge(*pe_gate.now(("wT", g), b))
                    copy(wT[:, g, :], ps[0:32, 1, :]).then_inc(*act_gate.raise_(("wT", g)))

            def attnT_out(t, b):
                if t == 0:
                    act.wait_ge(*pe_out.now(2 * E - 1, b))
                for h in range(2):
                    act.wait_ge(*pe_attnT.now((t, h), b))
                    copy(attnT[:, 4 * h:4 * h + 4, t * 128:(t + 1) * 128],
                         ps[:, h, :].rearrange("p (k n) -> p k n", k=4)).then_inc(*act_attnT.raise_((t, h)))

            def hidden(g, part, b):
                def rounded_product(c):
                    if c == 0:
                        act.wait_ge(*set_free[g, part][0].now(set_free[g, part][1], b))
                    act.wait_ge(*dve_prod.now((g, c), b))
                    copy(hid[:, sets[g, part], c, 0, :], ring[:, 2 * (c % 2) + 1, :]).then_inc(*act_hi.raise_((g, c)))

                for c in cs:
                    m = 2 * c if part == "ab" else {"h1": 8, "h2": 12}[part] + c
                    act.wait_ge(*pe_ffn.now((g, "a" if part == "ab" else part, c), b))
                    if part == "ab":
                        if c >= 2:
                            act.wait_ge(*dve_prod.now((g, c - 2), b))
                        else:
                            act.wait_ge(*(dve_split.now((0, "h2", 3), b) if g else pe_fin.now(("C", 3), b)))
                        sc.activation(ring[:, 2 * (c % 2), :], ps[:, 2 + m % 4, :], ACT.Silu,
                                      scale=fs[:, c:c + 1]).then_inc(*act_ffn.raise_((g, part, c)))
                        if c:
                            rounded_product(c - 1)
                        if c == HC - 1:
                            rounded_product(c)
                    else:
                        act.wait_ge(*dve_split.now((g, "ab", 2 + c // 2) if part == "h1" else (g, "h1", c), b))
                        if c == 0:
                            act.wait_ge(*set_free[g, part][0].now(set_free[g, part][1], b))
                        s = HC * (2 if part == "h1" else 3) + c
                        sc.activation(ring[:, c, :], ps[:, 2 + m % 4, :], ACT.Gelu, scale=fs[:, s:s + 1])
                        sc.activation(hid[:, sets[g, part], c, 0, :], ps[:, 2 + m % 4, :], ACT.Gelu,
                                      scale=fs[:, s:s + 1]).then_inc(*act_ffn.raise_((g, part, c)))

            def out_y(g, b):
                act.wait_ge(*pe_ffn.now((g, "y"), b))
                from_psum(7, tmp[:, g, :], act_y, ("F", g), ACT.Copy, scale=col(GBS3))

            def batch(b, more):
                load_table(ACT.Gelu)
                for n in ns:
                    g, e = divmod(n, E)
                    if n == 4:
                        gates("th", 1, b)
                    for c in cs:
                        m = n * HC + c
                        act.wait_ge(*pe_hid.now(m, b))
                        act.wait_ge(*(dve_split.now(m - 4, b) if m >= 4 else dve_split.before((1, "h2", c), b)))
                        bias = b1[:, e * HC + c:e * HC + c + 1]
                        if c in ACT_HI:
                            if n >= 2:
                                act.wait_ge(*pe_out.now(n - 2, b))
                            else:
                                act.wait_ge(*pe_ffn.before((1, "y"), b))
                            sc.activation(ring[:, m % 4, :], ps[:, 2 + m % 4, :], ACT.Gelu, bias=bias)
                            from_psum(2 + m % 4, hid[:, n % 2, c, 0, :], act_gelu, m, ACT.Gelu, bias=bias)
                        else:
                            from_psum(2 + m % 4, ring[:, m % 4, :], act_gelu, m, ACT.Gelu, bias=bias)
                    if n == 1:
                        gates("wT", 0, b)
                    if n == 6:
                        gates("wT", 1, b)
                    if n:
                        spread(n - 1, b)
                    if n == 9:
                        act.wait_ge(*pool_acc.now(E - 1, b))
                        acc = hn[:, GT:T, :]
                        copy(acc, acc, scale=col(GB0)).then_inc(*act_gb.raise_(0))
                spread(2 * E - 1, b)

                load_table(ACT.Exp)
                for t in range(T + 2):
                    if t < T:
                        act.wait_ge(*pe_maxT.now(t, b))
                        if t >= 1:
                            act.wait_ge(*pe_shift.now(t - 1, b))
                        copy(mTs, ps[0:32, 1, 0:128]).then_inc(*act_maxT.raise_(t))
                    if t == T + 1:
                        act.wait_ge(*pe_z.now(T - 1, b))
                        act.wait_ge(*pool_asum.now(T - 2, b))
                        act.wait_ge(*pe_attnT.now((T - 2, 1), b))
                        copy(ring[:, 0:2, :], ps[:, 6:8, :]).then_inc(*act_z.raise_("z"))
                    if t >= 2:
                        attnT_out(t - 2, b)
                    if t < T:
                        act.wait_ge(*pe_shift.now(t, b))
                        if t >= 2:
                            act.wait_ge(*pe_attnT.now((t - 2, 1), b))
                            act.wait_ge(*pool_asum.now(max(t - 2, 1), b))
                        else:
                            act.wait_ge(*dve_split.now(G * E * HC - 1, b))
                        e0 = 2 * (t % 2)
                        k0 = 2 + 2 * (t % 2)
                        sc.activation(ring[:, e0:e0 + 2, :], ps[:, k0:k0 + 2, :], ACT.Exp)\
                            .then_inc(*act_exp.raise_(t))
                    if t == 0:
                        act.wait_ge(*pool_acc.now(2 * E - 1, b))
                        copy(acc, acc, scale=col(GB0)).then_inc(*act_gb.raise_(1))
                        act.wait_ge(*act_y.before(("F", 1), b))
                        load_cols(1, b)
                act.wait_ge(*pool_acc.now(2 * E - 1, b))
                for g in gs2:
                    act.wait_ge(*pe_fin.now(("O", g), b))
                    from_psum(2 + g, tmp[:, g, :], act_y, ("A", g), ACT.Identity, scale=col(GA1), bias=col(GABO))
                    if g:
                        act.wait_ge(*pe_res.now(("h3T", 0), b))
                        act.wait_ge(*pe_fin.now("s", b))
                        from_psum(0, misc[:, 0, :], act_h3T, 0, ACT.Identity, scale=col(C1B1), bias=col(SB1))

                if more:
                    prepare_1(b + 1)
                    prepare_1b(b + 1)
                load_table(ACT.Silu)
                hidden(0, "ab", b)
                act.wait_ge(*pe_res.now(("h3T", 1), b))
                from_psum(0, misc[:, 1, :], act_h3T, 1, ACT.Identity, scale=col(C1B1), bias=col(SB1))
                load_table(ACT.Gelu)
                hidden(0, "h1", b)
                hidden(0, "h2", b)
                load_table(ACT.Silu)
                hidden(1, "ab", b)
                load_table(ACT.Gelu)
                out_y(0, b)
                hidden(1, "h1", b)
                if more:
                    prepare_2(b + 1)
                hidden(1, "h2", b)
                if more:
                    gates("th", 0, b + 1)
                out_y(1, b)

            def spread(n, b):
                act.wait_ge(*pe_wb.now(n, b))
                act.wait_ge(*(dve_gated.now(n - 2, b) if n >= 2 else dve_hT.now(("moe", n), b)))
                from_psum(0, misc[:, n % 2, :], act_wb, n)

            prepare_1(0)
            expert_hi(2)
            prepare_1b(0)
            expert_hi(3)
            act.wait_ge(u_pe, 4)
            act.wait_ge(u_dve, 2)
            copy(tmp[:, :, :], ps[:, 6:8, :], scale=DH ** -0.5).then_inc(u_act, 1)
            act.wait_ge(u_act, 2)
            copy(anch[:, 0, :], tmp[:, :, :].rearrange("p a n -> p (a n)")).then_inc(u_act, 1)
            act.wait_ge(l_l1, 16)
            for w, at, n in L1_PARTS:
                copy(w[:, 0, :], stage[:, at:at + n]).then_inc(u_hi, 1)
            act.wait_ge(u_pe, 5)
            copy(vout[:, :], ps[:, 2:6, :].rearrange("p a n -> p (a n)")).then_inc(u_act, 1)
            prepare_2(0)
            gates("th", 0, 0)
            act.wait_ge(u_lo, 9)
            with act.Fori(0, B - 1) as b:
                batch(b, True)
            batch(B - 1, False)

        @block.vector
        def _(dve):
            v = nc.vector
            flat = "p a n -> p (a n)"
            chain = [0]
            u_chain = sem("setup_chain")

            def link(ins_):
                chain[0] += 1
                ins_.then_inc(u_chain, 1)
                dve.wait_ge(u_chain, chain[0])

            def settle(own, ins_):
                ev, b = own
                at = ev.raised % len(ev.jobs)
                ins_.then_inc(*ev.raise_(at))
                dve.wait_ge(*ev.now(at, b))

            def settle_alone(own, ins_):
                settle(own, ins_)
                v.memset(pad[:, :], 0.0)

            def layer_norm_stats(own, k, srcs):
                n = len(srcs)
                for i, s in enumerate(srcs):
                    last = v.bn_stats(stats[:, i, :], s)
                settle_alone(own, last)
                for i in range(n):
                    last = v.bn_aggr(mv[:, i, :], stats[:, i, :])
                settle(own, last)
                v.tensor_scalar(ve[:, 0:n], mv[:, 0:n, 1], EPS, None, ALU.add).then_inc(*var[k].raise_(k))

            def layer_norm_apply(own, k, srcs, dst):
                dve.wait_ge(*root[k].now(k, own[1]))
                for i, s in enumerate(srcs):
                    last = v.tensor_scalar(dst[:, i, :], s, mv[:, i, 0:1], rs[:, i:i + 1],
                                           ALU.subtract, ALU.mult)
                last.then_inc(*norm[k].raise_(k))

            def layer_norm(own, k, srcs, dst):
                layer_norm_stats(own, k, srcs)
                layer_norm_apply(own, k, srcs, dst)

            def tiles(x, g):
                return [x[:, t, :] for t in range(g * GT, (g + 1) * GT)]

            def split(own, dst_hi, dst_lo, src, ev, job):
                settle(own, v.tensor_copy(dst_hi, src))
                v.tensor_tensor(dst_lo, src, f(dst_hi), ALU.subtract).then_inc(*ev.raise_(job))

            def prepare_1(b, part):
                own, x = (prep_step, b), tiles(xa, 0) + tiles(xa, 1)
                if part == "stats":
                    dve.wait_ge(*x_loaded.now("x", b))
                    layer_norm_stats(own, "L0a", x)
                else:
                    dve.wait_ge(*pe_z.before(T - 1, b))
                    layer_norm_apply(own, "L0a", x, hn)

            def prepare_2(b):
                dve.wait_ge(*pe_prep.now("P", b))
                v.scalar_tensor_tensor(pmat[:, :], ps[:, 7, 0:128], D ** -0.5, ident[:, :], ALU.mult, ALU.add)\
                    .then_inc(*dve_p.raise_("P"))

            def prepare_3(b, part):
                own = (prep_step, b)
                jn = [ps[:, g, t * 128:(t + 1) * 128] for g in gs2 for t in range(GT)]
                if part == "stats":
                    for g in gs2:
                        dve.wait_ge(*pe_prep.now(("jn", g), b))
                    layer_norm_stats(own, "L0i", jn)
                    return
                layer_norm_apply(own, "L0i", jn, hn)

            def prepare_4(b, part):
                own, x = (prep_step, b), tiles(xa, 0) + tiles(xa, 1)
                if part == "stats":
                    dve.wait_ge(*pool_x.now("x", b))
                    layer_norm_stats(own, "L0b", x)
                else:
                    layer_norm_apply(own, "L0b", x, hn)

            def prepare_5(b):
                own = (prep_step, b)
                dve.wait_ge(*pe_ffn.before((1, "b", 3), b))
                for g in gs2:
                    dve.wait_ge(*act_prep.now(("h1T", g), b))
                    split(own, hT[:, 0, g, :], hT[:, 1, g, :], misc[:, g, :], dve_hT, ("moe", g))

            def gates(g, b, step):
                own = (step, b)

                def over_e(ap):
                    return ap.unsqueeze(2).broadcast_to([128, GT, E])

                dve.wait_ge(*pe_gate.now(("gate", g), b))
                settle_alone(own, v.tensor_tensor(gt[:, :, :], ps[:, 1, 0:GT * E].rearrange("p (t e) -> p t e", t=GT),
                                                  gateb[:, :].unsqueeze(1).broadcast_to([128, GT, E]), ALU.add))
                for t in range(GT):
                    last = v.max(top[:, t, :], gt[:, t, :])
                settle(own, last)
                if g:
                    dve.wait_ge(*act_gate.now(("th", 0), b))
                v.tensor_tensor(gap[:, :], top[:, :, 0], top[:, :, 1], ALU.subtract)\
                    .then_inc(*dve_gap.raise_(g))
                v.tensor_tensor(above[:, :, :], gt[:, :, :], over_e(top[:, :, 1]), ALU.is_gt)
                settle(own, v.tensor_tensor(equal[:, :, :], gt[:, :, :], over_e(top[:, :, 1]), ALU.is_equal))
                settle_alone(own, v.tensor_tensor(equal[:, :, :], equal[:, :, :],
                                                  order[:, :].unsqueeze(1).broadcast_to([128, GT, E]), ALU.mult))
                for t in range(GT):
                    last = v.max(tops[:, t, :], equal[:, t, :])
                settle(own, last)
                v.tensor_tensor(wa[:, 0, :], top[:, :, 0], top[:, :, 1], ALU.is_gt)
                settle(own, v.tensor_tensor(wa[:, 1, :], tops[:, :, 0], tops[:, :, 1], ALU.subtract))
                settle(own, v.tensor_tensor(wa[:, 0, :], wa[:, 0, :], wa[:, 1, :], ALU.mult))
                settle(own, v.tensor_tensor(wa[:, 0, :], wa[:, 0, :], tops[:, :, 1], ALU.add))
                settle(own, v.tensor_tensor(equal[:, :, :], equal[:, :, :], over_e(wa[:, 0, :]), ALU.is_ge))
                dve.wait_ge(*act_gate.now(("th", g), b))
                v.tensor_scalar(wa[:, 0, :], th[:, :], 0.5, 0.5, ALU.mult, ALU.add)
                settle(own, v.tensor_scalar(wa[:, 1, :], th[:, :], -0.5, 0.5, ALU.mult, ALU.add))
                v.tensor_tensor(above[:, :, :], above[:, :, :], over_e(wa[:, 0, :]), ALU.mult)
                settle(own, v.tensor_tensor(equal[:, :, :], equal[:, :, :], over_e(wa[:, 1, :]), ALU.mult))
                settle(own, v.tensor_tensor(above[:, :, :], above[:, :, :], equal[:, :, :], ALU.add))
                if g:
                    dve.wait_ge(*pe_gate.now(("wT", 0), b))
                for r in range(2):
                    last = v.tensor_copy(w32[:, :, 0:8, r], above[:, :, :])
                settle(own, last)
                for r in range(2):
                    last = v.tensor_tensor(w32[:, :, 8:16, r], above[:, :, :], f(w32[:, :, 0:8, r]), ALU.subtract)
                last.then_inc(*dve_w.raise_(g))

            def split_hidden(job, slot, s, c, b, hi_made):
                if hi_made:
                    v.tensor_tensor(hid[:, s, c, 1, :], ring[:, slot, :], f(hid[:, s, c, 0, :]), ALU.subtract)\
                        .then_inc(*dve_split.raise_(job))
                else:
                    split((main_step, b), hid[:, s, c, 0, :], hid[:, s, c, 1, :], ring[:, slot, :], dve_split, job)

            def gated(n, b):
                dve.wait_ge(*pe_out.now(n, b))
                dve.wait_ge(*act_wb.now(n, b))
                if n % E == 0:
                    if n:
                        dve.wait_ge(*pe_res.now(("M", 0), b))
                    else:
                        dve.wait_ge(*pe_prep.now(("h1T", 1), b))
                    dst = hn[:, GT:T, :].rearrange("p t d -> p (t d)")
                else:
                    if (n - 2) % E and n >= 3:
                        dve.wait_ge(*pool_acc.now(n - 2, b))
                    if n < 3:
                        dve.wait_ge(*pe_res.before(("F", 1), b))
                    dst = tmp[:, n % 2, :]
                v.scalar_tensor_tensor(dst, ps[:, 6 + n % 2, :], b2[:, n % E:n % E + 1], misc[:, n % 2, :],
                                       ALU.add, ALU.mult).then_inc(*dve_gated.raise_(n))

            def residual(p, g, src, bank, b):
                dve.wait_ge(*pe_res.now((p, g), b))
                if p == "M":
                    dve.wait_ge(*out_stored[g].before("out", b))
                v.tensor_tensor(xb[:, g * GT:(g + 1) * GT, :], src[:, g * GT:(g + 1) * GT, :],
                                ps[:, bank, :].rearrange("p (t d) -> p t d", t=GT), ALU.add)\
                    .then_inc(*dve_res.raise_((p, g)))

            def residual_stats(p, g, k, src, b):
                residual(p, g, src, 1, b)
                dve.wait_ge(*dve_res.now((p, g), b))
                layer_norm_stats((main_step, b), (k, g), tiles(xb, g))

            def normalized(g, k, b):
                dst = hn[:, g * GT:(g + 1) * GT, :] if k == "L1a" else misc[:, g, :].rearrange("p (t d) -> p t d", t=GT)
                layer_norm_apply((main_step, b), (k, g), tiles(xb, g), dst)

            def hT_attn(g, b):
                dve.wait_ge(*pe_res.now(("h2T", g), b))
                dve.wait_ge(*pe_hid.now(g * 32 + 31, b))
                split((main_step, b), hT[:, 0, g, :], hT[:, 1, g, :], ps[:, 1, :], dve_hT, ("attn", g))

            def hT_ffn(g, b):
                dve.wait_ge(*act_h3T.now(g, b))
                split((main_step, b), hT[:, 0, g, :], hT[:, 1, g, :], misc[:, g, :], dve_hT, ("ffn", g))

            def neg_max(t, b):
                own = (main_step, b)
                dve.wait_ge(*pe_logits.now(t, b))
                if t:
                    dve.wait_ge(*dve_max.now(t - 1, b))
                k0 = 2 + 2 * (t % 2)
                settle(own, v.tensor_reduce(nmax[:, :], ps[:, k0:k0 + 2, :].rearrange("p k (h a) -> p (k h) a", a=A),
                                            X, ALU.max, negate=True))
                if t:
                    dve.wait_ge(*pe_maxT.now(t - 1, b))
                settle(own, v.tensor_copy(m32[:, 0:H], nmax[:, :]))
                v.tensor_tensor(m32[:, H:2 * H], nmax[:, :], f(m32[:, 0:H]), ALU.subtract)\
                    .then_inc(*dve_max.raise_(t))

            def normalize(t, b):
                own = (main_step, b)
                dve.wait_ge(*act_exp.now(t, b))
                e = ring[:, 2 * (t % 2):2 * (t % 2) + 2, :].rearrange("p k (h a) -> p (k h) a", a=A)
                settle(own, v.tensor_reduce(lsum[:, :], e, X, ALU.add))
                settle(own, v.reciprocal(lrec[:, :], lsum[:, :]))
                v.tensor_tensor(e, e, lrec[:, :].unsqueeze(2).broadcast_to([128, H, A]), ALU.mult)\
                    .then_inc(*dve_attn.raise_(t))

            def hidden(g, part, b, midway=None):
                ev, job = set_free[g, part]
                dve.wait_ge(*ev.now(job, b))

                def remainder(c):
                    dve.wait_ge(*act_hi.now((g, c), b))
                    split_hidden((g, part, c), 2 * (c % 2) + 1, sets[g, part], c, b, True)

                for c in cs:
                    dve.wait_ge(*act_ffn.now((g, part, c), b))
                    if part == "ab":
                        dve.wait_ge(*pe_ffn.now((g, "b", c), b))
                        if c >= 2:
                            dve.wait_ge(*dve_split.now((g, part, c - 2), b))
                        slot = 2 * (c % 2) + 1
                        v.scalar_tensor_tensor(ring[:, slot, :], ps[:, 2 + (2 * c + 1) % 4, :],
                                               fs[:, HC + c:HC + c + 1], ring[:, slot - 1, :], ALU.mult, ALU.mult)\
                            .then_inc(*dve_prod.raise_((g, c)))
                        if c:
                            remainder(c - 1)
                        if c == HC - 1:
                            remainder(c)
                    else:
                        split_hidden((g, part, c), c, sets[g, part], c, b, True)
                        if c == 1 and midway:
                            midway()

            def batch(b, more):
                for n in ns:
                    if n == 4:
                        gates(1, b, main_step)
                    for c in cs:
                        mm = n * HC + c
                        dve.wait_ge(*act_gelu.now(mm, b))
                        if c == 0:
                            dve.wait_ge(*(pe_out.now(n - 2, b) if n >= 2 else pe_ffn.before((1, "y"), b)))
                        split_hidden(mm, mm % 4, n % 2, c, b, c in ACT_HI)
                    if n:
                        gated(n - 1, b)
                    if n == 11:
                        residual_stats("M", 0, "L1a", xa, b)
                        normalized(0, "L1a", b)
                    if n == 14:
                        hT_attn(0, b)
                neg_max(0, b)
                gated(2 * E - 1, b)

                neg_max(1, b)
                normalize(0, b)
                residual_stats("M", 1, "L1a", xa, b)
                neg_max(2, b)
                normalized(1, "L1a", b)
                normalize(1, b)
                hT_attn(1, b)
                for t in range(3, T + 1):
                    if t < T:
                        neg_max(t, b)
                    normalize(t - 1, b)
                if more:
                    prepare_1(b + 1, "stats")
                own = (main_step, b)
                dve.wait_ge(*pe_fin.now("s", b))
                v.tensor_scalar(srec[:, 0, :], ps[:, 5, 0:AC], TINY, None, ALU.is_ge)
                v.tensor_scalar(srec[:, 1, :], ps[:, 5, 0:AC], TINY, None, ALU.max).then_inc(*dve_srec.raise_("s"))
                dve.wait_ge(*dve_srec.now("s", b))
                settle(own, v.reciprocal(srec[:, 2, :], srec[:, 1, :]))
                settle(own, v.tensor_tensor(srec[:, 2, :], srec[:, 2, :], srec[:, 0, :], ALU.mult))
                for j in range(4):
                    dve.wait_ge(*pe_fin.now(("C", j), b))
                    src = ps[:, 2 + j, :].rearrange("p (k n) -> p k n", k=2)
                    for half in range(2):
                        p = slice(64 * half, 64 * half + 64)
                        last = v.tensor_tensor(cmat[p, 2 * j:2 * j + 2, :], src[p, :, half * 128:half * 128 + 128],
                                               srec[p, 2, 2 * j:2 * j + 2].unsqueeze(2).broadcast_to([64, 2, 128]),
                                               ALU.mult)
                    last.then_inc(*dve_c.raise_(j))
                if more:
                    prepare_1(b + 1, "apply")
                for i, (w, _, n) in enumerate(L1_PARTS):
                    last = v.tensor_reduce(rest[:, i:i + 1], f(w[:, 1, :]), X, ALU.max, apply_absolute_value=True)
                settle(own, last)
                v.tensor_reduce(rest[:, 0:1], rest[:, :], X, ALU.max).then_inc(*dve_flag.raise_("rest"))
                dve.wait_ge(*pe_flag.now("rest", b))
                settle(own, v.tensor_reduce(flag[:, :], ps[0:1, 0, 0:128], X, ALU.max))
                settle(own, v.tensor_scalar(flag[:, :], flag[:, :], 0.0, None, ALU.is_gt))
                v.tensor_copy(flag_i[:, :], flag[:, :]).then_inc(*dve_flag.raise_("flag"))
                residual_stats("A", 0, "L1b", xb, b)
                normalized(0, "L1b", b)
                residual_stats("A", 1, "L1b", xb, b)
                hT_ffn(0, b)
                normalized(1, "L1b", b)

                hidden(0, "ab", b)
                hT_ffn(1, b)
                if more:
                    prepare_2(b + 1)
                hidden(0, "h1", b)
                if more:
                    prepare_3(b + 1, "stats")
                hidden(0, "h2", b, (lambda: prepare_3(b + 1, "apply")) if more else None)
                hidden(1, "ab", b)
                if more:
                    prepare_4(b + 1, "stats")
                    prepare_4(b + 1, "apply")
                hidden(1, "h1", b)
                residual("F", 0, xb, 7, b)
                if more:
                    prepare_5(b + 1)
                hidden(1, "h2", b)
                if more:
                    gates(0, b + 1, prep_step)
                residual("F", 1, xb, 7, b)
                for ev in (prep_step, main_step):
                    assert ev.raised % len(ev.jobs) == 0, (ev.raised, len(ev.jobs))

            prepare_1(0, "stats")
            raw = misc[0:B, :, :].rearrange(flat)
            raw1 = xb[0:B, :, :].rearrange("p t d -> p (t d)")
            m = [raw[:, 0:768].rearrange("p (j d) -> p j d", j=6), raw1[:, 0:768].rearrange("p (j d) -> p j d", j=6)]

            def modulation(l):
                for j in range(2):
                    last = v.tensor_copy(m[l][:, 3 * j:3 * j + 3, :].rearrange("p j d -> p (j d)"),
                                         ps[0:B, 2 + 2 * l + j, 0:384])
                link(last)
                mj = m[l].rearrange("p (a j) d -> p j a d", a=2)
                v.tensor_scalar(mj[:, 1], mj[:, 1], 1.0, None, ALU.add)
                v.tensor_scalar(cmat[0:B, 2:4, :], mj[:, 2], 0.0, 2.0, ALU.is_ge, ALU.mult)
                link(v.scalar_tensor_tensor(cmat[0:B, 4:6, :], mj[:, 2], -1.0, mj[:, 2], ALU.mult, ALU.max))
                link(v.tensor_scalar(cmat[0:B, 4:6, :], cmat[0:B, 4:6, :], 0.25, None, ALU.max))
                link(v.scalar_tensor_tensor(mj[:, 2], cmat[0:B, 2:4, :], -1.0, cmat[0:B, 4:6, :], ALU.add, ALU.mult))

            dve.wait_ge(u_raw, 1)
            modulation(0)
            v.tensor_copy(rows[0:B, R_C1A0, :], m[0][:, 1, :])
            v.tensor_copy(rows[0:B, R_SA0, :], m[0][:, 0, :])
            dve.wait_ge(l_ln, 32)
            v.tensor_tensor(rows[0:B, R_GG, :], m[0][:, 2, :], cmat[0:B, 0, :], ALU.mult)
            v.tensor_tensor(rows[0:B, R_GBETA, :], m[0][:, 2, :], cmat[0:B, 1, :], ALU.mult).then_inc(u_rows0, 1)
            prepare_1(0, "apply")
            dve.wait_ge(u_pe, 1)
            modulation(1)
            v.tensor_copy(rows[0:B, R_C1A1, :], m[1][:, 1, :])
            v.tensor_copy(rows[0:B, R_SA1, :], m[1][:, 0, :]).then_inc(u_dve, 1)
            dve.wait_ge(l_small, 8 * 16)
            dve.wait_ge(u_pool, 15)
            v.tensor_copy(onehot[:, :], tmp[0:32, :, :].rearrange(flat))
            link(v.tensor_copy(gatew[:, 0, :], vout[:, 256:256 + E]))
            v.tensor_tensor(gatew[:, 1, :], vout[:, 256:256 + E], f(gatew[:, 0, :]), ALU.subtract)
            dve.wait_ge(u_pe, 2)
            v.tensor_copy(wwt[:, :], ps[:, 3, 0:128]).then_inc(u_wwt, 1)
            mt = modt[:, :].rearrange("p (b j) -> p b j", b=B)
            pt = ps[:, 2, 0:7 * B].rearrange("p (j b) -> p b j", b=B)
            dve.wait_ge(u_pe, 3)
            v.tensor_copy(mt[:, :, C1B0:GA1 + 1], pt[:, :, 0:4])
            v.tensor_scalar(mt[:, :, GABO], pt[:, :, 3], nmax[:, 0:1], None, ALU.mult)
            v.tensor_copy(mt[:, :, C1B1:SB1 + 1], pt[:, :, 4:6])
            v.tensor_scalar(mt[:, :, GBS3], pt[:, :, 6], fs[:, 4 * HC:4 * HC + 1], None, ALU.mult).then_inc(u_dve, 1)
            def expert_lo(q):
                dve.wait_ge(u_hi, q + 1)
                w, o = (w1, q) if q < 2 else (w2, q - 2)
                v.tensor_tensor(w[:, 1, o * 2048:(o + 1) * 2048], stage[:, q * 2048:(q + 1) * 2048],
                                f(w[:, 0, o * 2048:(o + 1) * 2048]), ALU.subtract).then_inc(u_lo, 1)

            def ffn_lo(i):
                w, at, n = L1_PARTS[i]
                dve.wait_ge(u_hi, 5 + i)
                v.tensor_tensor(w[:, 1, :], stage[:, at:at + n], f(w[:, 0, :]), ALU.subtract).then_inc(u_lo, 1)

            for q in range(3):
                expert_lo(q)
            prepare_2(0)
            expert_lo(3)
            prepare_3(0, "stats")
            prepare_3(0, "apply")
            prepare_4(0, "stats")
            dve.wait_ge(u_act, 3)
            v.tensor_tensor(anch[:, 1, :], tmp[:, :, :].rearrange(flat), f(anch[:, 0, :]), ALU.subtract)\
                .then_inc(u_lo, 1)
            prepare_4(0, "apply")
            for i in (0, 1, 3):
                ffn_lo(i)
            prepare_5(0)
            gates(0, 0, prep_step)
            dve.wait_ge(u_lo, 9)
            with dve.Fori(0, B - 1) as b:
                batch(b, True)
            batch(B - 1, False)

        @block.tensor
        def _(pe):
            te = nc.tensor

            def transposes(bank, srcs, ev, job, rows_=128):
                for i, s in enumerate(srcs):
                    last_ = te.transpose(ps[0:rows_, bank, i * 128:(i + 1) * 128], s, ident[:, :])
                last_.then_inc(*ev.raise_(job))

            def three(out_, w, x, first, last_, all_=True):
                te.matmul(out_, w(0), x(0), start=first, stop=False)
                if not all_:
                    return te.matmul(out_, w(0), x(1), start=False, stop=last_)
                te.matmul(out_, w(0), x(1), start=False, stop=False)
                return te.matmul(out_, w(1), x(0), start=False, stop=last_)

            def tiles(x, g):
                return [x[:, t, :] for t in range(g * GT, (g + 1) * GT)]

            def quarters(x):
                return [x[:, t * 128:(t + 1) * 128] for t in range(GT)]

            def prepare_1(b):
                for g in gs2:
                    pe.wait_ge(*pool_h.now(("L0", g), b))
                    pe.wait_ge(*dve_c.before(3, b))
                    transposes(4 + g, tiles(hn, g), pe_prep, ("h0T", g))

            def prepare_1b(b):
                pe.wait_ge(*act_z.before("z", b))
                for t in ts:
                    last = te.matmul(ps[:, 6, 0:128], hn[:, t, :], hn[:, t, :], start=t == 0, stop=t == T - 1)
                last.then_inc(*pe_prep.raise_("gram"))

            def prepare_2(b):
                pe.wait_ge(*act_prep.now("gram", b))
                te.matmul(ps[:, 7, 0:128], wwt[:, :], gs[:, :], start=True, stop=True).then_inc(*pe_prep.raise_("P"))

            def prepare_3(b):
                pe.wait_ge(*dve_p.now("P", b))
                for g in gs2:
                    pe.wait_ge(*act_prep.now(("h0T", g), b))
                    pe.wait_ge(*(dve_res.before(("A", 1), b) if g else act_h3T.before(1, b)))
                    for t in range(GT):
                        last = te.matmul(ps[:, g, t * 128:(t + 1) * 128], h0T[:, g, t * 128:(t + 1) * 128],
                                         pmat[:, :], start=True, stop=True)
                    last.then_inc(*pe_prep.raise_(("jn", g)))

            def prepare_4(b):
                pe.wait_ge(*norm["L0b"].now("L0b", b))
                for g in gs2:
                    transposes(g, tiles(hn, g), pe_prep, ("h1T", g))

            def gates(g, b):
                pe.wait_ge(*dve_hT.now(("moe", 1), b))
                if g:
                    pe.wait_ge(*act_gate.now(("wT", 0), b))
                for t in range(GT):
                    last = three(ps[:, 1, t * E:(t + 1) * E], lambda i: hT[:, i, g, t * 128:(t + 1) * 128],
                                 lambda i: gatew[:, i, :], True, True)
                last.then_inc(*pe_gate.raise_(("gate", g)))

            def gates_transposed(g, b):
                pe.wait_ge(*dve_w.now(g, b))
                transposes(1, [f(w32[:, t, :, :]).rearrange("p a r -> p (a r)") for t in range(GT)],
                           pe_gate, ("wT", g), 32)

            def first_product(n, b):
                g, e = divmod(n, E)
                for c in cs:
                    mm = n * HC + c
                    pe.wait_ge(*(act_gelu.now(mm - 4, b) if mm >= 4 else act_ffn.before((1, "h2", c), b)))
                    at = (e * HC + c) * 128
                    three(ps[:, 2 + mm % 4, :], lambda i: w1[:, i, at:at + 128], lambda i: hT[:, i, g, :],
                          True, True).then_inc(*pe_hid.raise_(mm))

            def spread_gates(n, b):
                g, e = divmod(n, E)
                pe.wait_ge(*(act_wb.now(n - 1, b) if n else act_prep.now(("h1T", 0), b)))
                pe.wait_ge(*act_gate.now(("wT", g), b))
                te.matmul(ps[:, 0, :], onehot[:, e * 128:(e + 1) * 128], wT[:, g, :], start=True, stop=True)\
                    .then_inc(*pe_wb.raise_(n))

            def second_product(n, b):
                e = n % E
                if n >= 2:
                    pe.wait_ge(*dve_gated.now(n - 2, b))
                else:
                    pe.wait_ge(*(dve_res.before(("F", 1), b) if n else act_prep.now("gram", b)))
                for c in cs:
                    pe.wait_ge(*dve_split.now(n * HC + c, b))
                    at = (e * HC + c) * 128
                    last_ = three(ps[:, 6 + n % 2, :], lambda i: w2[:, i, at:at + 128],
                                  lambda i: hid[:, n % 2, c, i, :], c == 0, c == HC - 1)
                last_.then_inc(*pe_out.raise_(n))

            def logits(t, b):
                pe.wait_ge(*dve_hT.now(("attn", t // GT), b))
                pe.wait_ge(*(act_exp.now(t - 2, b) if t >= 2 else act_gelu.now(G * E * HC - 1, b)))
                tok = slice((t % GT) * 128, (t % GT + 1) * 128)
                for h in range(2):
                    last_ = three(ps[:, 2 + 2 * (t % 2) + h, :], lambda i: hT[:, i, t // GT, tok],
                                  lambda i: anch[:, i, h * 512:(h + 1) * 512], True, True)
                last_.then_inc(*pe_logits.raise_(t))

            def max_transposed(t, b):
                pe.wait_ge(*dve_max.now(t, b))
                if t == 0:
                    pe.wait_ge(*dve_hT.now(("attn", 0), b))
                if t == 2:
                    pe.wait_ge(*dve_res.now(("M", 1), b))
                if t == 3:
                    pe.wait_ge(*dve_hT.now(("attn", 1), b))
                if t >= 3:
                    pe.wait_ge(*act_attnT.now((t - 3, 1), b))
                transposes(1, [f(m32[:, :])], pe_maxT, t, 32)

            def shift(t, b):
                pe.wait_ge(*act_maxT.now(t, b))
                for h in range(2):
                    last_ = te.matmul(ps[:, 2 + 2 * (t % 2) + h, :], mTs, onehot[:, h * 512:(h + 1) * 512],
                                      start=False, stop=True, skip_group_check=True)
                last_.then_inc(*pe_shift.raise_(t))

            def gather(t, b):
                pe.wait_ge(*dve_attn.now(t, b))
                for h in range(2):
                    last_ = te.matmul(ps[:, 6 + h, :], hn[:, t, :], ring[:, 2 * (t % 2) + h, :],
                                      start=t == 0, stop=t == T - 1)
                last_.then_inc(*pe_z.raise_(t))

            def attn_transposed(t, b):
                for h in range(2):
                    if t:
                        pe.wait_ge(*act_attnT.now((t - 1, h), b))
                    elif h == 0:
                        pe.wait_ge(*act_wb.now(2 * E - 1, b))
                    if h == 1 and t + 2 < T:
                        pe.wait_ge(*act_maxT.now(t + 2, b))
                    transposes(h, quarters(ring[:, 2 * (t % 2) + h, :]), pe_attnT, (t, h))

            def outputs(g, ks, b):
                for k in ks:
                    if g == 0 and k % 2 == 0:
                        pe.wait_ge(*dve_c.now(k // 2, b))
                    last_ = te.matmul(ps[:, 2 + g, :], cmat[:, k, :], attnT[:, k, g * GW:(g + 1) * GW],
                                      start=k == 0, stop=k == AC - 1)
                if k == AC - 1:
                    last_.then_inc(*pe_fin.raise_(("O", g)))

            def residual_transposed(p, g, bank, b):
                pe.wait_ge(*act_y.now((p, g), b))
                if p == "F":
                    if g:
                        pe.wait_ge(*dve_res.now(("F", 0), b))
                else:
                    pe.wait_ge(*(dve_res.now(("A", 0), b) if g else dve_srec.now("s", b)))
                transposes(bank, quarters(tmp[:, g, :]), pe_res, (p, g))

            def h3_transposed(g, b):
                pe.wait_ge(*norm[("L1b", g)].now(("L1b", g), b))
                pe.wait_ge(*(act_h3T.now(0, b) if g else dve_flag.now("flag", b)))
                transposes(0, quarters(misc[:, g, :]), pe_res, ("h3T", g))

            def bank_read(g, m_, b):
                if m_ < 4:
                    return act_ffn.now((0, "h2", m_), b) if g else act_y.now(("A", 1), b)
                m_ -= 4
                if m_ >= 8:
                    return act_ffn.now((g, "h1", m_ - 8), b)
                return dve_prod.now((g, m_ // 2), b) if m_ % 2 else act_ffn.now((g, "ab", m_ // 2), b)

            def first_layer(g, b, all_):
                pe.wait_ge(*dve_hT.now(("ffn", g), b))
                for c in cs:
                    for k in range(2):
                        m_ = 2 * c + k
                        pe.wait_ge(*bank_read(g, m_, b))
                        at = (k * HC + c) * 128
                        three(ps[:, 2 + m_ % 4, :], lambda i: fab[:, i, at:at + 128], lambda i: hT[:, i, g, :],
                              True, True, all_).then_inc(*pe_ffn.raise_((g, "ab"[k], c)))

            def hidden_layer(g, part, w, src, src_set, base, b, all_):
                for pair in range(2):
                    for kc in cs:
                        pe.wait_ge(*dve_split.now((g, src, kc), b))
                        for o in (2 * pair, 2 * pair + 1):
                            if kc == 0:
                                pe.wait_ge(*bank_read(g, base + o, b))
                            at = kc * 512 + o * 128
                            last_ = three(ps[:, 2 + (base + o) % 4, :], lambda i: w[:, i, at:at + 128],
                                          lambda i: hid[:, src_set, kc, i, :], kc == 0, kc == HC - 1, all_)
                            if kc == HC - 1:
                                last_.then_inc(*pe_ffn.raise_((g, part, o)))

            def last_layer(g, src_set, b, all_):
                if g:
                    pe.wait_ge(*dve_res.now(("F", 0), b))
                for kc in cs:
                    pe.wait_ge(*dve_split.now((g, "h2", kc), b))
                    last_ = three(ps[:, 7, :], lambda i: fy[:, i, kc * 128:(kc + 1) * 128],
                                  lambda i: hid[:, src_set, kc, i, :], kc == 0, kc == HC - 1, all_)
                last_.then_inc(*pe_ffn.raise_((g, "y")))

            def ffn(b, more, all_):
                if more:
                    pe.wait_ge(*act_prep.now(("h0T", 1), b + 1))
                first_layer(0, b, all_)
                h3_transposed(1, b)
                if more:
                    prepare_2(b + 1)
                hidden_layer(0, "h1", fh1, "ab", 0, 8, b, all_)
                if more:
                    prepare_3(b + 1)
                hidden_layer(0, "h2", fh2, "h1", 1, 12, b, all_)
                first_layer(1, b, all_)
                last_layer(0, 0, b, all_)
                hidden_layer(1, "h1", fh1, "ab", 1, 8, b, all_)
                residual_transposed("F", 0, 7, b)
                if more:
                    prepare_4(b + 1)
                hidden_layer(1, "h2", fh2, "h1", 0, 12, b, all_)
                if more:
                    gates(0, b + 1)
                last_layer(1, 1, b, all_)
                residual_transposed("F", 1, 7, b)

            def batch(b, more):
                acc = hn[:, GT:T, :].rearrange("p t d -> p (t d)")
                for n in ns:
                    if n == 3:
                        gates(1, b)
                    first_product(n, b)
                    if n == 0:
                        gates_transposed(0, b)
                    if n == 5:
                        gates_transposed(1, b)
                    if n > 1:
                        spread_gates(n - 1, b)
                    if n:
                        second_product(n - 1, b)
                    if n == 1:
                        spread_gates(0, b)
                    if n == 10:
                        pe.wait_ge(*act_gb.now(0, b))
                        pe.wait_ge(*act_gate.now(("wT", 1), b))
                        transposes(1, quarters(acc), pe_res, ("M", 0))
                    if n == 13:
                        pe.wait_ge(*pool_h.now(("L1", 0), b))
                        transposes(1, tiles(hn, 0), pe_res, ("h2T", 0))
                logits(0, b)
                logits(1, b)
                spread_gates(2 * E - 1, b)
                second_product(2 * E - 1, b)
                for t in range(T + 2):
                    if t == 2:
                        pe.wait_ge(*dve_gated.now(2 * E - 1, b))
                    if t >= 2:
                        gather(t - 2, b)
                    if t < T:
                        max_transposed(t, b)
                    if t >= 2:
                        attn_transposed(t - 2, b)
                    if 2 <= t + 1 < T:
                        logits(t + 1, b)
                    if t < T:
                        shift(t, b)
                    if t == 1:
                        pe.wait_ge(*act_gb.now(1, b))
                        transposes(1, quarters(acc), pe_res, ("M", 1))
                    if t == 2:
                        pe.wait_ge(*pool_h.now(("L1", 1), b))
                        pe.wait_ge(*act_attnT.now((0, 1), b))
                        transposes(1, tiles(hn, 1), pe_res, ("h2T", 1))
                pe.wait_ge(*pool_asum.now(T - 1, b))
                asum = misc[:, :, :].rearrange("p a n -> p (a n)")
                for k in range(AC):
                    last = te.matmul(ps[:, 5, k:k + 1], asum[:, k * 128:(k + 1) * 128], ones[:, :], start=True, stop=True)
                last.then_inc(*pe_fin.raise_("s"))
                pe.wait_ge(*act_z.now("z", b))
                zT = ring[:, 0:2, :].rearrange("p a n -> p (a n)")
                for j in range(4):
                    if j == 3:
                        pe.wait_ge(*dve_srec.now("s", b))
                    for k in range(2):
                        q = 2 * j + k
                        last = te.matmul(ps[:, 2 + j, k * 256:(k + 1) * 256], zT[:, q * 128:(q + 1) * 128],
                                         vout[:, q * 256:(q + 1) * 256], start=True, stop=True)
                    last.then_inc(*pe_fin.raise_(("C", j)))
                pe.wait_ge(*act_attnT.now((T - 1, 1), b))
                outputs(0, range(AC), b)
                outputs(1, range(AC // 2), b)
                pe.wait_ge(*dve_flag.now("rest", b))
                te.transpose(ps[0:1, 0, 0:128], rest[:, 0:1], ident[:, :]).then_inc(*pe_flag.raise_("rest"))
                residual_transposed("A", 0, 1, b)
                outputs(1, range(AC // 2, AC), b)
                if more:
                    prepare_1(b + 1)
                residual_transposed("A", 1, 1, b)
                h3_transposed(0, b)
                if more:
                    prepare_1b(b + 1)
                pe.wait_ge(*dve_flag.now("flag", b))
                pe.nop(nofuse=True)
                pe.reg_load(inexact, flag_i[0:1, 0:1])
                before = {ev: ev.raised for ev in every}
                with pe.If_eq(inexact, 0):
                    ffn(b, more, False)
                for ev, n in before.items():
                    ev.raised = n
                with pe.Else():
                    ffn(b, more, True)

            pe.wait_ge(u_act, 1)
            wm = ring[:, 0:3, :].rearrange("p a n -> p (a n)")
            for l in range(2):
                if l:
                    pe.wait_ge(l_mod1, 16)
                for j in range(2):
                    last = te.matmul(ps[0:B, 2 + 2 * l + j, 0:384], lsum[:, 4 * l:4 * l + 4],
                                     wm[:, 768 * l + 384 * j:768 * l + 384 * (j + 1)], start=True, stop=True)
                last.then_inc(u_pe if l else u_raw, 1)
            pe.wait_ge(u_dve, 1)
            pe.wait_ge(l_small, 8 * 16)
            te.matmul(ps[:, 3, 0:128], vout[:, 0:128], vout[:, 128:256], start=True, stop=True).then_inc(u_pe, 1)
            pe.wait_ge(u_pool, 13)
            m0 = misc[0:B, :, :].rearrange("p a n -> p (a n)")
            m1 = xb[0:B, :, :].rearrange("p t d -> p (t d)")
            for j, (src, at) in enumerate([(m0, 4), (m0, 3), (m0, 5), (m1, 2), (m1, 4), (m1, 3), (m1, 5)]):
                last = te.transpose(ps[:, 2, j * B:(j + 1) * B], src[:, at * 128:(at + 1) * 128], ident[0:B, 0:B])
            last.then_inc(u_pe, 1)
            prepare_1(0)
            prepare_1b(0)
            pe.wait_ge(u_wwt, 1)
            prepare_2(0)
            prepare_3(0)
            pe.wait_ge(l_emb, 4 * 16)
            pe.wait_ge(u_dve, 2)
            for g in gs2:
                pe.wait_ge(*act_prep.now(("h0T", g), 0))
            pe.wait_ge(u_lo, 4)
            w_a = stage[0:64, EMB + 2048:EMB + 2048 + A]
            for h in range(H):
                last = te.matmul(ps[:, 6 + h // 8, (h % 8) * A:(h % 8 + 1) * A],
                                 stage[0:64, EMB + h * 128:EMB + (h + 1) * 128], w_a, start=True, stop=True)
            last.then_inc(u_pe, 1)
            for h in range(H):
                w_o = misc[64:128, h // 4, (h % 4) * 128:(h % 4 + 1) * 128] if h < 8 else xb[64:128, h % 8, :]
                last = te.matmul(ps[:, 2 + h // 4, (h % 4) * 128:(h % 4 + 1) * 128],
                                 stage[64:128, EMB + h * 128:EMB + (h + 1) * 128], w_o, start=True, stop=True)
            last.then_inc(u_pe, 1)
            prepare_4(0)
            gates(0, 0)
            pe.wait_ge(u_act, 4)
            pe.wait_ge(u_lo, 9)
            inexact = pe.alloc_register("inexact")

            with pe.Fori(0, B - 1) as b:
                batch(b, True)
            batch(B - 1, False)


def kernel(**inputs):
    import numpy as np
    import concourse.bacc as bacc
    from concourse.bass_utils import run_bass_kernel_spmd

    i = {k: np.asarray(v) for k, v in inputs.items()}

    def c(a):
        return np.ascontiguousarray(a)

    def out_chunks(w, k):
        o, n = w.shape
        return w.T.reshape(k, 128, o).transpose(1, 0, 2).reshape(128, k * o)

    emb = i["L1_attn_W_emb"]
    heads = emb.reshape(2, H, DH, D).transpose(0, 2, 1, 3).reshape(2 * DH, H * D)
    scales = np.concatenate([i[f"L1_ffn_{n}_s"].reshape(-1, 128).T for n in ("w1", "w2", "h1", "h2", "w3")], axis=1)
    arrays = {
        "x": c(i["L0_attn_J"]),
        "W_Q": c(i["L0_attn_W_Q"]), "W_K": c(i["L0_attn_W_K"]),
        "gamma": c(i["L0_attn_gamma"]), "beta": c(i["L0_attn_beta"]),
        "gate_w": c(i["L0_ffn_gate_w"].T), "gate_b": c(i["L0_ffn_gate_b"]),
        "w1": c(i["L0_ffn_w1"].transpose(1, 0, 2).reshape(128, -1)),
        "b1": c(i["L0_ffn_b1"].reshape(E * HC, 128).T),
        "w2": c(i["L0_ffn_w2"].reshape(E * HC, 128, D).transpose(1, 0, 2).reshape(128, -1)),
        "b2": c(i["L0_ffn_b2"].T),
        "cT": c(np.concatenate([i["L0_c"].T, i["L1_c"].T], axis=1)),
        "wmod": c(np.concatenate([i["L0_wmod"], i["L1_wmod"]], axis=1)),
        "w_emb": c(heads),
        "w_anchor": c(i["L1_attn_W_anchor"].T),
        "w_out": c(i["L1_attn_W_out"].reshape(D, H, DH).transpose(2, 1, 0)),
        "b_out": c(i["L1_attn_b_out"].reshape(D, 1)),
        "ffn": c(np.concatenate([i["L1_ffn_w1_w"].T, i["L1_ffn_w2_w"].T, out_chunks(i["L1_ffn_h1_w"], 4),
                                 out_chunks(i["L1_ffn_h2_w"], 4), out_chunks(i["L1_ffn_w3_w"], 4)], axis=1)),
        "scales": c(scales),
    }
    nc = bacc.Bacc("TRN2", target_bir_lowering=False, num_devices=1)
    aps = {k: nc.dram_tensor(f"in_{k}", a.shape, mybir.dt.from_np(a.dtype), kind="ExternalInput").ap()
           for k, a in arrays.items()}
    out = nc.dram_tensor("out_x", (B, N, D), F32, kind="ExternalOutput").ap()
    build(nc, aps, out)
    r = run_bass_kernel_spmd(nc, [{f"in_{k}": a for k, a in arrays.items()}], core_ids=[0])
    return r.results[0]["out_x"]
```

```python
from contextlib import ExitStack

import concourse.bass as bass
from concourse import mybir

ALU = mybir.AluOpType
ACT = mybir.ActivationFunctionType
F32 = mybir.dt.float32
F32R = mybir.dt.float32r
X = mybir.AxisListType.X

B, N, D = 4, 1024, 128
T = N // 128
G, GT = 2, 4
GW = GT * 128
E, HC = 8, 4
H, DH, A = 16, 64, 64
AC = H * A // 128
EPS = 1e-5
ACT_HI = (0, 2)
NC0, NC1 = 3, 5
NCOL = NC0 + NC1
C1B0, SB0, GB0, GA1, GABO, C1B1, SB1, GBS3 = range(NCOL)
R_C1A0, R_SA0, R_GG, R_GBETA, R_C1A1, R_SA1 = range(6)
TINY = 2.938737e-39
PREP_STEPS, MAIN_STEPS = 21, 84


class Events:

    def __init__(self, sem, jobs, by=1):
        self.sem, self.jobs, self.by = sem, list(jobs), by
        self.at = {job: i for i, job in enumerate(self.jobs)}
        self.raised = 0

    def credit(self):
        return len(self.jobs) * self.by

    def now(self, job, b):
        return self.sem, ((b + 1) * len(self.jobs) + self.at[job] + 1) * self.by

    def before(self, job, b):
        return self.sem, (b * len(self.jobs) + self.at[job] + 1) * self.by

    def raised_elsewhere(self, job):
        self.raise_(job)

    def raise_(self, job):
        assert self.jobs[self.raised % len(self.jobs)] == job, (job, self.jobs[self.raised])
        self.raised += 1
        return self.sem, self.by


def build(nc, ins, out):
    ctx = ExitStack()
    with ctx:
        def sb(name, shape, dt=F32):
            return ctx.enter_context(nc.sbuf_tensor(name, shape, dt))

        def sem(name):
            return ctx.enter_context(nc.semaphore(name))

        w1 = sb("w1", [128, 2, E * HC * 128], F32R)
        w2 = sb("w2", [128, 2, E * HC * 128], F32R)
        fab = sb("fab", [128, 2, 2 * HC * 128], F32R)
        fh1 = sb("fh1", [128, 2, HC * HC * 128], F32R)
        fh2 = sb("fh2", [128, 2, HC * HC * 128], F32R)
        fy = sb("fy", [128, 2, HC * 128], F32R)
        anch = sb("anch", [128, 2, H * A], F32R)
        gatew = sb("gatew", [128, 2, E], F32R)
        onehot = sb("onehot", [32, 1024], F32R)
        vout = sb("vout", [128, H * 128])
        wwt = sb("wwt", [128, 128])
        ident = sb("ident", [128, 128])
        ones = sb("ones", [128, 1])
        b1 = sb("b1", [128, E * HC])
        b2 = sb("b2", [128, E])
        gateb = sb("gateb", [128, E])
        order = sb("order", [128, E])
        fs = sb("fs", [128, 4 * HC + 1])
        neghalf = sb("neghalf", [128, T])
        modt = sb("modt", [128, B * NCOL])
        xa = sb("xa", [128, T, 128])
        xb = sb("xb", [128, T, 128])
        hn = sb("hn", [128, T, 128])
        hT = sb("hT", [128, 2, G, GW], F32R)
        ring = sb("ring", [128, 4, GW])
        misc = sb("misc", [128, 2, GW])
        tmp = sb("tmp", [128, 2, GW])
        hid_at = nc.sbuf_base
        hid = sb("hid", [128, 2, HC, 2, GW], F32R)
        cmat_at = nc.sbuf_base
        cmat = sb("cmat", [128, AC, 128])
        rows = sb("rows", [128, 6, 128])
        cols = sb("cols", [128, NCOL])
        pad = sb("pad", [128, 1])
        unused = sb("unused", [128, 1])
        rest = sb("rest", [128, 4])
        flag = sb("flag", [1, 1])
        flag_i = sb("flag_i", [1, 1], mybir.dt.int32)
        gs = sb("gs", [128, 128])
        pmat = sb("pmat", [128, 128])
        stats = sb("stats", [128, T, 6])
        mv = sb("mv", [128, T, 2])
        ve = sb("ve", [128, T])
        rs = sb("rs", [128, T])
        gt = sb("gt", [128, GT, E])
        top = sb("top", [128, GT, 8])
        above = sb("above", [128, GT, E])
        equal = sb("equal", [128, GT, E])
        tops = sb("tops", [128, GT, 8])
        gap = sb("gap", [128, GT])
        th = sb("th", [128, GT])
        wa = sb("wa", [128, 2, GT])
        w32 = sb("w32", [128, GT, 16, 2], F32R)
        nmax = sb("nmax", [128, 2, H])
        m32 = sb("m32", [128, 2, 2 * H], F32R)
        lsum = sb("lsum", [128, H])
        lrec = sb("lrec", [128, H])
        srec = nmax[:, :, :].rearrange("p i h -> p (i h)")[:, 0:3 * AC].rearrange("p (r k) -> p r k", r=3)
        attnT = nc.alloc_sbuf_tensor_at("attnT", [128, AC, N], F32, offset=hid_at)
        wT = nc.alloc_sbuf_tensor_at("wT", [32, G, GW], F32R, offset=cmat_at)
        mTs = wT[:, 0, 0:128]
        h0T = cmat[:, :, :].rearrange("p (g k) n -> p g (k n)", g=G)
        stage = attnT[:, :, :].rearrange("p k n -> p (k n)")

        ps = ctx.enter_context(nc.psum_tensor("ps", [128, 8, 512], F32))
        scratch = nc.dram_tensor("rows_by_batch", (B, 6 * 128), F32, kind="Internal").ap()

        def f(ap):
            return ap.bitcast(F32)

        gs2 = range(G)
        ns = range(G * E)
        ts = range(T)
        cs = range(HC)
        x_loaded = Events(sem("x_loaded"), ["x"], 16)
        rows_loaded = Events(sem("rows_loaded"), ["rows"], 16)
        out_stored = [Events(sem(f"out_stored{g}"), ["out"], 16) for g in range(G)]
        pe_prep = Events(sem("pe_prep"), [("h0T", 0), ("h0T", 1), "gram", "P", ("jn", 0), ("jn", 1),
                                          ("h1T", 0), ("h1T", 1)])
        pe_gate = Events(sem("pe_gate"), [("gate", 0), ("wT", 0), ("gate", 1), ("wT", 1)])
        pe_hid = Events(sem("pe_hid"), range(G * E * HC))
        pe_wb = Events(sem("pe_wb"), ns)
        pe_out = Events(sem("pe_out"), ns)
        pe_res = Events(sem("pe_res"), [("M", 0), ("h2T", 0), ("M", 1), ("h2T", 1), ("A", 0), ("h3T", 0),
                                        ("A", 1), ("h3T", 1), ("F", 0), ("F", 1)])
        pe_logits = Events(sem("pe_logits"), ts)
        pe_maxT = Events(sem("pe_maxT"), ts)
        pe_shift = Events(sem("pe_shift"), ts)
        pe_z = Events(sem("pe_z"), ts)
        pe_attnT = Events(sem("pe_attnT"), [(t, h) for t in ts for h in range(2)])
        pe_fin = Events(sem("pe_fin"), ["s"] + [("C", j) for j in range(4)] + [("O", g) for g in gs2])

        def ffn_jobs(g, part):
            if part == "ab":
                return [(g, k, c) for c in cs for k in "ab"]
            return [(g, part)] if part == "y" else [(g, part, c) for c in cs]

        ffn_order = [(0, "ab"), (0, "h1"), (0, "h2"), (1, "ab"), (1, "h1"), (1, "h2"), (1, "y")]
        pe_jobs = [j for o in ffn_order for j in ffn_jobs(*o)]
        pe_jobs.insert(pe_jobs.index((1, "a", 2)), (0, "y"))
        pe_ffn = Events(sem("pe_ffn"), pe_jobs)
        act_cols = Events(sem("act_cols"), [0, 1])
        act_prep = Events(sem("act_prep"), [("h0T", 0), ("h0T", 1), "gram", ("h1T", 0), ("h1T", 1)])
        act_hi = Events(sem("act_hi"), [(g, c) for g in gs2 for c in cs])
        act_gate = Events(sem("act_gate"), [("th", 0), ("wT", 0), ("th", 1), ("wT", 1)])
        act_gelu = Events(sem("act_gelu"), range(G * E * HC))
        act_wb = Events(sem("act_wb"), ns)
        act_gb = Events(sem("act_gb"), gs2)
        act_hT = Events(sem("act_hT"), gs2)
        act_maxT = Events(sem("act_maxT"), ts)
        act_exp = Events(sem("act_exp"), ts)
        act_attnT = Events(sem("act_attnT"), [(t, h) for t in ts for h in range(2)])
        act_z = Events(sem("act_z"), ["z"])
        act_y = Events(sem("act_y"), [("A", 0), ("A", 1), ("F", 0), ("F", 1)])
        act_h3T = Events(sem("act_h3T"), gs2)
        hidden_order = [(0, "ab"), (0, "h1"), (0, "h2"), (1, "ab"), (1, "h1"), (1, "h2")]
        act_ffn = Events(sem("act_ffn"), [(g, p, c) for g, p in hidden_order for c in cs])
        var, norm, root, every_ln = {}, {}, {}, []
        for layer, lns in ("L0", ["L0a", "L0i", "L0b"]), ("L1", [("L1a", 0), ("L1a", 1), ("L1b", 0), ("L1b", 1)]):
            events = [Events(sem(f"{n}_{layer}"), lns) for n in ("dve_var", "dve_norm", "pool_rs")]
            for k in lns:
                var[k], norm[k], root[k] = events
            every_ln += events
        dve_p = Events(sem("dve_p"), ["P"])
        dve_gap = Events(sem("dve_gap"), gs2)
        dve_w = Events(sem("dve_w"), gs2)
        dve_hT = Events(sem("dve_hT"), [(p, g) for p in ("moe", "attn", "ffn") for g in gs2])
        dve_split = Events(sem("dve_split"), list(range(G * E * HC)) + [(g, p, c) for g, p in hidden_order for c in cs])
        dve_gated = Events(sem("dve_gated"), ns)
        dve_res = Events(sem("dve_res"), [(p, g) for p in "MAF" for g in gs2])
        dve_max = Events(sem("dve_max"), ts)
        dve_rec = Events(sem("dve_rec"), ts)
        dve_attn = Events(sem("dve_attn"), range(1, T))
        pool_attn0 = Events(sem("pool_attn0"), [0])
        dve_srec = Events(sem("dve_srec"), ["s"])
        dve_c = Events(sem("dve_c"), range(4))
        dve_flag = Events(sem("dve_flag"), ["rest", "flag"])
        pe_flag = Events(sem("pe_flag"), ["rest"])
        dve_prod = Events(sem("dve_prod"), [(g, c) for g in gs2 for c in cs])
        prep_step = Events(sem("prep_step"), range(PREP_STEPS))
        main_step = Events(sem("main_step"), range(MAIN_STEPS))
        pool_mul = Events(sem("pool_mul"), [("L0", 0), ("L0", 1), ("L1", 0), ("L1", 1)])
        pool_h = Events(sem("pool_h"), [("L0", 0), ("L0", 1), ("L1", 0), ("L1", 1)])
        pool_x = Events(sem("pool_x"), ["beta", "gamma", "x"])
        pool_acc = Events(sem("pool_acc"), [n for n in ns if n % E])
        pool_asum = Events(sem("pool_asum"), range(1, T))
        every = [v for v in list(locals().values()) if isinstance(v, Events)] + out_stored + every_ln

        l_small, l_l1, l_emb, l_mod, l_mod1, l_ln, l_scr0, l_scr1, l_rows1 = (sem(n) for n in
            ("small_loaded", "ffn_loaded", "emb_loaded", "mod_loaded", "mod1_loaded", "gamma_beta_loaded",
             "rows0_written", "rows1_written", "rows1_loaded"))
        u_raw, u_rows0 = sem("raw_rows0"), sem("rows0_made")
        u_wwt = sem("wwt_made")
        l_moe = [sem(f"moe_loaded{q}") for q in range(4)]
        u_pool, u_act, u_hi, u_lo, u_pe, u_dve = (sem(n) for n in
            ("consts_made", "act_setup", "hi_parts", "lo_parts", "pe_setup", "dve_setup"))

        sets = {(0, "ab"): 0, (0, "h1"): 1, (0, "h2"): 0, (1, "ab"): 1, (1, "h1"): 0, (1, "h2"): 1}
        set_free = {(0, "ab"): (pe_fin, ("O", 1)), (0, "h1"): (pe_fin, ("O", 1)),
                    (0, "h2"): (pe_ffn, (0, "h1", 3)), (1, "ab"): (pe_ffn, (0, "h2", 3)),
                    (1, "h1"): (pe_ffn, (0, "y")), (1, "h2"): (pe_ffn, (1, "h1", 3))}
        L1_PARTS = [(fab, 0, 1024), (fh1, 1024, 2048), (fh2, 3072, 2048), (fy, 5120, 512)]
        all_rows = vout[0:B, 512:1280].rearrange("p (r d) -> p r d", r=6)
        work = vout[0:B, 1280:1792].rearrange("p (r d) -> p r d", r=4)
        w_emb = ring[:, :, :].rearrange("p a n -> p (a n)")
        w_anchor = f(m32[0:64, :, :]).rearrange("p a n -> p (a n)")
        block = ctx.enter_context(nc.Block())

        def by_tile(ap):
            return ap.rearrange("(p t) d -> p t d", t=T)

        @block.sync
        def _(sp):
            for ev in every:
                sp.sem_inc(ev.sem, ev.credit())
            sp.dma_start(cols[:, :], ins["cT"]).then_inc(l_mod, 16)
            wm = ring[:, 0:3, :].rearrange("p a n -> p (a n)")
            sp.dma_start(wm[:, 0:768], ins["wmod"][:, 0:768]).then_inc(l_mod, 16)
            sp.dma_start(xa[:, :, :], by_tile(ins["x"][0])).then_inc(x_loaded.sem, 16)
            sp.dma_start(cmat[0:B, 0, :], ins["gamma"].partition_broadcast(B)).then_inc(l_ln, 16)
            sp.dma_start(cmat[0:B, 1, :], ins["beta"].partition_broadcast(B)).then_inc(l_ln, 16)
            sp.dma_start(wm[:, 768:1536], ins["wmod"][:, 768:1536]).then_inc(l_mod1, 16)
            for dst, src in [(vout[:, 0:128], ins["W_K"]), (vout[:, 128:256], ins["W_Q"]),
                             (vout[:, 256:256 + E], ins["gate_w"]), (nmax[:, 0, 0:1], ins["b_out"]),
                             (fs[:, :], ins["scales"]), (b1[:, :], ins["b1"]), (b2[:, :], ins["b2"]),
                             (gateb[:, :], ins["gate_b"].partition_broadcast(128))]:
                sp.dma_start(dst, src).then_inc(l_small, 16)
            def expert_weights(q):
                w = slice(q * 2048, (q + 1) * 2048)
                src = ins["w1"][:, w] if q < 2 else ins["w2"][:, slice((q - 2) * 2048, (q - 1) * 2048)]
                sp.dma_start(stage[:, w], src).then_inc(l_moe[q], 16)

            expert_weights(0)
            by_row = scratch.rearrange("b (r d) -> b r d", r=6)
            first = scratch[0].rearrange("(r d) -> r d", r=6)
            sp.wait_ge(u_rows0, 1)
            sp.dma_start(by_row[:, 0:4, :], all_rows[:, 0:4, :]).then_inc(l_scr0, 16)
            for q in range(1, 4):
                expert_weights(q)
            sp.dma_start(xb[64:128, :, :], ins["w_out"][:, 8:16, :]).then_inc(l_emb, 16)
            sp.wait_ge(u_pe, 1)
            sp.dma_start(w_emb, ins["w_emb"]).then_inc(l_emb, 16)
            sp.dma_start(w_anchor, ins["w_anchor"]).then_inc(l_emb, 16)
            sp.wait_ge(u_dve, 1)
            sp.dma_start(by_row[:, 4:6, :], all_rows[:, 4:6, :]).then_inc(l_scr1, 16)
            sp.dma_start(misc[64:128, :, :].rearrange("p a (h d) -> p (a h) d", d=128), ins["w_out"][:, 0:8, :])\
                .then_inc(l_emb, 16)
            sp.wait_ge(l_scr0, 16)
            sp.wait_ge(l_scr1, 16)
            sp.dma_start(rows[:, 4:6, :], first[4:6].partition_broadcast(128)).then_inc(l_rows1, 16)
            sp.wait_ge(u_lo, 4)
            sp.dma_start(stage[:, 0:5632], ins["ffn"]).then_inc(l_l1, 16)

            def store(b):
                for g in gs2:
                    sp.wait_ge(*dve_res.now(("F", g), b))
                    sp.dma_start(by_tile(out[b])[:, g * GT:(g + 1) * GT, :], xb[:, g * GT:(g + 1) * GT, :])\
                        .then_inc(out_stored[g].sem, 16)

            with sp.Fori(0, B - 1) as b:
                sp.wait_ge(*dve_res.now(("M", 1), b))
                sp.dma_start(xa[:, :, :], by_tile(ins["x"][b + 1])).then_inc(x_loaded.sem, 16)
                sp.wait_ge(*pool_h.now(("L1", 1), b))
                sp.dma_start(rows[:, :, :], scratch[b + 1].rearrange("(r d) -> r d", r=6).partition_broadcast(128))\
                    .then_inc(rows_loaded.sem, 16)
                store(b)
            store(B - 1)
            for g in gs2:
                sp.wait_ge(out_stored[g].sem, (B + 1) * 16)

        @block.gpsimd
        def _(pool):
            gp = nc.gpsimd
            oh = tmp[0:32, :, :].rearrange("p a n -> p (a n)")
            gp.memset(ident[:, :], 0.0).then_inc(u_pool, 1)
            gp.memset(oh, 0.0).then_inc(u_pool, 1)
            gp.memset(ones[:, :], 1.0).then_inc(u_pool, 1)
            gp.memset(neghalf[:, :], -0.5).then_inc(u_pool, 1)
            for e in range(E):
                gp.memset(order[:, e:e + 1], float(E - e)).then_inc(u_pool, 1)
            pool.wait_ge(u_pool, 12)
            gp.affine_select(out=ident[:, :], in_=ident[:, :], compare_op=ALU.not_equal, fill=1.0, base=0,
                             pattern=[[-1, 128]], channel_multiplier=1).then_inc(u_pool, 1)
            for base in (0, -H):
                v = oh.rearrange("p (h a) -> p h a", h=H)
                gp.affine_select(out=v, in_=v, compare_op=ALU.not_equal, fill=1.0, base=base,
                                 pattern=[[-1, H], [0, A]], channel_multiplier=1).then_inc(u_pool, 1)
                pool.wait_ge(u_pool, 14 if base == 0 else 15)

            def rstd(k, n, b):
                pool.wait_ge(*var[k].now(k, b))
                gp.tensor_tensor(rs[:, 0:n], ve[:, 0:n], neghalf[:, 0:n], ALU.pow).then_inc(*root[k].raise_(k))

            def modulate(layer, g, mul, add, b):
                h = hn[:, g * GT:(g + 1) * GT, :]
                gp.tensor_tensor(h, h, rows[:, mul, :].unsqueeze(1).broadcast_to([128, GT, 128]), ALU.mult)\
                    .then_inc(*pool_mul.raise_((layer, g)))
                pool.wait_ge(*pool_mul.now((layer, g), b))
                gp.tensor_tensor(h, h, rows[:, add, :].unsqueeze(1).broadcast_to([128, GT, 128]), ALU.add)\
                    .then_inc(*pool_h.raise_((layer, g)))

            def prepare_1(b):
                rstd("L0a", T, b)
                pool.wait_ge(*rows_loaded.now("rows", b))
                pool.wait_ge(*norm["L0a"].now("L0a", b))
                for g in gs2:
                    modulate("L0", g, R_C1A0, R_SA0, b)
                add_beta()

            def add_beta():
                gp.tensor_tensor(xa[:, :, :], xa[:, :, :],
                                 rows[:, R_GBETA, :].unsqueeze(1).broadcast_to([128, T, 128]), ALU.add)\
                    .then_inc(*pool_x.raise_("beta"))

            def prepare_2(b):
                rstd("L0i", T, b)
                pool.wait_ge(*norm["L0i"].now("L0i", b))
                gp.tensor_tensor(hn[:, :, :], hn[:, :, :], rows[:, R_GG, :].unsqueeze(1).broadcast_to([128, T, 128]),
                                 ALU.mult).then_inc(*pool_x.raise_("gamma"))
                pool.wait_ge(*pool_x.now("gamma", b))
                gp.tensor_tensor(xa[:, :, :], xa[:, :, :], hn[:, :, :], ALU.add).then_inc(*pool_x.raise_("x"))
                rstd("L0b", T, b)

            def batch(b, more):
                acc = hn[:, GT:T, :].rearrange("p t d -> p (t d)")
                for n in ns:
                    if n % E:
                        pool.wait_ge(*dve_gated.now(n, b))
                        if n % E > 1:
                            pool.wait_ge(*pool_acc.now(n - 1, b))
                        gp.tensor_tensor(acc, acc, tmp[:, n % 2, :], ALU.add).then_inc(*pool_acc.raise_(n))
                    if n == 10:
                        rstd(("L1a", 0), GT, b)
                        pool.wait_ge(*norm[("L1a", 0)].now(("L1a", 0), b))
                        modulate("L1", 0, R_C1A1, R_SA1, b)
                pool.wait_ge(*dve_rec.now(0, b))
                e = ring[:, 0:2, :].rearrange("p k (h a) -> p (k h) a", a=A)
                asum = misc[:, :, :].rearrange("p a n -> p (a n)")
                gp.tensor_tensor(misc[:, :, :].rearrange("p k (h a) -> p (k h) a", a=A), e,
                                 lrec[:, :].unsqueeze(2).broadcast_to([128, H, A]), ALU.mult)\
                    .then_inc(*pool_attn0.raise_(0))
                rstd(("L1a", 1), GT, b)
                pool.wait_ge(*norm[("L1a", 1)].now(("L1a", 1), b))
                modulate("L1", 1, R_C1A1, R_SA1, b)
                for t in range(1, T):
                    pool.wait_ge(*dve_attn.now(t, b))
                    if t == 1:
                        pool.wait_ge(*pe_attnT.now((0, 1), b))
                    else:
                        pool.wait_ge(*pool_asum.now(t - 1, b))
                    gp.tensor_tensor(asum, asum, ring[:, 2 * (t % 2):2 * (t % 2) + 2, :]
                                     .rearrange("p a n -> p (a n)"), ALU.add).then_inc(*pool_asum.raise_(t))
                if more:
                    prepare_1(b + 1)
                rstd(("L1b", 0), GT, b)
                rstd(("L1b", 1), GT, b)
                if more:
                    prepare_2(b + 1)

            rstd("L0a", T, 0)
            for g in gs2:
                pool_mul.raised_elsewhere(("L0", g))
                pool_h.raised_elsewhere(("L0", g))
            pool.wait_ge(*norm["L0a"].now("L0a", 0))
            pool.wait_ge(*rows_loaded.now("rows", 0))
            add_beta()
            for q in range(2):
                pool.wait_ge(u_hi, q + 1)
                gp.tensor_tensor(w1[:, 1, q * 2048:(q + 1) * 2048], stage[:, q * 2048:(q + 1) * 2048],
                                 f(w1[:, 0, q * 2048:(q + 1) * 2048]), ALU.subtract).then_inc(u_lo, 1)
            rstd("L0i", T, 0)
            for job in ("gamma", "x"):
                pool_x.raised_elsewhere(job)
            rstd("L0b", T, 0)
            w, at, n = L1_PARTS[2]
            pool.wait_ge(u_hi, 6)
            gp.tensor_tensor(w[:, 1, :], stage[:, at:at + n], f(w[:, 0, :]), ALU.subtract).then_inc(u_lo, 1)
            pool.wait_ge(l_rows1, 16)
            with pool.Fori(0, B - 1) as b:
                batch(b, True)
            batch(B - 1, False)

        @block.scalar
        def _(act):
            sc = nc.scalar

            def copy(dst, src, scale=1.0):
                return sc.activation(dst, src, ACT.Copy, scale=scale)

            act.wait_ge(l_mod, 32)
            sc.activation(lsum[:, 0:8].rearrange("p (l b) -> p l b", l=2), cols[:, :].rearrange("p (l b) -> p l b", l=2), ACT.Silu)\
                .then_inc(u_act, 1)
            def expert_hi(q):
                act.wait_ge(l_moe[q], 16)
                w, o = (w1, q) if q < 2 else (w2, q - 2)
                copy(w[:, 0, o * 2048:(o + 1) * 2048], stage[:, q * 2048:(q + 1) * 2048]).then_inc(u_hi, 1)

            act.wait_ge(u_pe, 2)
            copy(rows[:, 0:4, :], ps[:, 6, :].rearrange("p (r d) -> p r d", r=4)).then_inc(rows_loaded.sem, 16)
            expert_hi(0)
            expert_hi(1)

            def col(j):
                return cols[:, j:j + 1]

            def load_table(func):
                sc.activation(unused[:, :], ones[:, :], func)

            def from_psum(bank, dst, ev, job, func=ACT.Copy, **kw):
                sc.activation(dst, ps[:, bank, :], func, **kw).then_inc(*ev.raise_(job))

            def load_cols(layer, b):
                at, n = ((0, NC0), (NC0, NC1))[layer]
                copy(cols[:, at:at + n], modt[:, bass.ds(b * NCOL + at, n)]).then_inc(*act_cols.raise_(layer))
                act.wait_ge(*act_cols.now(layer, b))

            def prepare_1(b):
                act.wait_ge(*pe_fin.before(("O", 1), b))
                for g in gs2:
                    act.wait_ge(*pe_prep.now(("h0T", g), b))
                    from_psum(4 + g, h0T[:, g, :], act_prep, ("h0T", g))

            def prepare_1b(b):
                act.wait_ge(*pe_prep.now("gram", b))
                copy(gs[:, :], ps[:, 6, 0:128]).then_inc(*act_prep.raise_("gram"))

            def prepare_2(b):
                act.wait_ge(*act_gb.before(1, b))
                load_cols(0, b)
                act.wait_ge(*dve_hT.before(("ffn", 1), b))
                for g in gs2:
                    act.wait_ge(*pe_prep.now(("h1T", g), b))
                    from_psum(g, misc[:, g, :], act_prep, ("h1T", g), ACT.Identity, scale=col(C1B0), bias=col(SB0))

            def gates(step, g, b):
                if step == "th":
                    act.wait_ge(*dve_gap.now(g, b))
                    sc.activation(th[:, :], gap[:, :], ACT.Tanh, scale=0.5).then_inc(*act_gate.raise_(("th", g)))
                else:
                    act.wait_ge(*pe_gate.now(("wT", g), b))
                    copy(wT[:, g, :], ps[0:32, 1, :]).then_inc(*act_gate.raise_(("wT", g)))

            def attnT_out(t, b):
                if t == 0:
                    act.wait_ge(*pe_out.now(2 * E - 1, b))
                for h in range(2):
                    act.wait_ge(*pe_attnT.now((t, h), b))
                    copy(attnT[:, 4 * h:4 * h + 4, t * 128:(t + 1) * 128],
                         ps[:, h, :].rearrange("p (k n) -> p k n", k=4)).then_inc(*act_attnT.raise_((t, h)))

            def hidden(g, part, b, midway=None):
                def rounded_product(c):
                    if c == 0:
                        act.wait_ge(*set_free[g, part][0].now(set_free[g, part][1], b))
                    act.wait_ge(*dve_prod.now((g, c), b))
                    copy(hid[:, sets[g, part], c, 0, :], ring[:, 2 * (c % 2) + 1, :]).then_inc(*act_hi.raise_((g, c)))

                for c in cs:
                    m = 2 * c if part == "ab" else {"h1": 8, "h2": 12}[part] + c
                    act.wait_ge(*pe_ffn.now((g, "a" if part == "ab" else part, c), b))
                    if part == "ab":
                        if c >= 2:
                            act.wait_ge(*dve_prod.now((g, c - 2), b))
                        else:
                            act.wait_ge(*(dve_split.now((0, "h2", 2 * c), b) if g else pe_fin.now(("C", 3), b)))
                        sc.activation(ring[:, 2 * (c % 2), :], ps[:, 2 + m % 4, :], ACT.Silu,
                                      scale=fs[:, c:c + 1]).then_inc(*act_ffn.raise_((g, part, c)))
                        if c:
                            rounded_product(c - 1)
                        if c == HC - 1:
                            rounded_product(c)
                    else:
                        act.wait_ge(*dve_split.now((g, "ab", 2 + c // 2) if part == "h1" else (g, "h1", c), b))
                        if c == 0:
                            act.wait_ge(*set_free[g, part][0].now(set_free[g, part][1], b))
                        s = HC * (2 if part == "h1" else 3) + c
                        sc.activation(ring[:, c, :], ps[:, 2 + m % 4, :], ACT.Gelu, scale=fs[:, s:s + 1])
                        sc.activation(hid[:, sets[g, part], c, 0, :], ps[:, 2 + m % 4, :], ACT.Gelu,
                                      scale=fs[:, s:s + 1]).then_inc(*act_ffn.raise_((g, part, c)))
                        if c == 1 and midway:
                            midway()

            def out_y(g, b):
                act.wait_ge(*pe_ffn.now((g, "y"), b))
                from_psum(7, tmp[:, g, :], act_y, ("F", g), ACT.Copy, scale=col(GBS3))

            def batch(b, more):
                def hT_attn(g):
                    act.wait_ge(*pe_res.now(("h2T", g), b))
                    act.wait_ge(*pe_hid.now(g * 32 + 31, b))
                    from_psum(1 + g, hT[:, 0, g, :], act_hT, g)

                load_table(ACT.Gelu)
                for n in ns:
                    g, e = divmod(n, E)
                    if n == 4:
                        gates("th", 1, b)
                    for c in cs:
                        m = n * HC + c
                        act.wait_ge(*pe_hid.now(m, b))
                        act.wait_ge(*(dve_split.now(m - 4, b) if m >= 4 else dve_split.before((1, "h2", c), b)))
                        bias = b1[:, e * HC + c:e * HC + c + 1]
                        if c in ACT_HI:
                            if n >= 2:
                                act.wait_ge(*pe_out.now(n - 2, b))
                            else:
                                act.wait_ge(*pe_ffn.before((1, "y"), b))
                            sc.activation(ring[:, m % 4, :], ps[:, 2 + m % 4, :], ACT.Gelu, bias=bias)
                            from_psum(2 + m % 4, hid[:, n % 2, c, 0, :], act_gelu, m, ACT.Gelu, bias=bias)
                        else:
                            from_psum(2 + m % 4, ring[:, m % 4, :], act_gelu, m, ACT.Gelu, bias=bias)
                    if n == 0:
                        gates("wT", 0, b)
                    if n == 6:
                        gates("wT", 1, b)
                    if n:
                        spread(n - 1, b)
                    if n == 9:
                        act.wait_ge(*pool_acc.now(E - 1, b))
                        acc = hn[:, GT:T, :]
                        copy(acc, acc, scale=col(GB0)).then_inc(*act_gb.raise_(0))
                    if n == 14:
                        hT_attn(0)
                load_table(ACT.Exp)
                spread(2 * E - 1, b)

                for t in range(T + 2):
                    if t < T:
                        act.wait_ge(*pe_maxT.now(t, b))
                        if t >= 1:
                            act.wait_ge(*pe_shift.now(t - 1, b))
                        copy(mTs, ps[0:32, 1, 0:128]).then_inc(*act_maxT.raise_(t))
                    if t == T + 1:
                        act.wait_ge(*pe_z.now(T - 1, b))
                        act.wait_ge(*pool_asum.now(T - 2, b))
                        act.wait_ge(*pe_attnT.now((T - 2, 1), b))
                        copy(ring[:, 0:2, :], ps[:, 6:8, :]).then_inc(*act_z.raise_("z"))
                    if t >= 2:
                        attnT_out(t - 2, b)
                    if t < T:
                        act.wait_ge(*pe_shift.now(t, b))
                        if t >= 2:
                            act.wait_ge(*pe_attnT.now((t - 2, 1), b))
                            act.wait_ge(*(pool_asum.now(t - 2, b) if t > 2 else pool_attn0.now(0, b)))
                        else:
                            act.wait_ge(*dve_split.now(G * E * HC - 1, b))
                        e0 = 2 * (t % 2)
                        k0 = 2 + 2 * (t % 2)
                        sc.activation(ring[:, e0:e0 + 2, :], ps[:, k0:k0 + 2, :], ACT.Exp)\
                            .then_inc(*act_exp.raise_(t))
                    if t == 0:
                        act.wait_ge(*pool_acc.now(2 * E - 1, b))
                        copy(acc, acc, scale=col(GB0)).then_inc(*act_gb.raise_(1))
                        act.wait_ge(*act_y.before(("F", 1), b))
                        load_cols(1, b)
                    if t == 2:
                        hT_attn(1)
                act.wait_ge(*pool_acc.now(2 * E - 1, b))
                for g in gs2:
                    act.wait_ge(*pe_fin.now(("O", g), b))
                    from_psum(2 + g, tmp[:, g, :], act_y, ("A", g), ACT.Identity, scale=col(GA1), bias=col(GABO))
                    if g == 0:
                        load_table(ACT.Silu)
                        act.wait_ge(*pe_res.now(("h3T", 0), b))
                        act.wait_ge(*pe_fin.now("s", b))
                        from_psum(0, misc[:, 0, :], act_h3T, 0, ACT.Identity, scale=col(C1B1), bias=col(SB1))

                if more:
                    prepare_1(b + 1)
                hidden(0, "ab", b)
                if more:
                    prepare_1b(b + 1)
                load_table(ACT.Gelu)

                def modulated():
                    act.wait_ge(*pe_res.now(("h3T", 1), b))
                    from_psum(0, misc[:, 1, :], act_h3T, 1, ACT.Identity, scale=col(C1B1), bias=col(SB1))

                hidden(0, "h1", b, modulated)
                hidden(0, "h2", b)
                load_table(ACT.Silu)
                hidden(1, "ab", b)
                load_table(ACT.Gelu)
                out_y(0, b)
                hidden(1, "h1", b)
                if more:
                    prepare_2(b + 1)
                hidden(1, "h2", b)
                if more:
                    gates("th", 0, b + 1)
                out_y(1, b)

            def spread(n, b):
                act.wait_ge(*pe_wb.now(n, b))
                act.wait_ge(*(dve_gated.now(n - 2, b) if n >= 2 else dve_hT.now(("moe", n), b)))
                from_psum(0, misc[:, n % 2, :], act_wb, n)

            prepare_1(0)
            expert_hi(2)
            prepare_1b(0)
            expert_hi(3)
            act.wait_ge(u_pe, 5)
            act.wait_ge(u_dve, 2)
            copy(tmp[:, :, :], ps[:, 6:8, :], scale=DH ** -0.5).then_inc(u_act, 1)
            act.wait_ge(u_act, 2)
            copy(anch[:, 0, :], tmp[:, :, :].rearrange("p a n -> p (a n)")).then_inc(u_act, 1)
            act.wait_ge(l_l1, 16)
            for i in (0, 2, 1, 3):
                w, at, n = L1_PARTS[i]
                copy(w[:, 0, :], stage[:, at:at + n]).then_inc(u_hi, 1)
                if i == 2:
                    prepare_2(0)
            act.wait_ge(u_pe, 6)
            act.wait_ge(l_scr1, 16)
            copy(vout[:, :], ps[:, 2:6, :].rearrange("p a n -> p (a n)")).then_inc(u_act, 1)
            gates("th", 0, 0)
            act.wait_ge(u_lo, 9)
            with act.Fori(0, B - 1) as b:
                batch(b, True)
            batch(B - 1, False)

        @block.vector
        def _(dve):
            v = nc.vector
            flat = "p a n -> p (a n)"
            chain = [0]
            u_chain = sem("setup_chain")

            def link(ins_):
                chain[0] += 1
                ins_.then_inc(u_chain, 1)
                dve.wait_ge(u_chain, chain[0])

            def settle(own, ins_):
                ev, b = own
                at = ev.raised % len(ev.jobs)
                ins_.then_inc(*ev.raise_(at))
                dve.wait_ge(*ev.now(at, b))

            def settle_alone(own, ins_):
                settle(own, ins_)
                v.memset(pad[:, :], 0.0)

            def layer_norm_stats(own, k, srcs):
                n = len(srcs)
                for i, s in enumerate(srcs):
                    last = v.bn_stats(stats[:, i, :], s)
                settle_alone(own, last)
                for i in range(n):
                    last = v.bn_aggr(mv[:, i, :], stats[:, i, :])
                settle(own, last)
                v.tensor_scalar(ve[:, 0:n], mv[:, 0:n, 1], EPS, None, ALU.add).then_inc(*var[k].raise_(k))

            def layer_norm_apply(own, k, srcs, dst):
                dve.wait_ge(*root[k].now(k, own[1]))
                for i, s in enumerate(srcs):
                    last = v.tensor_scalar(dst[:, i, :], s, mv[:, i, 0:1], rs[:, i:i + 1],
                                           ALU.subtract, ALU.mult)
                last.then_inc(*norm[k].raise_(k))

            def layer_norm(own, k, srcs, dst):
                layer_norm_stats(own, k, srcs)
                layer_norm_apply(own, k, srcs, dst)

            def tiles(x, g):
                return [x[:, t, :] for t in range(g * GT, (g + 1) * GT)]

            def split(own, dst_hi, dst_lo, src, ev, job):
                settle(own, v.tensor_copy(dst_hi, src))
                v.tensor_tensor(dst_lo, src, f(dst_hi), ALU.subtract).then_inc(*ev.raise_(job))

            def prepare_1(b, part):
                own, x = (prep_step, b), tiles(xa, 0) + tiles(xa, 1)
                if part == "stats":
                    dve.wait_ge(*x_loaded.now("x", b))
                    layer_norm_stats(own, "L0a", x)
                else:
                    dve.wait_ge(*pe_z.before(T - 1, b))
                    layer_norm_apply(own, "L0a", x, hn)

            def prepare_2(b):
                dve.wait_ge(*pe_prep.now("P", b))
                v.scalar_tensor_tensor(pmat[:, :], ps[:, 7, 0:128], D ** -0.5, ident[:, :], ALU.mult, ALU.add)\
                    .then_inc(*dve_p.raise_("P"))

            def prepare_3(b, part):
                own = (prep_step, b)
                jn = [ps[:, g, t * 128:(t + 1) * 128] for g in gs2 for t in range(GT)]
                if part == "stats":
                    for g in gs2:
                        dve.wait_ge(*pe_prep.now(("jn", g), b))
                    layer_norm_stats(own, "L0i", jn)
                    return
                layer_norm_apply(own, "L0i", jn, hn)

            def prepare_4(b, part):
                own, x = (prep_step, b), tiles(xa, 0) + tiles(xa, 1)
                if part == "stats":
                    dve.wait_ge(*pool_x.now("x", b))
                    layer_norm_stats(own, "L0b", x)
                else:
                    layer_norm_apply(own, "L0b", x, hn)

            def prepare_5(b):
                own = (prep_step, b)
                dve.wait_ge(*pe_ffn.before((1, "b", 3), b))
                for g in gs2:
                    dve.wait_ge(*act_prep.now(("h1T", g), b))
                    split(own, hT[:, 0, g, :], hT[:, 1, g, :], misc[:, g, :], dve_hT, ("moe", g))

            def gates(g, b, step):
                own = (step, b)

                def over_e(ap):
                    return ap.unsqueeze(2).broadcast_to([128, GT, E])

                dve.wait_ge(*pe_gate.now(("gate", g), b))
                settle_alone(own, v.tensor_tensor(gt[:, :, :], ps[:, 1, 0:GT * E].rearrange("p (t e) -> p t e", t=GT),
                                                  gateb[:, :].unsqueeze(1).broadcast_to([128, GT, E]), ALU.add))
                for t in range(GT):
                    last = v.max(top[:, t, :], gt[:, t, :])
                settle(own, last)
                if g:
                    dve.wait_ge(*act_gate.now(("th", 0), b))
                v.tensor_tensor(gap[:, :], top[:, :, 0], top[:, :, 1], ALU.subtract)\
                    .then_inc(*dve_gap.raise_(g))
                v.tensor_tensor(above[:, :, :], gt[:, :, :], over_e(top[:, :, 1]), ALU.is_gt)
                settle(own, v.tensor_tensor(equal[:, :, :], gt[:, :, :], over_e(top[:, :, 1]), ALU.is_equal))
                settle_alone(own, v.tensor_tensor(equal[:, :, :], equal[:, :, :],
                                                  order[:, :].unsqueeze(1).broadcast_to([128, GT, E]), ALU.mult))
                for t in range(GT):
                    last = v.max(tops[:, t, :], equal[:, t, :])
                settle(own, last)
                v.tensor_tensor(wa[:, 0, :], top[:, :, 0], top[:, :, 1], ALU.is_gt)
                settle(own, v.tensor_tensor(wa[:, 1, :], tops[:, :, 0], tops[:, :, 1], ALU.subtract))
                settle(own, v.tensor_tensor(wa[:, 0, :], wa[:, 0, :], wa[:, 1, :], ALU.mult))
                settle(own, v.tensor_tensor(wa[:, 0, :], wa[:, 0, :], tops[:, :, 1], ALU.add))
                settle(own, v.tensor_tensor(equal[:, :, :], equal[:, :, :], over_e(wa[:, 0, :]), ALU.is_ge))
                dve.wait_ge(*act_gate.now(("th", g), b))
                v.tensor_scalar(wa[:, 0, :], th[:, :], 0.5, 0.5, ALU.mult, ALU.add)
                settle(own, v.tensor_scalar(wa[:, 1, :], th[:, :], -0.5, 0.5, ALU.mult, ALU.add))
                v.tensor_tensor(above[:, :, :], above[:, :, :], over_e(wa[:, 0, :]), ALU.mult)
                settle(own, v.tensor_tensor(equal[:, :, :], equal[:, :, :], over_e(wa[:, 1, :]), ALU.mult))
                settle(own, v.tensor_tensor(above[:, :, :], above[:, :, :], equal[:, :, :], ALU.add))
                if g:
                    dve.wait_ge(*pe_gate.now(("wT", 0), b))
                for r in range(2):
                    last = v.tensor_copy(w32[:, :, 0:8, r], above[:, :, :])
                settle(own, last)
                for r in range(2):
                    last = v.tensor_tensor(w32[:, :, 8:16, r], above[:, :, :], f(w32[:, :, 0:8, r]), ALU.subtract)
                last.then_inc(*dve_w.raise_(g))

            def split_hidden(job, slot, s, c, b, hi_made):
                if hi_made:
                    v.tensor_tensor(hid[:, s, c, 1, :], ring[:, slot, :], f(hid[:, s, c, 0, :]), ALU.subtract)\
                        .then_inc(*dve_split.raise_(job))
                else:
                    split((main_step, b), hid[:, s, c, 0, :], hid[:, s, c, 1, :], ring[:, slot, :], dve_split, job)

            def gated(n, b):
                dve.wait_ge(*pe_out.now(n, b))
                dve.wait_ge(*act_wb.now(n, b))
                if n % E == 0:
                    if n:
                        dve.wait_ge(*pe_res.now(("M", 0), b))
                    else:
                        dve.wait_ge(*pe_prep.now(("h1T", 1), b))
                    dst = hn[:, GT:T, :].rearrange("p t d -> p (t d)")
                else:
                    if (n - 2) % E and n >= 3:
                        dve.wait_ge(*pool_acc.now(n - 2, b))
                    if n < 3:
                        dve.wait_ge(*pe_res.before(("F", 1), b))
                    dst = tmp[:, n % 2, :]
                v.scalar_tensor_tensor(dst, ps[:, 6 + n % 2, :], b2[:, n % E:n % E + 1], misc[:, n % 2, :],
                                       ALU.add, ALU.mult).then_inc(*dve_gated.raise_(n))

            def residual(p, g, src, bank, b):
                dve.wait_ge(*pe_res.now((p, g), b))
                if p == "M":
                    dve.wait_ge(*out_stored[g].before("out", b))
                v.tensor_tensor(xb[:, g * GT:(g + 1) * GT, :], src[:, g * GT:(g + 1) * GT, :],
                                ps[:, bank, :].rearrange("p (t d) -> p t d", t=GT), ALU.add)\
                    .then_inc(*dve_res.raise_((p, g)))

            def residual_stats(p, g, k, src, b):
                residual(p, g, src, 0 if (p, g) == ("M", 1) else 1, b)
                dve.wait_ge(*dve_res.now((p, g), b))
                layer_norm_stats((main_step, b), (k, g), tiles(xb, g))

            def normalized(g, k, b):
                dst = hn[:, g * GT:(g + 1) * GT, :] if k == "L1a" else misc[:, g, :].rearrange("p (t d) -> p t d", t=GT)
                layer_norm_apply((main_step, b), (k, g), tiles(xb, g), dst)

            def hT_attn(g, b):
                dve.wait_ge(*act_hT.now(g, b))
                v.tensor_tensor(hT[:, 1, g, :], ps[:, 1 + g, :], f(hT[:, 0, g, :]), ALU.subtract)\
                    .then_inc(*dve_hT.raise_(("attn", g)))

            def hT_ffn(g, b):
                dve.wait_ge(*act_h3T.now(g, b))
                split((main_step, b), hT[:, 0, g, :], hT[:, 1, g, :], misc[:, g, :], dve_hT, ("ffn", g))

            def neg_max(t, b):
                own = (main_step, b)
                dve.wait_ge(*pe_logits.now(t, b))
                k0, i = 2 + 2 * (t % 2), t % 2
                if t >= 2:
                    dve.wait_ge(*dve_max.now(t - 2, b))
                settle(own, v.tensor_reduce(nmax[:, i, :], ps[:, k0:k0 + 2, :].rearrange("p k (h a) -> p (k h) a", a=A),
                                            X, ALU.max, negate=True))
                if t >= 2:
                    dve.wait_ge(*pe_maxT.now(t - 2, b))
                settle(own, v.tensor_copy(m32[:, i, 0:H], nmax[:, i, :]))
                v.tensor_tensor(m32[:, i, H:2 * H], nmax[:, i, :], f(m32[:, i, 0:H]), ALU.subtract)\
                    .then_inc(*dve_max.raise_(t))

            def exponentials(t):
                return ring[:, 2 * (t % 2):2 * (t % 2) + 2, :].rearrange("p k (h a) -> p (k h) a", a=A)

            def sums(t, b):
                dve.wait_ge(*act_exp.now(t, b))
                if t == 1:
                    dve.wait_ge(*pool_attn0.now(0, b))
                settle((main_step, b), v.tensor_reduce(lsum[:, :], exponentials(t), X, ALU.add))
                v.reciprocal(lrec[:, :], lsum[:, :]).then_inc(*dve_rec.raise_(t))

            def scaled(t, b):
                dve.wait_ge(*dve_rec.now(t, b))
                e = exponentials(t)
                v.tensor_tensor(e, e, lrec[:, :].unsqueeze(2).broadcast_to([128, H, A]), ALU.mult)\
                    .then_inc(*dve_attn.raise_(t))

            def normalize(t, b):
                sums(t, b)
                scaled(t, b)

            def hidden(g, part, b, midway=None):
                ev, job = set_free[g, part]
                dve.wait_ge(*ev.now(job, b))

                def remainder(c):
                    dve.wait_ge(*act_hi.now((g, c), b))
                    split_hidden((g, part, c), 2 * (c % 2) + 1, sets[g, part], c, b, True)

                for c in cs:
                    dve.wait_ge(*act_ffn.now((g, part, c), b))
                    if part == "ab":
                        dve.wait_ge(*pe_ffn.now((g, "b", c), b))
                        if c >= 2:
                            dve.wait_ge(*dve_split.now((g, part, c - 2), b))
                        elif g:
                            dve.wait_ge(*dve_split.now((0, "h2", 2 * c + 1), b))
                        slot = 2 * (c % 2) + 1
                        v.scalar_tensor_tensor(ring[:, slot, :], ps[:, 2 + (2 * c + 1) % 4, :],
                                               fs[:, HC + c:HC + c + 1], ring[:, slot - 1, :], ALU.mult, ALU.mult)\
                            .then_inc(*dve_prod.raise_((g, c)))
                        if c:
                            remainder(c - 1)
                        if c == HC - 1:
                            remainder(c)
                    else:
                        split_hidden((g, part, c), c, sets[g, part], c, b, True)
                        if c == 1 and midway:
                            midway()

            def remainders_max(parts):
                for i in parts:
                    last = v.tensor_reduce(rest[:, i:i + 1], f(L1_PARTS[i][0][:, 1, :]), X, ALU.max,
                                           apply_absolute_value=True)
                return last

            def batch(b, more):
                for n in ns:
                    if n == 4:
                        gates(1, b, main_step)
                    for c in cs:
                        mm = n * HC + c
                        dve.wait_ge(*act_gelu.now(mm, b))
                        if c == 0:
                            dve.wait_ge(*(pe_out.now(n - 2, b) if n >= 2 else pe_ffn.before((1, "y"), b)))
                        split_hidden(mm, mm % 4, n % 2, c, b, c in ACT_HI)
                        if (n, c) == (12, 1):
                            normalized(0, "L1a", b)
                    if n:
                        gated(n - 1, b)
                    if n == 11:
                        residual_stats("M", 0, "L1a", xa, b)
                    if n == 14:
                        hT_attn(0, b)
                neg_max(0, b)
                neg_max(1, b)
                gated(2 * E - 1, b)

                sums(0, b)
                neg_max(2, b)
                residual_stats("M", 1, "L1a", xa, b)
                sums(1, b)
                normalized(1, "L1a", b)
                scaled(1, b)
                neg_max(3, b)
                sums(2, b)
                hT_attn(1, b)
                scaled(2, b)
                for t in range(4, T + 1):
                    if t < T:
                        neg_max(t, b)
                    normalize(t - 1, b)
                if more:
                    prepare_1(b + 1, "stats")
                own = (main_step, b)
                remainders_max((0, 3))
                dve.wait_ge(*pe_fin.now("s", b))
                v.tensor_scalar(srec[:, 0, :], ps[:, 5, 0:AC], TINY, None, ALU.is_ge)
                v.tensor_scalar(srec[:, 1, :], ps[:, 5, 0:AC], TINY, None, ALU.max).then_inc(*dve_srec.raise_("s"))
                dve.wait_ge(*dve_srec.now("s", b))
                settle(own, v.reciprocal(srec[:, 2, :], srec[:, 1, :]))
                settle(own, v.tensor_tensor(srec[:, 2, :], srec[:, 2, :], srec[:, 0, :], ALU.mult))
                for j in range(4):
                    dve.wait_ge(*pe_fin.now(("C", j), b))
                    src = ps[:, 2 + j, :].rearrange("p (k n) -> p k n", k=2)
                    for half in range(2):
                        p = slice(64 * half, 64 * half + 64)
                        last = v.tensor_tensor(cmat[p, 2 * j:2 * j + 2, :], src[p, :, half * 128:half * 128 + 128],
                                               srec[p, 2, 2 * j:2 * j + 2].unsqueeze(2).broadcast_to([64, 2, 128]),
                                               ALU.mult)
                    last.then_inc(*dve_c.raise_(j))
                if more:
                    prepare_1(b + 1, "apply")
                settle(own, remainders_max((1, 2)))
                v.tensor_reduce(rest[:, 0:1], rest[:, :], X, ALU.max).then_inc(*dve_flag.raise_("rest"))
                dve.wait_ge(*pe_flag.now("rest", b))
                settle(own, v.tensor_reduce(flag[:, :], ps[0:1, 0, 0:128], X, ALU.max))
                settle(own, v.tensor_scalar(flag[:, :], flag[:, :], 0.0, None, ALU.is_gt))
                v.tensor_copy(flag_i[:, :], flag[:, :]).then_inc(*dve_flag.raise_("flag"))
                residual_stats("A", 0, "L1b", xb, b)
                normalized(0, "L1b", b)
                hT_ffn(0, b)
                residual_stats("A", 1, "L1b", xb, b)

                hidden(0, "ab", b)
                normalized(1, "L1b", b)
                hidden(0, "h1", b, (lambda: prepare_2(b + 1)) if more else None)
                hT_ffn(1, b)
                if more:
                    prepare_3(b + 1, "stats")
                hidden(0, "h2", b, (lambda: prepare_3(b + 1, "apply")) if more else None)
                hidden(1, "ab", b)
                if more:
                    prepare_4(b + 1, "stats")
                hidden(1, "h1", b, (lambda: prepare_4(b + 1, "apply")) if more else None)
                residual("F", 0, xb, 7, b)
                if more:
                    prepare_5(b + 1)
                hidden(1, "h2", b)
                if more:
                    gates(0, b + 1, prep_step)
                residual("F", 1, xb, 7, b)
                for ev in (prep_step, main_step):
                    assert ev.raised % len(ev.jobs) == 0, (ev.raised, len(ev.jobs))

            v.memset(pmat[0:1, :], 1.0)
            prepare_1(0, "stats")
            raw = misc[0:B, :, :].rearrange(flat)
            raw1 = xb[0:B, :, :].rearrange("p t d -> p (t d)")
            m = [raw[:, 0:768].rearrange("p (j d) -> p j d", j=6), raw1[:, 0:768].rearrange("p (j d) -> p j d", j=6)]

            def modulation(l):
                for j in range(2):
                    last = v.tensor_copy(m[l][:, 3 * j:3 * j + 3, :].rearrange("p j d -> p (j d)"),
                                         ps[0:B, 2 - 2 * l + j, 0:384])
                link(last)
                mj = m[l].rearrange("p (a j) d -> p j a d", a=2)
                v.tensor_scalar(mj[:, 1], mj[:, 1], 1.0, None, ALU.add)
                v.tensor_scalar(work[:, 0:2, :], mj[:, 2], 0.0, 2.0, ALU.is_ge, ALU.mult)
                link(v.scalar_tensor_tensor(work[:, 2:4, :], mj[:, 2], -1.0, mj[:, 2], ALU.mult, ALU.max))
                link(v.tensor_scalar(work[:, 2:4, :], work[:, 2:4, :], 0.25, None, ALU.max))
                link(v.scalar_tensor_tensor(mj[:, 2], work[:, 0:2, :], -1.0, work[:, 2:4, :], ALU.add, ALU.mult))

            dve.wait_ge(u_raw, 1)
            modulation(0)
            v.tensor_copy(all_rows[:, R_C1A0, :], m[0][:, 1, :])
            v.tensor_copy(all_rows[:, R_SA0, :], m[0][:, 0, :])
            dve.wait_ge(l_ln, 32)
            v.tensor_tensor(all_rows[:, R_GG, :], m[0][:, 2, :], cmat[0:B, 0, :], ALU.mult)
            v.tensor_tensor(all_rows[:, R_GBETA, :], m[0][:, 2, :], cmat[0:B, 1, :], ALU.mult).then_inc(u_rows0, 1)
            prepare_1(0, "apply")

            def over_tiles(row, n):
                return rows[:, row, :].unsqueeze(1).broadcast_to([128, n, 128])

            dve.wait_ge(*rows_loaded.now("rows", 0))
            dve.wait_ge(*norm["L0a"].now("L0a", 0))
            for g in gs2:
                h = hn[:, g * GT:(g + 1) * GT, :]
                v.tensor_tensor(h, h, over_tiles(R_C1A0, GT), ALU.mult).then_inc(pool_mul.sem, 1)
            for g in gs2:
                h = hn[:, g * GT:(g + 1) * GT, :]
                dve.wait_ge(*pool_mul.now(("L0", g), 0))
                v.tensor_tensor(h, h, over_tiles(R_SA0, GT), ALU.add).then_inc(pool_h.sem, 1)
            dve.wait_ge(u_pe, 1)
            modulation(1)
            v.tensor_copy(all_rows[:, R_C1A1, :], m[1][:, 1, :])
            v.tensor_copy(all_rows[:, R_SA1, :], m[1][:, 0, :]).then_inc(u_dve, 1)
            dve.wait_ge(l_small, 8 * 16)
            dve.wait_ge(u_pool, 15)
            v.tensor_copy(onehot[:, :], tmp[0:32, :, :].rearrange(flat))
            link(v.tensor_copy(gatew[:, 0, :], vout[:, 256:256 + E]))
            v.tensor_tensor(gatew[:, 1, :], vout[:, 256:256 + E], f(gatew[:, 0, :]), ALU.subtract)
            dve.wait_ge(u_pe, 3)
            v.tensor_copy(wwt[:, :], ps[:, 3, 0:128]).then_inc(u_wwt, 1)
            mt = modt[:, :].rearrange("p (b j) -> p b j", b=B)
            pt = ps[:, 2, 0:7 * B].rearrange("p (j b) -> p b j", b=B)
            dve.wait_ge(u_pe, 4)
            v.tensor_copy(mt[:, :, C1B0:GA1 + 1], pt[:, :, 0:4])
            v.tensor_scalar(mt[:, :, GABO], pt[:, :, 3], nmax[:, 0, 0:1], None, ALU.mult)
            v.tensor_copy(mt[:, :, C1B1:SB1 + 1], pt[:, :, 4:6])
            v.tensor_scalar(mt[:, :, GBS3], pt[:, :, 6], fs[:, 4 * HC:4 * HC + 1], None, ALU.mult).then_inc(u_dve, 1)
            def expert_lo(q):
                dve.wait_ge(u_hi, q + 1)
                w, o = w2, q - 2
                v.tensor_tensor(w[:, 1, o * 2048:(o + 1) * 2048], stage[:, q * 2048:(q + 1) * 2048],
                                f(w[:, 0, o * 2048:(o + 1) * 2048]), ALU.subtract).then_inc(u_lo, 1)

            def ffn_lo(i):
                w, at, n = L1_PARTS[i]
                dve.wait_ge(u_hi, 7 if i == 1 else 5 + i)
                v.tensor_tensor(w[:, 1, :], stage[:, at:at + n], f(w[:, 0, :]), ALU.subtract).then_inc(u_lo, 1)

            prepare_2(0)
            expert_lo(2)
            prepare_3(0, "stats")
            expert_lo(3)
            prepare_3(0, "apply")
            dve.wait_ge(*pool_x.now("beta", 0))
            dve.wait_ge(*norm["L0i"].now("L0i", 0))
            v.tensor_tensor(hn[:, :, :], hn[:, :, :], over_tiles(R_GG, T), ALU.mult).then_inc(pool_x.sem, 1)
            dve.wait_ge(*pool_x.now("gamma", 0))
            v.tensor_tensor(xa[:, :, :], xa[:, :, :], hn[:, :, :], ALU.add).then_inc(pool_x.sem, 1)
            prepare_4(0, "stats")
            dve.wait_ge(u_act, 3)
            v.tensor_tensor(anch[:, 1, :], tmp[:, :, :].rearrange(flat), f(anch[:, 0, :]), ALU.subtract)\
                .then_inc(u_lo, 1)
            prepare_4(0, "apply")
            ffn_lo(0)
            prepare_5(0)
            ffn_lo(1)
            ffn_lo(3)
            gates(0, 0, prep_step)
            dve.wait_ge(u_lo, 9)
            with dve.Fori(0, B - 1) as b:
                batch(b, True)
            batch(B - 1, False)

        @block.tensor
        def _(pe):
            te = nc.tensor

            def transposes(bank, srcs, ev, job, rows_=128):
                for i, s in enumerate(srcs):
                    last_ = te.transpose(ps[0:rows_, bank, i * 128:(i + 1) * 128], s, ident[:, :])
                last_.then_inc(*ev.raise_(job))

            def three(out_, w, x, first, last_, all_=True):
                te.matmul(out_, w(0), x(0), start=first, stop=False)
                if not all_:
                    return te.matmul(out_, w(0), x(1), start=False, stop=last_)
                te.matmul(out_, w(0), x(1), start=False, stop=False)
                return te.matmul(out_, w(1), x(0), start=False, stop=last_)

            def tiles(x, g):
                return [x[:, t, :] for t in range(g * GT, (g + 1) * GT)]

            def quarters(x):
                return [x[:, t * 128:(t + 1) * 128] for t in range(GT)]

            def prepare_1(b):
                for g in gs2:
                    pe.wait_ge(*pool_h.now(("L0", g), b))
                    pe.wait_ge(*dve_c.before(3, b))
                    transposes(4 + g, tiles(hn, g), pe_prep, ("h0T", g))

            def prepare_1b(b, tiles_=ts):
                pe.wait_ge(*act_z.before("z", b))
                for t in tiles_:
                    last = te.matmul(ps[:, 6, 0:128], hn[:, t, :], hn[:, t, :], start=t == 0, stop=t == T - 1)
                if T - 1 in tiles_:
                    last.then_inc(*pe_prep.raise_("gram"))

            def prepare_2(b):
                pe.wait_ge(*act_prep.now("gram", b))
                te.matmul(ps[:, 7, 0:128], wwt[:, :], gs[:, :], start=True, stop=True).then_inc(*pe_prep.raise_("P"))

            def prepare_3(b):
                pe.wait_ge(*dve_p.now("P", b))
                for g in gs2:
                    pe.wait_ge(*act_prep.now(("h0T", g), b))
                    pe.wait_ge(*(dve_res.before(("A", 1), b) if g else act_h3T.before(1, b)))
                    for t in range(GT):
                        last = te.matmul(ps[:, g, t * 128:(t + 1) * 128], h0T[:, g, t * 128:(t + 1) * 128],
                                         pmat[:, :], start=True, stop=True)
                    last.then_inc(*pe_prep.raise_(("jn", g)))

            def prepare_4(b):
                pe.wait_ge(*norm["L0b"].now("L0b", b))
                for g in gs2:
                    transposes(g, tiles(hn, g), pe_prep, ("h1T", g))

            def gates(g, b):
                pe.wait_ge(*dve_hT.now(("moe", 1), b))
                if g:
                    pe.wait_ge(*act_gate.now(("wT", 0), b))
                for t in range(GT):
                    last = three(ps[:, 1, t * E:(t + 1) * E], lambda i: hT[:, i, g, t * 128:(t + 1) * 128],
                                 lambda i: gatew[:, i, :], True, True)
                last.then_inc(*pe_gate.raise_(("gate", g)))

            def gates_transposed(g, b):
                pe.wait_ge(*dve_w.now(g, b))
                transposes(1, [f(w32[:, t, :, :]).rearrange("p a r -> p (a r)") for t in range(GT)],
                           pe_gate, ("wT", g), 32)

            def first_product(n, b):
                g, e = divmod(n, E)
                for c in cs:
                    mm = n * HC + c
                    pe.wait_ge(*(act_gelu.now(mm - 4, b) if mm >= 4 else act_ffn.before((1, "h2", c), b)))
                    at = (e * HC + c) * 128
                    three(ps[:, 2 + mm % 4, :], lambda i: w1[:, i, at:at + 128], lambda i: hT[:, i, g, :],
                          True, True).then_inc(*pe_hid.raise_(mm))

            def spread_gates(n, b):
                g, e = divmod(n, E)
                pe.wait_ge(*(act_wb.now(n - 1, b) if n else act_prep.now(("h1T", 0), b)))
                pe.wait_ge(*act_gate.now(("wT", g), b))
                te.matmul(ps[:, 0, :], onehot[:, e * 128:(e + 1) * 128], wT[:, g, :], start=True, stop=True)\
                    .then_inc(*pe_wb.raise_(n))

            def second_product(n, b, midway={}):
                e = n % E
                if n >= 2:
                    pe.wait_ge(*dve_gated.now(n - 2, b))
                else:
                    pe.wait_ge(*(dve_res.before(("F", 1), b) if n else act_prep.now("gram", b)))
                for c in cs:
                    pe.wait_ge(*dve_split.now(n * HC + c, b))
                    at = (e * HC + c) * 128
                    last_ = three(ps[:, 6 + n % 2, :], lambda i: w2[:, i, at:at + 128],
                                  lambda i: hid[:, n % 2, c, i, :], c == 0, c == HC - 1)
                    if c in midway:
                        midway[c]()
                last_.then_inc(*pe_out.raise_(n))

            def logits(t, b):
                pe.wait_ge(*dve_hT.now(("attn", t // GT), b))
                pe.wait_ge(*(act_exp.now(t - 2, b) if t >= 2 else act_gelu.now(G * E * HC - 1, b)))
                tok = slice((t % GT) * 128, (t % GT + 1) * 128)
                for h in range(2):
                    last_ = three(ps[:, 2 + 2 * (t % 2) + h, :], lambda i: hT[:, i, t // GT, tok],
                                  lambda i: anch[:, i, h * 512:(h + 1) * 512], True, True)
                last_.then_inc(*pe_logits.raise_(t))

            def max_transposed(t, b):
                pe.wait_ge(*dve_max.now(t, b))
                if t == 0:
                    pe.wait_ge(*dve_hT.now(("attn", 0), b))
                if t >= 3:
                    pe.wait_ge(*act_attnT.now((t - 3, 1), b))
                transposes(1, [f(m32[:, t % 2, :])], pe_maxT, t, 32)

            def shift(t, b):
                pe.wait_ge(*act_maxT.now(t, b))
                for h in range(2):
                    last_ = te.matmul(ps[:, 2 + 2 * (t % 2) + h, :], mTs, onehot[:, h * 512:(h + 1) * 512],
                                      start=False, stop=True, skip_group_check=True)
                last_.then_inc(*pe_shift.raise_(t))

            def attention(t, h):
                return ring[:, 2 * (t % 2) + h, :] if t else misc[:, h, :]

            def gather(t, b):
                pe.wait_ge(*(dve_attn.now(t, b) if t else pool_attn0.now(0, b)))
                for h in range(2):
                    last_ = te.matmul(ps[:, 6 + h, :], hn[:, t, :], attention(t, h),
                                      start=t == 0, stop=t == T - 1)
                last_.then_inc(*pe_z.raise_(t))

            def attn_transposed(t, b):
                for h in range(2):
                    if t:
                        pe.wait_ge(*act_attnT.now((t - 1, h), b))
                    elif h == 0:
                        pe.wait_ge(*dve_res.now(("M", 1), b))
                    if h == 1 and t + 2 < T:
                        pe.wait_ge(*act_maxT.now(t + 2, b))
                    transposes(h, quarters(attention(t, h)), pe_attnT, (t, h))

            def outputs(g, ks, b):
                for k in ks:
                    if g == 0 and k % 2 == 0:
                        pe.wait_ge(*dve_c.now(k // 2, b))
                    last_ = te.matmul(ps[:, 2 + g, :], cmat[:, k, :], attnT[:, k, g * GW:(g + 1) * GW],
                                      start=k == 0, stop=k == AC - 1)
                if AC - 1 in ks:
                    last_.then_inc(*pe_fin.raise_(("O", g)))

            def residual_transposed(p, g, bank, b):
                pe.wait_ge(*act_y.now((p, g), b))
                if p == "F":
                    if g:
                        pe.wait_ge(*dve_res.now(("F", 0), b))
                else:
                    pe.wait_ge(*(dve_res.now(("A", 0), b) if g else dve_srec.now("s", b)))
                transposes(bank, quarters(tmp[:, g, :]), pe_res, (p, g))

            def h3_transposed(g, b):
                pe.wait_ge(*norm[("L1b", g)].now(("L1b", g), b))
                pe.wait_ge(*(act_h3T.now(0, b) if g else dve_flag.now("flag", b)))
                transposes(0, quarters(misc[:, g, :]), pe_res, ("h3T", g))

            def bank_read(g, m_, b):
                if m_ < 4:
                    return act_ffn.now((0, "h2", m_), b) if g else act_y.now(("A", 1), b)
                m_ -= 4
                if m_ >= 8:
                    return act_ffn.now((g, "h1", m_ - 8), b)
                return dve_prod.now((g, m_ // 2), b) if m_ % 2 else act_ffn.now((g, "ab", m_ // 2), b)

            def first_layer(g, b, all_):
                pe.wait_ge(*dve_hT.now(("ffn", g), b))
                for c in cs:
                    if g and c == 2:
                        last_layer(0, 0, b, all_)
                    for k in range(2):
                        m_ = 2 * c + k
                        pe.wait_ge(*bank_read(g, m_, b))
                        at = (k * HC + c) * 128
                        three(ps[:, 2 + m_ % 4, :], lambda i: fab[:, i, at:at + 128], lambda i: hT[:, i, g, :],
                              True, True, all_).then_inc(*pe_ffn.raise_((g, "ab"[k], c)))

            def hidden_layer(g, part, w, src, src_set, base, b, all_, midway=None):
                for pair in range(2):
                    if pair and midway:
                        midway()
                    for kc in cs:
                        pe.wait_ge(*dve_split.now((g, src, kc), b))
                        for o in (2 * pair, 2 * pair + 1):
                            if kc == 0:
                                pe.wait_ge(*bank_read(g, base + o, b))
                            at = kc * 512 + o * 128
                            last_ = three(ps[:, 2 + (base + o) % 4, :], lambda i: w[:, i, at:at + 128],
                                          lambda i: hid[:, src_set, kc, i, :], kc == 0, kc == HC - 1, all_)
                            if kc == HC - 1:
                                last_.then_inc(*pe_ffn.raise_((g, part, o)))

            def last_layer(g, src_set, b, all_):
                if g:
                    pe.wait_ge(*dve_res.now(("F", 0), b))
                for kc in cs:
                    pe.wait_ge(*dve_split.now((g, "h2", kc), b))
                    last_ = three(ps[:, 7, :], lambda i: fy[:, i, kc * 128:(kc + 1) * 128],
                                  lambda i: hid[:, src_set, kc, i, :], kc == 0, kc == HC - 1, all_)
                last_.then_inc(*pe_ffn.raise_((g, "y")))

            def ffn(b, more, all_):
                if more:
                    pe.wait_ge(*act_prep.now(("h0T", 1), b + 1))
                first_layer(0, b, all_)
                if more:
                    prepare_1b(b + 1, range(GT, T))

                def between():
                    h3_transposed(1, b)
                    if more:
                        prepare_2(b + 1)

                hidden_layer(0, "h1", fh1, "ab", 0, 8, b, all_, between)
                if more:
                    prepare_3(b + 1)
                hidden_layer(0, "h2", fh2, "h1", 1, 12, b, all_)
                first_layer(1, b, all_)
                hidden_layer(1, "h1", fh1, "ab", 1, 8, b, all_)
                residual_transposed("F", 0, 7, b)
                hidden_layer(1, "h2", fh2, "h1", 0, 12, b, all_, (lambda: prepare_4(b + 1)) if more else None)
                if more:
                    gates(0, b + 1)
                last_layer(1, 1, b, all_)
                if more:
                    first_product(0, b + 1)
                residual_transposed("F", 1, 7, b)

            def batch(b, more):
                acc = hn[:, GT:T, :].rearrange("p t d -> p (t d)")
                for n in ns:
                    if n == 3:
                        gates(1, b)
                    if n:
                        first_product(n, b)
                    if n == 0:
                        gates_transposed(0, b)
                    if n == 5:
                        gates_transposed(1, b)
                    if n > 1:
                        spread_gates(n - 1, b)
                    if n:
                        second_product(n - 1, b)
                    if n == 1:
                        spread_gates(0, b)
                    if n == 10:
                        pe.wait_ge(*act_gb.now(0, b))
                        pe.wait_ge(*act_gate.now(("wT", 1), b))
                        transposes(1, quarters(acc), pe_res, ("M", 0))
                    if n == 14:
                        pe.wait_ge(*pool_h.now(("L1", 0), b))
                        transposes(1, tiles(hn, 0), pe_res, ("h2T", 0))
                logits(0, b)
                logits(1, b)
                spread_gates(2 * E - 1, b)
                second_product(2 * E - 1, b, {1: lambda: max_transposed(0, b), 2: lambda: shift(0, b)})
                for t in range(T + 2):
                    if t == 2:
                        pe.wait_ge(*dve_gated.now(2 * E - 1, b))
                    if t >= 2:
                        gather(t - 2, b)
                    if t == 3:
                        pe.wait_ge(*pool_h.now(("L1", 1), b))
                        pe.wait_ge(*act_exp.now(2, b))
                        transposes(2, tiles(hn, 1), pe_res, ("h2T", 1))
                    if 0 < t < T:
                        max_transposed(t, b)
                    if t >= 2:
                        attn_transposed(t - 2, b)
                    if 2 <= t + 1 < T:
                        logits(t + 1, b)
                    if t == 1:
                        pe.wait_ge(*act_gb.now(1, b))
                        pe.wait_ge(*act_wb.now(2 * E - 1, b))
                        transposes(0, quarters(acc), pe_res, ("M", 1))
                    if 0 < t < T:
                        shift(t, b)
                pe.wait_ge(*pool_asum.now(T - 1, b))
                asum = misc[:, :, :].rearrange("p a n -> p (a n)")
                for k in range(AC):
                    last = te.matmul(ps[:, 5, k:k + 1], asum[:, k * 128:(k + 1) * 128], ones[:, :], start=True, stop=True)
                last.then_inc(*pe_fin.raise_("s"))
                pe.wait_ge(*act_z.now("z", b))
                zT = ring[:, 0:2, :].rearrange("p a n -> p (a n)")
                for j in range(4):
                    if j == 3:
                        pe.wait_ge(*dve_srec.now("s", b))
                    for k in range(2):
                        q = 2 * j + k
                        last = te.matmul(ps[:, 2 + j, k * 256:(k + 1) * 256], zT[:, q * 128:(q + 1) * 128],
                                         vout[:, q * 256:(q + 1) * 256], start=True, stop=True)
                    last.then_inc(*pe_fin.raise_(("C", j)))
                pe.wait_ge(*act_attnT.now((T - 1, 1), b))
                outputs(0, range(AC), b)
                outputs(1, range(1), b)
                pe.wait_ge(*dve_flag.now("rest", b))
                te.transpose(ps[0:1, 0, 0:128], rest[:, 0:1], ident[:, :]).then_inc(*pe_flag.raise_("rest"))
                residual_transposed("A", 0, 1, b)
                outputs(1, range(1, 7), b)
                h3_transposed(0, b)
                outputs(1, range(7, AC), b)
                if more:
                    prepare_1(b + 1)
                residual_transposed("A", 1, 1, b)
                if more:
                    prepare_1b(b + 1, range(GT))
                pe.wait_ge(*dve_flag.now("flag", b))
                pe.nop(nofuse=True)
                pe.reg_load(inexact, flag_i[0:1, 0:1])
                before = {ev: ev.raised for ev in every}
                with pe.If_eq(inexact, 0):
                    ffn(b, more, False)
                for ev, n in before.items():
                    ev.raised = n
                with pe.Else():
                    ffn(b, more, True)

            pe.wait_ge(u_act, 1)
            wm = ring[:, 0:3, :].rearrange("p a n -> p (a n)")
            for l in range(2):
                if l:
                    pe.wait_ge(l_mod1, 16)
                for j in range(2):
                    last = te.matmul(ps[0:B, 2 - 2 * l + j, 0:384], lsum[:, 4 * l:4 * l + 4],
                                     wm[:, 768 * l + 384 * j:768 * l + 384 * (j + 1)], start=True, stop=True)
                last.then_inc(u_pe if l else u_raw, 1)
            pe.wait_ge(u_rows0, 1)
            te.matmul(ps[:, 6, :], pmat[0:1, :], all_rows[0:1, 0:4, :].rearrange("p r d -> p (r d)"),
                      start=True, stop=True).then_inc(u_pe, 1)
            prepare_1(0)
            prepare_1b(0)
            pe.wait_ge(u_dve, 1)
            pe.wait_ge(l_small, 8 * 16)
            te.matmul(ps[:, 3, 0:128], vout[:, 0:128], vout[:, 128:256], start=True, stop=True).then_inc(u_pe, 1)
            pe.wait_ge(u_pool, 13)
            m0 = misc[0:B, :, :].rearrange("p a n -> p (a n)")
            m1 = xb[0:B, :, :].rearrange("p t d -> p (t d)")
            for j, (src, at) in enumerate([(m0, 4), (m0, 3), (m0, 5), (m1, 2), (m1, 4), (m1, 3), (m1, 5)]):
                last = te.transpose(ps[:, 2, j * B:(j + 1) * B], src[:, at * 128:(at + 1) * 128], ident[0:B, 0:B])
            last.then_inc(u_pe, 1)
            pe.wait_ge(u_wwt, 1)
            prepare_2(0)
            prepare_3(0)
            pe.wait_ge(l_emb, 4 * 16)
            pe.wait_ge(u_dve, 2)
            for g in gs2:
                pe.wait_ge(*act_prep.now(("h0T", g), 0))
            for h in range(H):
                last = te.matmul(ps[:, 6 + h // 8, (h % 8) * A:(h % 8 + 1) * A],
                                 w_emb[0:64, h * 128:(h + 1) * 128], w_anchor, start=True, stop=True)
            last.then_inc(u_pe, 1)
            for h in range(H):
                w_o = misc[64:128, h // 4, (h % 4) * 128:(h % 4 + 1) * 128] if h < 8 else xb[64:128, h % 8, :]
                last = te.matmul(ps[:, 2 + h // 4, (h % 4) * 128:(h % 4 + 1) * 128],
                                 w_emb[64:128, h * 128:(h + 1) * 128], w_o, start=True, stop=True)
            last.then_inc(u_pe, 1)
            prepare_4(0)
            gates(0, 0)
            pe.wait_ge(u_act, 4)
            pe.wait_ge(u_lo, 9)
            first_product(0, 0)
            inexact = pe.alloc_register("inexact")

            with pe.Fori(0, B - 1) as b:
                batch(b, True)
            batch(B - 1, False)


def kernel(**inputs):
    import numpy as np
    import concourse.bacc as bacc
    from concourse.bass_utils import run_bass_kernel_spmd

    i = {k: np.asarray(v) for k, v in inputs.items()}

    def c(a):
        return np.ascontiguousarray(a)

    def out_chunks(w, k):
        o, n = w.shape
        return w.T.reshape(k, 128, o).transpose(1, 0, 2).reshape(128, k * o)

    emb = i["L1_attn_W_emb"]
    heads = emb.reshape(2, H, DH, D).transpose(0, 2, 1, 3).reshape(2 * DH, H * D)
    scales = np.concatenate([i[f"L1_ffn_{n}_s"].reshape(-1, 128).T for n in ("w1", "w2", "h1", "h2", "w3")], axis=1)
    arrays = {
        "x": c(i["L0_attn_J"]),
        "W_Q": c(i["L0_attn_W_Q"]), "W_K": c(i["L0_attn_W_K"]),
        "gamma": c(i["L0_attn_gamma"]), "beta": c(i["L0_attn_beta"]),
        "gate_w": c(i["L0_ffn_gate_w"].T), "gate_b": c(i["L0_ffn_gate_b"]),
        "w1": c(i["L0_ffn_w1"].transpose(1, 0, 2).reshape(128, -1)),
        "b1": c(i["L0_ffn_b1"].reshape(E * HC, 128).T),
        "w2": c(i["L0_ffn_w2"].reshape(E * HC, 128, D).transpose(1, 0, 2).reshape(128, -1)),
        "b2": c(i["L0_ffn_b2"].T),
        "cT": c(np.concatenate([i["L0_c"].T, i["L1_c"].T], axis=1)),
        "wmod": c(np.concatenate([i["L0_wmod"], i["L1_wmod"]], axis=1)),
        "w_emb": c(heads),
        "w_anchor": c(i["L1_attn_W_anchor"].T),
        "w_out": c(i["L1_attn_W_out"].reshape(D, H, DH).transpose(2, 1, 0)),
        "b_out": c(i["L1_attn_b_out"].reshape(D, 1)),
        "ffn": c(np.concatenate([i["L1_ffn_w1_w"].T, i["L1_ffn_w2_w"].T, out_chunks(i["L1_ffn_h1_w"], 4),
                                 out_chunks(i["L1_ffn_h2_w"], 4), out_chunks(i["L1_ffn_w3_w"], 4)], axis=1)),
        "scales": c(scales),
    }
    nc = bacc.Bacc("TRN2", target_bir_lowering=False, num_devices=1)
    aps = {k: nc.dram_tensor(f"in_{k}", a.shape, mybir.dt.from_np(a.dtype), kind="ExternalInput").ap()
           for k, a in arrays.items()}
    out = nc.dram_tensor("out_x", (B, N, D), F32, kind="ExternalOutput").ap()
    build(nc, aps, out)
    r = run_bass_kernel_spmd(nc, [{f"in_{k}": a for k, a in arrays.items()}], core_ids=[0])
    return r.results[0]["out_x"]
```
